# Optimizing a Trainium2 kernel written in Bass

```python
import numpy as np
import jax
import jax.numpy as jnp

def _softmax(x, axis=-1):
    return jax.nn.softmax(x, axis=axis)

def _gelu(x):
    return jax.nn.gelu(x, approximate=True)

def _silu(x):
    return jax.nn.silu(x)

def _sigmoid(x):
    return jax.nn.sigmoid(x)

def _layernorm(x, axis=-1, eps=1e-05):
    m = jnp.mean(x, axis=axis, keepdims=True)
    v = jnp.var(x, axis=axis, keepdims=True)
    return (x - m) / jnp.sqrt(v + eps)

def _scatter_add(tgt, idx, src, axis=0):
    return tgt.at[idx].add(src)

def _segment_sum(src, seg, n):
    return jax.ops.segment_sum(src, seg, n)
kernel_name = 'mk_seq_preln_d2_jaxref_r8_3b0ab9'

def setup_inputs(seed: int=0):
    np.random.seed(seed)
    _w = jnp.asarray

    def _L0_attn_setup():
        import jax, jax.numpy as jnp
        import numpy as np
        B, N, H = (1, 512, 256)
        NH, HD = (16, H // 16)
        WINDOW = 512
        EPS = 1e-06
        THETA = 10000.0
        NEG = -1e+30

        def rmsnorm(x, w):
            var = jnp.mean(jnp.square(x.astype(jnp.float32)), axis=-1, keepdims=True)
            return (x * jax.lax.rsqrt(var + EPS)).astype(w.dtype) * w

        def rotate_half(x):
            x1, x2 = (x[..., :x.shape[-1] // 2], x[..., x.shape[-1] // 2:])
            return jnp.concatenate((-x2, x1), axis=-1)
        key = jax.random.key(seed)
        k1, k2, k3 = jax.random.split(key, 3)
        x = jax.random.normal(k1, (B, N, H), dtype=jnp.float32)
        w_qkv = jax.random.normal(k2, (H, 3 * H), dtype=jnp.float32) * (1.0 / np.sqrt(H))
        w_out = jax.random.normal(k3, (H, H), dtype=jnp.float32) * (1.0 / np.sqrt(H))
        q_gamma = jnp.ones((HD,), dtype=jnp.float32)
        k_gamma = jnp.ones((HD,), dtype=jnp.float32)
        return {'x': x, 'w_qkv': w_qkv, 'w_out': w_out, 'q_gamma': q_gamma, 'k_gamma': k_gamma}
    _L0_attn_in = _L0_attn_setup()

    def _L0_ffn_setup():
        import jax, jax.numpy as jnp
        import numpy as np
        DIM = 256
        EXPERT_DIM = 128
        N_EXPERTS = 16
        TOPK = 2
        N_SHARED = 1
        B, T = (4, 256)
        key = jax.random.key(seed)
        ks = jax.random.split(key, 9)
        s = 0.02
        return {'x': jax.random.normal(ks[0], (B, T, DIM), jnp.float32), 'router_w': jax.random.normal(ks[1], (N_EXPERTS, DIM), jnp.float32) * s, 'router_bias': jnp.zeros((N_EXPERTS,), jnp.float32), 'Wu': jax.random.normal(ks[2], (N_EXPERTS, DIM, EXPERT_DIM), jnp.float32) * s, 'Wg': jax.random.normal(ks[3], (N_EXPERTS, DIM, EXPERT_DIM), jnp.float32) * s, 'Wd': jax.random.normal(ks[4], (N_EXPERTS, EXPERT_DIM, DIM), jnp.float32) * s, 'Su': jax.random.normal(ks[5], (N_SHARED, DIM, EXPERT_DIM * TOPK), jnp.float32) * s, 'Sg': jax.random.normal(ks[6], (N_SHARED, DIM, EXPERT_DIM * TOPK), jnp.float32) * s, 'Sd': jax.random.normal(ks[7], (N_SHARED, EXPERT_DIM * TOPK, DIM), jnp.float32) * s}
    _L0_ffn_in = _L0_ffn_setup()

    def _L1_attn_setup():
        import jax, jax.numpy as jnp
        import numpy as np
        D_MODEL = 256
        N_HEADS = 16
        HEAD_DIM = D_MODEL // N_HEADS
        SCALE_BASE = 64

        def rotate_half(x):
            x1, x2 = jnp.split(x, 2, axis=-1)
            return jnp.concatenate((-x2, x1), axis=-1)

        def rotary_xpos(seq_len, dim, dtype=jnp.float32):
            inv_freq = 1.0 / 10000.0 ** (jnp.arange(0, dim, 2, dtype=jnp.float32) / dim)
            t = jnp.arange(seq_len, dtype=jnp.float32)
            freqs = jnp.einsum('i,j->ij', t, inv_freq)
            freqs = jnp.concatenate((freqs, freqs), axis=-1)
            scale_base = (jnp.arange(0, dim, 2, dtype=jnp.float32) + 0.4 * dim) / (1.4 * dim)
            power = (t - seq_len // 2) / SCALE_BASE
            scale = scale_base[None, :] ** power[:, None]
            scale = jnp.concatenate((scale, scale), axis=-1)
            return (freqs.astype(dtype), scale.astype(dtype))

        def apply_rotary(t, pos, scale):
            return t * jnp.cos(pos) * scale + rotate_half(t) * jnp.sin(pos) * scale
        key = jax.random.key(seed)
        ks = jax.random.split(key, 5)
        B, S = (2, 256)
        hidden_states = jax.random.normal(ks[0], (B, S, D_MODEL), dtype=jnp.float32)
        w_q = jax.random.normal(ks[1], (N_HEADS * HEAD_DIM, D_MODEL), dtype=jnp.float32) * 0.02
        w_kv = jax.random.normal(ks[2], (2 * HEAD_DIM, D_MODEL), dtype=jnp.float32) * 0.02
        w_proj = jax.random.normal(ks[3], (D_MODEL, N_HEADS * HEAD_DIM), dtype=jnp.float32) * 0.02
        b_proj = jax.random.normal(ks[4], (D_MODEL,), dtype=jnp.float32) * 0.02
        return {'hidden_states': hidden_states, 'w_q': w_q, 'w_kv': w_kv, 'w_proj': w_proj, 'b_proj': b_proj}
    _L1_attn_in = _L1_attn_setup()

    def _L1_ffn_setup():
        import jax, jax.numpy as jnp
        import numpy as np
        B, S, H = (2, 256, 256)
        E, G, TKG, K = (32, 8, 4, 8)
        I, SI = (128, 256)
        ROUTED_SCALE = 2.5

        def _moe_forward(hidden_states, router_w, router_bias, w_gate, w_up, w_down, sw_gate, sw_up, sw_down):
            x = hidden_states.reshape(-1, H)
            T = x.shape[0]
            logits = x.astype(jnp.float32) @ router_w.astype(jnp.float32)
            scores = jax.nn.sigmoid(logits)
            scores_grouped = (scores + router_bias).reshape(T, G, E // G)
            top2, _ = jax.lax.top_k(scores_grouped, 2)
            group_scores = top2.sum(-1)
            _, top_groups = jax.lax.top_k(group_scores, TKG)
            mask = jnp.ones((T, G), bool).at[jnp.arange(T)[:, None], top_groups].set(False)
            masked = jnp.where(mask[:, :, None], 0.0, scores_grouped).reshape(T, E)
            _, top_k_index = jax.lax.top_k(masked, K)
            tkw = jnp.take_along_axis(scores, top_k_index, axis=-1)
            tkw = tkw / tkw.sum(-1, keepdims=True)
            tkw = (tkw * ROUTED_SCALE).astype(hidden_states.dtype)
            flat_idx = top_k_index.reshape(-1)
            sort_idx = jnp.argsort(flat_idx)
            xs = jnp.repeat(x, K, axis=0)[sort_idx]
            group_sizes = jnp.bincount(flat_idx, length=E).astype(jnp.int32)
            gate = jax.lax.ragged_dot(xs, w_gate, group_sizes)
            up = jax.lax.ragged_dot(xs, w_up, group_sizes)
            down = jax.lax.ragged_dot(jax.nn.silu(gate) * up, w_down, group_sizes)
            unsort = jnp.argsort(sort_idx)
            routed = (down[unsort].reshape(T, K, H) * tkw[..., None]).sum(axis=1)
            shared = jax.nn.silu(x @ sw_gate) * (x @ sw_up) @ sw_down
            return (routed + shared).reshape(hidden_states.shape)
        key = jax.random.key(seed)
        ks = jax.random.split(key, 9)

        def w(k, shape, fan_in):
            return jax.random.normal(k, shape, jnp.float32) / np.float32(np.sqrt(fan_in))
        return dict(hidden_states=jax.random.normal(ks[0], (B, S, H), jnp.float32), router_w=w(ks[1], (H, E), H), router_bias=jnp.zeros((E,), jnp.float32), w_gate=w(ks[2], (E, H, I), H), w_up=w(ks[3], (E, H, I), H), w_down=w(ks[4], (E, I, H), I), sw_gate=w(ks[5], (H, SI), H), sw_up=w(ks[6], (H, SI), H), sw_down=w(ks[7], (SI, H), SI))
    _L1_ffn_in = _L1_ffn_setup()
    _d = {'L0_attn_x': _L0_attn_in['x'], 'L0_attn_w_qkv': _L0_attn_in['w_qkv'], 'L0_attn_w_out': _L0_attn_in['w_out'], 'L0_attn_q_gamma': _L0_attn_in['q_gamma'], 'L0_attn_k_gamma': _L0_attn_in['k_gamma'], 'L0_ffn_router_w': _L0_ffn_in['router_w'], 'L0_ffn_router_bias': _L0_ffn_in['router_bias'], 'L0_ffn_Wu': _L0_ffn_in['Wu'], 'L0_ffn_Wg': _L0_ffn_in['Wg'], 'L0_ffn_Wd': _L0_ffn_in['Wd'], 'L0_ffn_Su': _L0_ffn_in['Su'], 'L0_ffn_Sg': _L0_ffn_in['Sg'], 'L0_ffn_Sd': _L0_ffn_in['Sd'], 'L1_attn_w_q': _L1_attn_in['w_q'], 'L1_attn_w_kv': _L1_attn_in['w_kv'], 'L1_attn_w_proj': _L1_attn_in['w_proj'], 'L1_attn_b_proj': _L1_attn_in['b_proj'], 'L1_ffn_router_w': _L1_ffn_in['router_w'], 'L1_ffn_router_bias': _L1_ffn_in['router_bias'], 'L1_ffn_w_gate': _L1_ffn_in['w_gate'], 'L1_ffn_w_up': _L1_ffn_in['w_up'], 'L1_ffn_w_down': _L1_ffn_in['w_down'], 'L1_ffn_sw_gate': _L1_ffn_in['sw_gate'], 'L1_ffn_sw_up': _L1_ffn_in['sw_up'], 'L1_ffn_sw_down': _L1_ffn_in['sw_down']}
    _x0 = _d['L0_attn_x']
    _d['L0_attn_x'] = jax.random.normal(jax.random.fold_in(jax.random.key(seed), 1), (8, 256, 256), dtype=_x0.dtype)
    del _x0
    return _d

def reference(L0_attn_x, L0_attn_w_qkv, L0_attn_w_out, L0_attn_q_gamma, L0_attn_k_gamma, L0_ffn_router_w, L0_ffn_router_bias, L0_ffn_Wu, L0_ffn_Wg, L0_ffn_Wd, L0_ffn_Su, L0_ffn_Sg, L0_ffn_Sd, L1_attn_w_q, L1_attn_w_kv, L1_attn_w_proj, L1_attn_b_proj, L1_ffn_router_w, L1_ffn_router_bias, L1_ffn_w_gate, L1_ffn_w_up, L1_ffn_w_down, L1_ffn_sw_gate, L1_ffn_sw_up, L1_ffn_sw_down):

    def _L0_attn_ref(x, w_qkv, w_out, q_gamma, k_gamma):
        import jax, jax.numpy as jnp
        import numpy as np
        B, N, H = (1, 512, 256)
        NH, HD = (16, H // 16)
        WINDOW = 512
        EPS = 1e-06
        THETA = 10000.0
        NEG = -1e+30

        def rmsnorm(x, w):
            var = jnp.mean(jnp.square(x.astype(jnp.float32)), axis=-1, keepdims=True)
            return (x * jax.lax.rsqrt(var + EPS)).astype(w.dtype) * w

        def rotate_half(x):
            x1, x2 = (x[..., :x.shape[-1] // 2], x[..., x.shape[-1] // 2:])
            return jnp.concatenate((-x2, x1), axis=-1)
        b, n, _ = x.shape
        qkv = jnp.einsum('bnh,hm->bnm', x, w_qkv)
        q, k, v = jnp.split(qkv, 3, axis=-1)
        q = q.reshape(b, n, NH, HD).transpose(0, 2, 1, 3)
        k = k.reshape(b, n, NH, HD).transpose(0, 2, 1, 3)
        v = v.reshape(b, n, NH, HD).transpose(0, 2, 1, 3)
        q = rmsnorm(q, q_gamma)
        k = rmsnorm(k, k_gamma)
        inv_freq = 1.0 / THETA ** (jnp.arange(0, HD, 2, dtype=jnp.float32) / HD)
        t = jnp.arange(n, dtype=jnp.float32)
        freqs = t[:, None] * inv_freq[None, :]
        emb = jnp.concatenate((freqs, freqs), axis=-1)
        cos = jnp.cos(emb)[None, None, :, :]
        sin = jnp.sin(emb)[None, None, :, :]
        q = q * cos + rotate_half(q) * sin
        k = k * cos + rotate_half(k) * sin
        kv_len = k.shape[-2]
        q_idx = jnp.arange(n)[:, None] + (kv_len - n)
        k_idx = jnp.arange(kv_len)[None, :]
        mask = (q_idx >= k_idx) & (q_idx - k_idx <= WINDOW)
        scores = jnp.einsum('bhqd,bhkd->bhqk', q, k) / np.sqrt(HD)
        scores = jnp.where(mask[None, None, :, :], scores, NEG)
        attn = jax.nn.softmax(scores, axis=-1)
        out = jnp.einsum('bhqk,bhkd->bhqd', attn, v)
        out = out.transpose(0, 2, 1, 3).reshape(b, n, H)
        return jnp.einsum('bnh,hm->bnm', out, w_out)

    def _L0_ffn_ref(x, router_w, router_bias, Wu, Wg, Wd, Su, Sg, Sd):
        import jax, jax.numpy as jnp
        import numpy as np
        DIM = 256
        EXPERT_DIM = 128
        N_EXPERTS = 16
        TOPK = 2
        N_SHARED = 1
        B, T = (4, 256)
        Bx, Tx, D = x.shape
        flat = x.reshape(Bx * Tx, D)
        logits = flat @ router_w.T
        scores = jax.nn.softmax(logits, axis=-1)
        _, topk_idx = jax.lax.top_k(logits + router_bias, TOPK)
        topk_scores = jnp.take_along_axis(scores, topk_idx, axis=-1)
        topk_scores = topk_scores / topk_scores.sum(-1, keepdims=True)
        combine = jnp.einsum('nk,nke->ne', topk_scores, jax.nn.one_hot(topk_idx, N_EXPERTS, dtype=scores.dtype))
        out = jnp.zeros_like(flat)
        for e in range(N_EXPERTS):
            h = jax.nn.silu(flat @ Wu[e]) * (flat @ Wg[e])
            out = out + combine[:, e:e + 1] * (h @ Wd[e])
        for s in range(N_SHARED):
            out = out + jax.nn.silu(flat @ Su[s]) * (flat @ Sg[s]) @ Sd[s]
        return out.reshape(Bx, Tx, D)

    def _L1_attn_ref(hidden_states, w_q, w_kv, w_proj, b_proj):
        import jax, jax.numpy as jnp
        import numpy as np
        D_MODEL = 256
        N_HEADS = 16
        HEAD_DIM = D_MODEL // N_HEADS
        SCALE_BASE = 64

        def rotate_half(x):
            x1, x2 = jnp.split(x, 2, axis=-1)
            return jnp.concatenate((-x2, x1), axis=-1)

        def rotary_xpos(seq_len, dim, dtype=jnp.float32):
            inv_freq = 1.0 / 10000.0 ** (jnp.arange(0, dim, 2, dtype=jnp.float32) / dim)
            t = jnp.arange(seq_len, dtype=jnp.float32)
            freqs = jnp.einsum('i,j->ij', t, inv_freq)
            freqs = jnp.concatenate((freqs, freqs), axis=-1)
            scale_base = (jnp.arange(0, dim, 2, dtype=jnp.float32) + 0.4 * dim) / (1.4 * dim)
            power = (t - seq_len // 2) / SCALE_BASE
            scale = scale_base[None, :] ** power[:, None]
            scale = jnp.concatenate((scale, scale), axis=-1)
            return (freqs.astype(dtype), scale.astype(dtype))

        def apply_rotary(t, pos, scale):
            return t * jnp.cos(pos) * scale + rotate_half(t) * jnp.sin(pos) * scale
        B, S, _ = hidden_states.shape
        q = hidden_states @ w_q.T
        kv = hidden_states @ w_kv.T
        k, v = jnp.split(kv, 2, axis=-1)
        q = q.reshape(B, S, N_HEADS, HEAD_DIM).transpose(0, 2, 1, 3)
        scale_w = HEAD_DIM ** (-0.5)
        q = q * scale_w
        k = k * scale_w
        pos, xscale = rotary_xpos(S, HEAD_DIM, q.dtype)
        q = apply_rotary(q, pos, xscale)
        k = apply_rotary(k, pos, 1.0 / xscale)
        attn = jnp.einsum('bnih,bjh->bnij', q, k)
        causal = jnp.triu(jnp.ones((S, S), dtype=bool), 1)
        attn = jnp.where(causal, -jnp.finfo(attn.dtype).max, attn)
        attn = jax.nn.softmax(attn, axis=-1)
        out = jnp.einsum('bnij,bjd->bind', attn, v)
        out = out.reshape(B, S, N_HEADS * HEAD_DIM)
        out = out @ w_proj.T + b_proj
        return out

    def _L1_ffn_ref(hidden_states, router_w, router_bias, w_gate, w_up, w_down, sw_gate, sw_up, sw_down):
        import jax, jax.numpy as jnp
        import numpy as np
        B, S, H = (2, 256, 256)
        E, G, TKG, K = (32, 8, 4, 8)
        I, SI = (128, 256)
        ROUTED_SCALE = 2.5

        def _moe_forward(hidden_states, router_w, router_bias, w_gate, w_up, w_down, sw_gate, sw_up, sw_down):
            x = hidden_states.reshape(-1, H)
            T = x.shape[0]
            logits = x.astype(jnp.float32) @ router_w.astype(jnp.float32)
            scores = jax.nn.sigmoid(logits)
            scores_grouped = (scores + router_bias).reshape(T, G, E // G)
            top2, _ = jax.lax.top_k(scores_grouped, 2)
            group_scores = top2.sum(-1)
            _, top_groups = jax.lax.top_k(group_scores, TKG)
            mask = jnp.ones((T, G), bool).at[jnp.arange(T)[:, None], top_groups].set(False)
            masked = jnp.where(mask[:, :, None], 0.0, scores_grouped).reshape(T, E)
            _, top_k_index = jax.lax.top_k(masked, K)
            tkw = jnp.take_along_axis(scores, top_k_index, axis=-1)
            tkw = tkw / tkw.sum(-1, keepdims=True)
            tkw = (tkw * ROUTED_SCALE).astype(hidden_states.dtype)
            flat_idx = top_k_index.reshape(-1)
            sort_idx = jnp.argsort(flat_idx)
            xs = jnp.repeat(x, K, axis=0)[sort_idx]
            group_sizes = jnp.bincount(flat_idx, length=E).astype(jnp.int32)
            gate = jax.lax.ragged_dot(xs, w_gate, group_sizes)
            up = jax.lax.ragged_dot(xs, w_up, group_sizes)
            down = jax.lax.ragged_dot(jax.nn.silu(gate) * up, w_down, group_sizes)
            unsort = jnp.argsort(sort_idx)
            routed = (down[unsort].reshape(T, K, H) * tkw[..., None]).sum(axis=1)
            shared = jax.nn.silu(x @ sw_gate) * (x @ sw_up) @ sw_down
            return (routed + shared).reshape(hidden_states.shape)
        return _moe_forward(hidden_states, router_w, router_bias, w_gate, w_up, w_down, sw_gate, sw_up, sw_down)
    x = L0_attn_x
    x = x + _L0_attn_ref(_layernorm(x, axis=-1), L0_attn_w_qkv, L0_attn_w_out, L0_attn_q_gamma, L0_attn_k_gamma)
    x = x + _L0_ffn_ref(_layernorm(x, axis=-1), L0_ffn_router_w, L0_ffn_router_bias, L0_ffn_Wu, L0_ffn_Wg, L0_ffn_Wd, L0_ffn_Su, L0_ffn_Sg, L0_ffn_Sd)
    x = x + _L1_attn_ref(_layernorm(x, axis=-1), L1_attn_w_q, L1_attn_w_kv, L1_attn_w_proj, L1_attn_b_proj)
    x = x + _L1_ffn_ref(_layernorm(x, axis=-1), L1_ffn_router_w, L1_ffn_router_bias, L1_ffn_w_gate, L1_ffn_w_up, L1_ffn_w_down, L1_ffn_sw_gate, L1_ffn_sw_up, L1_ffn_sw_down)
    return x

_drawn_inputs = setup_inputs


def setup_inputs(seed=0):
    import zlib

    import numpy as np

    out = dict(_drawn_inputs(seed))
    spreads = {'L0_attn_q_gamma': (1.0, 0.2),
     'L0_attn_k_gamma': (1.0, 0.2),
     'L0_ffn_router_bias': (0.0, 0.28),
     'L1_ffn_router_bias': (0.0, 0.1)}
    factors = {'L1_attn_w_q': 23.282}
    for name, (base, spread) in spreads.items():
        noise = np.random.default_rng([zlib.crc32(name.encode()), seed]).standard_normal(out[name].shape)
        drawn = base * np.exp(spread * noise) if base else spread * noise
        out[name] = jnp.asarray(drawn.astype(out[name].dtype))
    for name, factor in factors.items():
        out[name] = (out[name] * factor).astype(out[name].dtype)
    return out
```

```python
from contextlib import ExitStack, contextmanager

import concourse.bass as bass
from concourse import mybir

F32 = mybir.dt.float32
F32R = mybir.dt.float32r
ALU = mybir.AluOpType
ACT = mybir.ActivationFunctionType
AX_X = mybir.AxisListType.X

P = 128
H = 256
FC = H // P
B, N = 8, 256
T = B * N
NT = T // P
TB = N // P
NH, HD = 16, 16
PAIRS = NH // 2
STK = 4 * HD
TRI = N + P
HV = HD + 1
NEG = -1e30
LN_EPS = 1e-5
BLK = 512
HALF = 2 * BLK
HALVES = T // HALF
WCOLS = 2 * FC * P + H
BIG = 3.0e38


def ds(start, size):
    return bass.DynSlice(start, size)


class Chain:

    def __init__(self, sem, per_round):
        self.sem, self.per_round = sem, per_round
        self.base = self.n = 0

    def start(self, r):
        self.base, self.n = r * self.per_round, 0

    def inc(self, ins):
        ins.then_inc(self.sem, 1)
        self.n += 1

    def wait(self, eng):
        eng.wait_ge(self.sem, self.base + self.n)

    def end(self):
        assert self.n == self.per_round, (self.n, self.per_round)


def wait(eng, sem, value):
    if isinstance(value, int) and value <= 0:
        return
    eng.wait_ge(sem, value)


@contextmanager
def semaphores(nc):
    used = []

    def make(name):
        used.append(nc.alloc_semaphore(name=name))
        return used[-1]

    yield make
    nc.clear_and_free_semaphores(used)
    nc.all_engine_barrier()


def passed(eng, sem):
    eng.sem_inc(sem, 1)


def split_passes(hi_a, lo_a, hi_b, lo_b):
    return ((hi_a, hi_b), (hi_a, lo_b), (lo_a, hi_b))


def setup(nc, env, x_in):
    x, ident, ident_r, mask_r, sel_head, sel_exp, half_neg = (
        env["x"], env["ident"], env["ident_r"], env["mask_r"], env["sel_head"], env["sel_exp"], env["half_neg"])
    with semaphores(nc) as make_sem, ExitStack() as ctx:
        tmp = ctx.enter_context(nc.sbuf_tensor("setup_tmp", [P, 32, P], F32))
        mask = ctx.enter_context(nc.sbuf_tensor("setup_mask", [P, P], F32))
        hd = ctx.enter_context(nc.sbuf_tensor("setup_head", [32, NH, P], F32))
        x_loaded = make_sem("x_loaded")
        made = make_sem("made")
        rounded = make_sem("rounded")
        block = ctx.enter_context(nc.Block())

        @block.sync
        def _(sp):
            sp.dma_start(x[:, :, :], x_in.rearrange("b (t p) n -> p (b t) n", p=P)).then_inc(x_loaded, 16)
            sp.wait_ge(x_loaded, 16)

        @block.gpsimd
        def _(pool):
            nc.gpsimd.memset(half_neg[:], -0.5)
            nc.gpsimd.memset(ident[:], 0.0)
            nc.gpsimd.memset(mask[:], 0.0)
            nc.gpsimd.memset(hd[:], 1.0)
            nc.gpsimd.memset(tmp[:], 0.0).then_inc(made, 1)
            pool.wait_ge(made, 1)
            nc.gpsimd.affine_select(out=ident[:], in_=ident[:], compare_op=ALU.not_equal, fill=1.0, base=0,
                                    pattern=[[-1, P]], channel_multiplier=1).then_inc(made, 1)
            nc.gpsimd.affine_select(out=mask[:], in_=mask[:], compare_op=ALU.is_ge, fill=NEG, base=0,
                                    pattern=[[-1, P]], channel_multiplier=1).then_inc(made, 1)
            nc.gpsimd.affine_select(out=hd[:], in_=hd[:], compare_op=ALU.is_ge, fill=0.0, base=0,
                                    pattern=[[-2, NH], [0, P]], channel_multiplier=1).then_inc(made, 1)
            pool.wait_ge(made, 4)
            nc.gpsimd.affine_select(out=hd[:], in_=hd[:], compare_op=ALU.is_ge, fill=0.0, base=1,
                                    pattern=[[2, NH], [0, P]], channel_multiplier=-1).then_inc(made, 1)
            nc.gpsimd.affine_select(out=tmp[:], in_=tmp[:], compare_op=ALU.not_equal, fill=1.0, base=0,
                                    pattern=[[-1, 32], [0, P]], channel_multiplier=1).then_inc(made, 1)
            pool.wait_ge(made, 6)
            nc.gpsimd.affine_select(out=tmp[:], in_=tmp[:], compare_op=ALU.not_equal, fill=1.0, base=-32,
                                    pattern=[[-1, 32], [0, P]], channel_multiplier=1).then_inc(made, 1)

        @block.vector
        def _(dve):
            dve.wait_ge(made, 7)
            nc.vector.tensor_copy(ident_r[:], ident[:])
            nc.vector.tensor_copy(mask_r[:], mask[:])
            nc.vector.tensor_copy(sel_head[:], hd[:])
            nc.vector.tensor_copy(sel_exp[:], tmp[0:64, :, :]).then_inc(rounded, 1)
            dve.wait_ge(rounded, 1)


def load_split(nc, weights, pre):
    with semaphores(nc) as make_sem, ExitStack() as ctx:
        raws = [ctx.enter_context(nc.sbuf_tensor(f"{pre}_raw{i}", w[1], F32)) for i, w in enumerate(weights)]
        loaded = [make_sem(f"{pre}_loaded{i}") for i in range(len(weights))]
        hi_done = make_sem(f"{pre}_hi_done")
        lo_done = make_sem(f"{pre}_lo_done")
        block = ctx.enter_context(nc.Block())

        @block.sync
        def _(sp):
            for (dram, *_), raw, sem in zip(weights, raws, loaded):
                sp.dma_start(raw[:], dram).then_inc(sem, 16)

        @block.scalar
        def _(act):
            for (_, _, hi, _), raw, sem in zip(weights, raws, loaded):
                act.wait_ge(sem, 16)
                nc.scalar.activation(hi[:], raw[:], ACT.Copy).then_inc(hi_done, 1)

        @block.vector
        def _(dve):
            for i, ((_, _, hi, lo), raw, sem) in enumerate(zip(weights, raws, loaded)):
                dve.wait_ge(sem, 16)
                dve.wait_ge(hi_done, i + 1)
                nc.vector.tensor_tensor(lo[:], raw[:], hi[:].bitcast(F32), ALU.subtract).then_inc(lo_done, 1)
            dve.wait_ge(lo_done, len(weights))


def rope_tables(nc, rope_c, rope_s, gam_q, gam_k, tab_c, tab_s):
    half = HD // 2
    with semaphores(nc) as make_sem, ExitStack() as ctx:
        cs = ctx.enter_context(nc.sbuf_tensor("rope_cs", [P, 2, TB, HD], F32))
        gam = ctx.enter_context(nc.sbuf_tensor("rope_gamma", [P, 2, HD], F32))
        loaded = make_sem("rope_loaded")
        done = make_sem("rope_done")
        block = ctx.enter_context(nc.Block())

        @block.sync
        def _(sp):
            sp.dma_start(cs[:, 0], rope_c.rearrange("(t p) d -> p t d", p=P)).then_inc(loaded, 16)
            sp.dma_start(cs[:, 1], rope_s.rearrange("(t p) d -> p t d", p=P)).then_inc(loaded, 16)
            sp.dma_start(gam[:, 0], gam_q.partition_broadcast(P)).then_inc(loaded, 16)
            sp.dma_start(gam[:, 1], gam_k.partition_broadcast(P)).then_inc(loaded, 16)

        @block.vector
        def _(dve):
            dve.wait_ge(loaded, 64)
            for t in range(TB):
                nc.vector.tensor_tensor(tab_c[:, t], gam[:], cs[:, 0, t].unsqueeze(1).to_broadcast([P, 2, HD]),
                                        ALU.mult)
                for a, b in ((0, half), (half, 0)):
                    last = nc.vector.tensor_tensor(
                        tab_s[:, t, :, a:a + half], gam[:, :, b:b + half],
                        cs[:, 1, t, a:a + half].unsqueeze(1).to_broadcast([P, 2, half]), ALU.mult)
            last.then_inc(done, 1)
            dve.wait_ge(done, 1)


def load_tables(nc, loads, pre):
    with semaphores(nc) as make_sem, ExitStack() as ctx:
        loaded = make_sem(f"{pre}_tables_loaded")
        block = ctx.enter_context(nc.Block())

        @block.sync
        def _(sp):
            for dst, src in loads:
                sp.dma_start(dst, src).then_inc(loaded, 16)
            sp.wait_ge(loaded, 16 * len(loads))


def attention(nc, env, layer, wts):
    x, ident, ident_r, mask_r, sel_head, half_neg = (
        env["x"], env["ident"], env["ident_r"], env["mask_r"], env["sel_head"], env["half_neg"])
    wqkv_hi, wqkv_lo, wout_hi, wout_lo, tab_c, tab_s = (
        wts["qkv_hi"], wts["qkv_lo"], wts["out_hi"], wts["out_lo"], wts["tab_c"], wts["tab_s"])
    bias = wts.get("bias")
    multi = layer == 0
    NK = NH if multi else 1
    QK = (NH + NK) * HD
    VW = NK * HD
    groups = [(0, 4, False), (4, 4, False)] + ([(8, 4, True), (12, 4, True)] if multi else [(8, 1, True)])
    NG = len(groups)
    NF = TB * NG
    exp_scale = HD ** -0.5 if multi else 1.0
    pre = f"a{layer}_"

    with semaphores(nc) as make_sem, ExitStack() as ctx:
        def sb(name, shape, dt=F32):
            return ctx.enter_context(nc.sbuf_tensor(pre + name, shape, dt))

        def pb(name, shape):
            return ctx.enter_context(nc.psum_tensor(pre + name, shape, F32))

        def sem(name):
            return make_sem(pre + name)

        stats = sb("stats", [P, TB, 6])
        mv = sb("mv", [P, TB, 2])
        var_eps = sb("var_eps", [P, TB])
        rstd = sb("rstd", [P, TB])
        y = sb("y", [P, TB, H])
        yT_hi = sb("yT_hi", [P, FC, N], F32R)
        yT_lo = sb("yT_lo", [P, FC, N], F32R)
        sq = sb("sq", [P, TB, QK])
        ss = sb("ss", [P, TB, NH + NK])
        ss_eps = sb("ss_eps", [P, TB, NH + NK])
        rs = sb("rs", [P, TB, NH + NK])
        qn = sb("qn", [P, TB, QK])
        rot_c = sb("rot_c", [P, TB, QK])
        rot_s = sb("rot_s", [P, TB, QK])
        rotated = sb("rotated", [P, TB, QK])
        pieces = NH // 2 + (NK // 2 if multi else 1)
        stack = sb("stack", [P, TB, pieces * P], F32R)
        qT = [sb(f"qT{i}", [P, PAIRS, N], F32R) for i in range(2)]
        kT = [sb(f"kT{i}", [P, PAIRS if multi else 1, N], F32R) for i in range(2)]
        v = [sb(f"v{i}", [P, TB, NK, HV]) for i in range(2)]
        neg_max = sb("neg_max", [P, TB, NH])
        max_stack = sb("max_stack", [P, TB, NH, 2], F32R)
        maxT = sb("maxT", [2 * NH, N], F32R)
        probs = sb("probs", [P, 2, 2, TRI])
        recip = sb("recip", [P, TB, NH // 2])
        o = sb("o", [P, TB, NH, HD])
        oT_hi = sb("oT_hi", [P, FC, N], F32R)
        oT_lo = sb("oT_lo", [P, FC, N], F32R)

        ring = pb("ring", [P, 4, 512])
        ps_av = pb("ps_av", [P, 512])
        ps_t = [pb(f"ps_t{i}", [P, 512]) for i in range(2)]
        ps_p = pb("ps_p", [P, 512])

        y_ready = sem("y_ready")
        yT_ps = sem("yT_ps")
        yT_hi_done = sem("yT_hi_done")
        yT_lo_done = sem("yT_lo_done")
        qk_ps = sem("qk_ps")
        v_ps = sem("v_ps")
        v_done = sem("v_done")
        var_ready = sem("var_ready")
        rstd_ready = sem("rstd_ready")
        sq_done = sem("sq_done")
        ss_done = sem("ss_done")
        rs_done = sem("rs_done")
        qn_done = sem("qn_done")
        rot_s_done = sem("rot_s_done")
        rot_done = sem("rot_done")
        stack_hi = sem("stack_hi")
        stack_lo = sem("stack_lo")
        group_ps = sem("group_ps")
        group_done = sem("group_done")
        s_ps = sem("s_ps")
        max_done = sem("max_done")
        max_stacked = sem("max_stacked")
        maxT_ps = sem("maxT_ps")
        maxT_done = sem("maxT_done")
        st_ps = sem("st_ps")
        exp_done = sem("exp_done")
        cut_done = sem("cut_done")
        av_ps = sem("av_ps")
        av_norm = sem("av_norm")
        oT_ps = sem("oT_ps")
        oT_hi_done = sem("oT_hi_done")
        oT_lo_done = sem("oT_lo_done")
        out_ps = sem("out_ps")
        out_added = sem("out_added")
        ones_set = sem("ones_set")
        waited_dve = sem("waited_dve")
        waited_pool = sem("waited_pool")
        dve_ln = Chain(sem("dve_ln"), 1)
        pool_ln = Chain(sem("pool_ln"), 1)
        pool_rs = Chain(sem("pool_rs"), TB)
        dve_max = Chain(sem("dve_max"), 1)
        dve_norm = Chain(sem("dve_norm"), 2)
        dve_rot = Chain(sem("dve_rot"), TB)
        dve_bias = Chain(sem("dve_bias"), 1)
        block = ctx.enter_context(nc.Block())

        def head_view(ap, t):
            return ap[:, t, :].rearrange("p (k h d) -> p k h d", k=2, d=HD)

        def rot_parts(ap, t):
            if multi:
                return [(head_view(ap, t), slice(0, 2))]
            q = ap[:, t, 0:NH * HD].rearrange("p (k h d) -> p k h d", k=1, d=HD)
            k = ap[:, t, NH * HD:QK].rearrange("p (k h d) -> p k h d", k=1, d=HD)
            return [(q, slice(0, 1)), (k, slice(1, 2))]

        def table(tab, t, which, heads, lo=0, hi=HD):
            k = which.stop - which.start
            return tab[:, t, which, lo:hi].unsqueeze(2).to_broadcast([P, k, heads, hi - lo])

        def q_stack(t):
            return stack[:, t, 0:NH * STK].rearrange("p (h r d) -> p h r d", r=4, d=HD)

        def k_stack(t):
            if multi:
                return stack[:, t, NH * STK:].rearrange("p (h r s d) -> p h r s d", r=2, s=2, d=HD)
            return stack[:, t, NH * STK:].rearrange("p (c r s d) -> p c r s d", c=2, r=2, s=2, d=HD)

        def q_part(ap, t):
            return ap[:, t, 0:NH * HD].rearrange("p (h d) -> p h d", d=HD).unsqueeze(2).to_broadcast([P, NH, 2, HD])

        def k_part(ap, t):
            c = ap[:, t, NH * HD:QK]
            if multi:
                return c.rearrange("p (h d) -> p h d", d=HD).unsqueeze(2).to_broadcast([P, NH, 2, HD])
            return c.unsqueeze(1).unsqueeze(1).to_broadcast([P, 2, 2, HD])

        @block.tensor
        def _(pe):
            def proj_transpose(s):
                pe.wait_ge(y_ready, s + 1)
                wait(pe, group_done, NF * s)
                for c in range(FC):
                    for t in range(TB):
                        last = nc.tensor.transpose(ps_t[0][:, c * N + t * P:c * N + (t + 1) * P],
                                                   y[:, t, c * P:(c + 1) * P], ident[:])
                last.then_inc(yT_ps, 1)

            def project(out, t, lo, hi, first):
                n = 0
                for c in range(FC):
                    for a, w in split_passes(yT_hi, yT_lo, wqkv_hi, wqkv_lo):
                        last = nc.tensor.matmul(out, a[:, c, t * P:(t + 1) * P], w[:, c, lo:hi],
                                                start=first and n == 0, stop=n == 3 * FC - 1,
                                                skip_group_check=True)
                        n += 1
                return last

            def proj_qk(s, t):
                if t == 0:
                    pe.wait_ge(yT_hi_done, s + 1)
                    pe.wait_ge(yT_lo_done, s + 1)
                    wait(pe, v_done, s)
                    wait(pe, out_added, s - 1)
                else:
                    pe.wait_ge(qn_done, TB * s + t)
                    if multi:
                        pe.wait_ge(sq_done, TB * s + t)
                project(ps_p[:, 0:QK], t, 0, QK, True).then_inc(qk_ps, 1)

            def proj_v(s):
                pe.wait_ge(qn_done, TB * s + TB)
                if multi:
                    pe.wait_ge(sq_done, TB * s + TB)
                for t in range(TB):
                    last = project(ps_p[:, t * VW:(t + 1) * VW], t, QK, QK + VW, t == 0)
                last.then_inc(v_ps, 1)

            def proj_group(s, i, maxes):
                t, g = divmod(i, NG)
                first, count, _ = groups[g]
                if g == 0:
                    pe.wait_ge(stack_hi, TB * s + t + 1)
                    pe.wait_ge(stack_lo, TB * s + t + 1)
                if i >= 2:
                    pe.wait_ge(group_done, NF * s + i - 1)
                elif i == 1:
                    wait(pe, maxT_done, maxes)
                for k in range(count):
                    last = nc.tensor.transpose(ps_t[i % 2][:, k * P:(k + 1) * P].bitcast(F32R),
                                               stack[:, t, (first + k) * P:(first + k + 1) * P], ident_r[:])
                last.then_inc(group_ps, 1)

            def keys(p, j, row):
                return kT[p][row:row + STK, j if multi else 0]

            def scores(s, p, j):
                if j == 0:
                    pe.wait_ge(group_done, NF * (s + 1))
                    wait(pe, exp_done, PAIRS * s)
                if j >= 2:
                    pe.wait_ge(max_done, PAIRS * s + j - 1)
                for hh in range(2):
                    row, out = STK * hh, ring[:, 2 * (j % 2) + hh]
                    nc.tensor.matmul(out[:, 0:P], qT[p][row:row + STK, j, 0:P], keys(p, j, row)[:, 0:P],
                                     start=True, stop=False, skip_group_check=True)
                    nc.tensor.matmul(out[:, P:TRI], qT[p][row:row + STK, j, P:N], keys(p, j, row)[:, 0:N],
                                     start=False, stop=False, skip_group_check=True)
                    last = nc.tensor.matmul(
                        out[:, 0:2 * N].rearrange("p (a k) -> p a k", k=N)[:, :, 0:P], ident_r[:],
                        mask_r[:].unsqueeze(1).to_broadcast([P, 2, P]), start=False, stop=True,
                        skip_group_check=True)
                last.then_inc(s_ps, 1)

            def transpose_maxima(s):
                pe.wait_ge(max_stacked, s + 1)
                wait(pe, oT_hi_done, s)
                wait(pe, oT_lo_done, s)
                for t in range(TB):
                    last = nc.tensor.transpose(ps_t[1][0:2 * NH, t * P:(t + 1) * P].bitcast(F32R),
                                               max_stack[:, t].rearrange("p h s -> p (h s)"), ident_r[:])
                last.then_inc(maxT_ps, 1)

            def shifted_scores(s, p, j):
                if j == 0:
                    pe.wait_ge(maxT_done, s + 1)
                    pe.wait_ge(max_done, PAIRS * (s + 1))
                if j >= 2:
                    pe.wait_ge(exp_done, PAIRS * s + j - 1)
                for hh in range(2):
                    row, out = STK * hh, ring[:, 2 * (j % 2) + hh]
                    nc.tensor.matmul(out[:, 0:N], keys(p, j, row)[:, 0:P], qT[p][row:row + STK, j, 0:N],
                                     start=True, stop=False, skip_group_check=True)
                    nc.tensor.matmul(out[:, N:TRI], keys(p, j, row)[:, P:N], qT[p][row:row + STK, j, P:N],
                                     start=False, stop=False, skip_group_check=True)
                    nc.tensor.matmul(out[:, 0:N], sel_head[:, 2 * j + hh], maxT[:, 0:N],
                                     start=False, stop=False, skip_group_check=True)
                    last = nc.tensor.matmul(out[:, N:TRI], sel_head[:, 2 * j + hh], maxT[:, P:N],
                                            start=False, stop=True, skip_group_check=True)
                last.then_inc(st_ps, 1)

            def attend(s, p, j):
                pe.wait_ge(cut_done, PAIRS * s + j + 1)
                if j == 0:
                    pe.wait_ge(v_done, s + 1)
                    wait(pe, av_norm, 2 * s)
                if j == PAIRS // 2:
                    pe.wait_ge(av_norm, 2 * s + 1)
                av = ps_av[:, 0:TB * (NH // 2) * HV].rearrange("p (c h d) -> p c h d", c=TB, d=HV)
                for hh in range(2):
                    h = 2 * j + hh
                    pr, hc, vh = probs[:, j % 2, hh], h % (NH // 2), h if multi else 0
                    nc.tensor.matmul(av[:, 0, hc], pr[:, 0:P], v[p][:, 0, vh],
                                     start=hc == 0, stop=False, skip_group_check=True)
                    nc.tensor.matmul(av[:, 1, hc], pr[:, P:N], v[p][:, 0, vh],
                                     start=False, stop=False, skip_group_check=True)
                    last = nc.tensor.matmul(av[:, 1, hc], pr[:, N:TRI], v[p][:, 1, vh],
                                            start=False, stop=True, skip_group_check=True)
                last.then_inc(av_ps, 1)

            def out_transpose(s, groups_out):
                pe.wait_ge(av_norm, 2 * (s + 1))
                pe.wait_ge(group_done, groups_out)
                for c in range(FC):
                    for t in range(TB):
                        last = nc.tensor.transpose(
                            ps_t[1][:, c * N + t * P:c * N + (t + 1) * P],
                            o[:, t].rearrange("p h d -> p (h d)")[:, c * P:(c + 1) * P], ident[:])
                last.then_inc(oT_ps, 1)

            def out_project(s, v_out):
                pe.wait_ge(oT_hi_done, s + 1)
                pe.wait_ge(oT_lo_done, s + 1)
                pe.wait_ge(v_done, v_out)
                for t in range(TB):
                    n = 0
                    for c in range(FC):
                        for a, w in split_passes(oT_hi, oT_lo, wout_hi, wout_lo):
                            last = nc.tensor.matmul(ps_p[:, t * H:(t + 1) * H], a[:, c, t * P:(t + 1) * P],
                                                    w[:, c, :], start=t == 0 and n == 0,
                                                    stop=n == 3 * FC - 1, skip_group_check=True)
                            n += 1
                last.then_inc(out_ps, 1)

            def sequence(s, p, before, after):
                for j in range(PAIRS):
                    scores(s, p, j)
                    if j == 1 and before:
                        out_transpose(s - 1, NF * (s + 1))
                    if j == 3 and after:
                        proj_transpose(s + 1)
                    if j == 4 and before:
                        out_project(s - 1, s + 1)
                    if j == 6 and after:
                        proj_qk(s + 1, 0)
                transpose_maxima(s)
                if after:
                    proj_qk(s + 1, 1)
                group = 0
                for j in range(PAIRS):
                    shifted_scores(s, p, j)
                    if j == 0 and after:
                        proj_v(s + 1)
                    if j >= 1:
                        attend(s, p, j - 1)
                        if after and group < NF:
                            proj_group(s + 1, group, s + 1)
                            group += 1
                while after and group < NF:
                    proj_group(s + 1, group, s + 1)
                    group += 1
                attend(s, p, PAIRS - 1)

            pe.wait_ge(ones_set, 1)
            proj_transpose(0)
            for t in range(TB):
                proj_qk(0, t)
            proj_v(0)
            for i in range(NF):
                proj_group(0, i, 0)
            sequence(0, 0, False, True)
            with pe.Fori(0, (B - 2) // 2) as r:
                for k in range(2):
                    sequence(2 * r + 1 + k, (1 + k) % 2, True, True)
            sequence(B - 1, (B - 1) % 2, True, False)
            out_transpose(B - 1, NF * B)
            out_project(B - 1, B)

        @block.scalar
        def _(act):
            def y_hi(s):
                act.wait_ge(yT_ps, s + 1)
                wait(act, v_ps, s)
                nc.scalar.activation(yT_hi[:].rearrange("p c n -> p (c n)"), ps_t[0][:],
                                     ACT.Copy).then_inc(yT_hi_done, 1)

            def square(s, t):
                if not multi:
                    return
                act.wait_ge(qk_ps, TB * s + t + 1)
                wait(act, ss_done, TB * s)
                nc.scalar.activation(sq[:, t], ps_p[:, 0:QK], ACT.Square).then_inc(sq_done, 1)

            def copy_v(s, p):
                act.wait_ge(v_ps, s + 1)
                nc.scalar.activation(v[p][:, :, :, 0:HD],
                                     ps_p[:, 0:TB * VW].rearrange("p (t h d) -> p t h d", t=TB, d=HD),
                                     ACT.Copy).then_inc(v_done, 1)

            def stack_his(s, t):
                act.wait_ge(rot_done, TB * s + t + 1)
                wait(act, group_ps, NF * s)
                nc.scalar.activation(q_stack(t)[:, :, 0:2], q_part(rotated, t), ACT.Copy)
                nc.scalar.activation(k_stack(t)[:, :, :, 0], k_part(rotated, t),
                                     ACT.Copy).then_inc(stack_hi, 1)

            def copy_group(s, p, i):
                t, g = divmod(i, NG)
                first, count, is_key = groups[g]
                act.wait_ge(group_ps, NF * s + i + 1)
                dst, at = (kT[p], first - PAIRS) if is_key else (qT[p], first)
                nc.scalar.activation(dst[:, at:at + count, t * P:(t + 1) * P],
                                     ps_t[i % 2][:, 0:count * P].rearrange("p (k n) -> p k n", n=P),
                                     ACT.Copy).then_inc(group_done, 1)

            def maxima(s):
                act.wait_ge(maxT_ps, s + 1)
                wait(act, st_ps, PAIRS * s)
                nc.scalar.activation(maxT[:], ps_t[1][0:2 * NH, 0:N], ACT.Copy).then_inc(maxT_done, 1)

            def exponentials(s, j):
                act.wait_ge(st_ps, PAIRS * s + j + 1)
                if j >= 2:
                    act.wait_ge(av_ps, PAIRS * s + j - 1)
                else:
                    wait(act, av_ps, PAIRS * s)
                nc.scalar.activation(probs[:, j % 2], ring[:, 2 * (j % 2):2 * (j % 2) + 2, 0:TRI], ACT.Exp,
                                     scale=exp_scale).then_inc(exp_done, 1)

            def out_hi(s):
                act.wait_ge(oT_ps, s + 1)
                wait(act, out_ps, s)
                nc.scalar.activation(oT_hi[:].rearrange("p c n -> p (c n)"), ps_t[1][:],
                                     ACT.Copy).then_inc(oT_hi_done, 1)

            def sequence(s, p, before, after):
                if before:
                    out_hi(s - 1)
                if after:
                    y_hi(s + 1)
                    square(s + 1, 0)
                maxima(s)
                if after:
                    square(s + 1, 1)
                group = 0
                for j in range(PAIRS):
                    exponentials(s, j)
                    if after:
                        if j == 0:
                            copy_v(s + 1, 1 - p)
                            stack_his(s + 1, 0)
                        if j == 2:
                            stack_his(s + 1, 1)
                        if j >= 1 and group < NF:
                            copy_group(s + 1, 1 - p, group)
                            group += 1
                while after and group < NF:
                    copy_group(s + 1, 1 - p, group)
                    group += 1

            y_hi(0)
            for t in range(TB):
                square(0, t)
            copy_v(0, 0)
            for t in range(TB):
                stack_his(0, t)
            for i in range(NF):
                copy_group(0, 0, i)
            sequence(0, 0, False, True)
            with act.Fori(0, (B - 2) // 2) as r:
                for k in range(2):
                    sequence(2 * r + 1 + k, (1 + k) % 2, True, True)
            sequence(B - 1, (B - 1) % 2, True, False)
            out_hi(B - 1)

        @block.vector
        def _(dve):
            def ln_stats(s):
                dve_ln.start(s)
                for t in range(TB):
                    last = nc.vector.bn_stats(stats[:, t], x[:, ds(TB * s + t, 1)].rearrange("p a n -> p (a n)"))
                dve_ln.inc(last)
                dve_ln.wait(dve)
                passed(dve, waited_dve)
                for t in range(TB):
                    last = nc.vector.bn_aggr(mv[:, t], stats[:, t])
                last.then_inc(var_ready, 1)

            def ln_apply(s):
                dve.wait_ge(rstd_ready, s + 1)
                wait(dve, yT_ps, s)
                for t in range(TB):
                    last = nc.vector.tensor_scalar(y[:, t], x[:, ds(TB * s + t, 1)].rearrange("p a n -> p (a n)"),
                                                   mv[:, t, 0:1], rstd[:, t:t + 1], ALU.subtract, ALU.mult)
                last.then_inc(y_ready, 1)

            def y_lo(s):
                dve.wait_ge(yT_hi_done, s + 1)
                wait(dve, v_ps, s)
                nc.vector.tensor_tensor(yT_lo[:].rearrange("p c n -> p (c n)"), ps_t[0][:],
                                        yT_hi[:].rearrange("p c n -> p (c n)").bitcast(F32),
                                        ALU.subtract).then_inc(yT_lo_done, 1)

            def sum_squares(s, t):
                if not multi:
                    return
                dve.wait_ge(sq_done, TB * s + t + 1)
                nc.vector.tensor_reduce(ss[:, t], sq[:, t].rearrange("p (h d) -> p h d", d=HD), AX_X,
                                        ALU.add).then_inc(ss_done, 1)

            def norm_qk(s, t):
                if multi:
                    dve.wait_ge(rs_done, TB * s + t + 1)
                else:
                    dve.wait_ge(qk_ps, TB * s + t + 1)
                wait(dve, rot_s_done, TB * s)
                src = ps_p[:, 0:QK].rearrange("p (h d) -> p h d", d=HD)
                dst = qn[:, t].rearrange("p (h d) -> p h d", d=HD)
                if multi:
                    ins = nc.vector.tensor_tensor(dst, src, rs[:, t].unsqueeze(2).to_broadcast([P, NH + NK, HD]),
                                                  ALU.mult)
                else:
                    ins = nc.vector.tensor_copy(dst, src)
                ins.then_inc(qn_done, 1)

            def rotate_cos(s, t):
                if t == 0:
                    dve_rot.start(s)
                dve.wait_ge(qn_done, TB * s + t + 1)
                for (src, which), (dst, _) in zip(rot_parts(qn, t), rot_parts(rot_c, t)):
                    last = nc.vector.tensor_tensor(dst, src, table(tab_c, t, which, src.shape[2]), ALU.mult)
                dve_rot.inc(last)

            def rotate_add(s, t):
                dve_rot.wait(dve)
                dve.wait_ge(rot_s_done, TB * s + t + 1)
                wait(dve, stack_hi, TB * s)
                nc.vector.tensor_tensor(rotated[:, t], rot_c[:, t], rot_s[:, t], ALU.add).then_inc(rot_done, 1)

            def stack_los(s, t):
                dve.wait_ge(stack_hi, TB * s + t + 1)
                wait(dve, group_ps, NF * s)
                nc.vector.tensor_tensor(q_stack(t)[:, :, 2:4], q_part(rotated, t),
                                        q_stack(t)[:, :, 0:2].bitcast(F32), ALU.subtract)
                nc.vector.tensor_tensor(k_stack(t)[:, :, :, 1], k_part(rotated, t),
                                        k_stack(t)[:, :, :, 0].bitcast(F32), ALU.subtract).then_inc(stack_lo, 1)

            def maxima(s, j):
                dve.wait_ge(s_ps, PAIRS * s + j + 1)
                for c, lo, hi in ((0, 0, P), (1, P, TRI)):
                    last = nc.vector.tensor_reduce(neg_max[:, c, 2 * j:2 * j + 2],
                                                   ring[:, 2 * (j % 2):2 * (j % 2) + 2, lo:hi],
                                                   AX_X, ALU.max, negate=True)
                last.then_inc(max_done, 1)

            def stack_maxima(s):
                dve_max.start(s)
                dve.wait_ge(max_done, PAIRS * (s + 1))
                wait(dve, maxT_ps, s)
                dve_max.inc(nc.vector.tensor_copy(max_stack[:, :, :, 0], neg_max[:]))
                dve_max.wait(dve)
                nc.vector.tensor_tensor(max_stack[:, :, :, 1], neg_max[:], max_stack[:, :, :, 0].bitcast(F32),
                                        ALU.subtract).then_inc(max_stacked, 1)
                dve_max.end()

            def norm_av(s, half):
                if half == 0:
                    dve_norm.start(s)
                dve.wait_ge(av_ps, PAIRS * s + (half + 1) * PAIRS // 2)
                if half == 0:
                    wait(dve, oT_ps, s)
                hn = NH // 2
                av = ps_av[:, 0:TB * hn * HV].rearrange("p (c h d) -> p c h d", c=TB, d=HV)
                dve_norm.inc(nc.vector.reciprocal(recip[:], av[:, :, :, HD]))
                dve_norm.wait(dve)
                nc.vector.tensor_tensor(o[:, :, half * hn:(half + 1) * hn], av[:, :, :, 0:HD],
                                        recip[:].unsqueeze(3).to_broadcast([P, TB, hn, HD]),
                                        ALU.mult).then_inc(av_norm, 1)

            def out_lo(s):
                dve.wait_ge(oT_hi_done, s + 1)
                wait(dve, out_ps, s)
                nc.vector.tensor_tensor(oT_lo[:].rearrange("p c n -> p (c n)"), ps_t[1][:],
                                        oT_hi[:].rearrange("p c n -> p (c n)").bitcast(F32),
                                        ALU.subtract).then_inc(oT_lo_done, 1)

            def out_add(s):
                dve_bias.start(s)
                tiles = x[:, ds(TB * s, TB)]
                if bias is not None:
                    dve_bias.inc(nc.vector.tensor_tensor(tiles, tiles, bias[:].unsqueeze(1).to_broadcast([P, TB, H]),
                                                         ALU.add))
                    dve_bias.wait(dve)
                dve.wait_ge(out_ps, s + 1)
                nc.vector.tensor_tensor(tiles, ps_p[:].rearrange("p (t n) -> p t n", t=TB), tiles,
                                        ALU.add).then_inc(out_added, 1)

            def sequence(s, p, before, after):
                if after:
                    ln_stats(s + 1)
                for j in range(PAIRS):
                    maxima(s, j)
                    if j == 1 and after:
                        ln_apply(s + 1)
                    if j == 2 and before:
                        out_lo(s - 1)
                    if j == 4 and after:
                        y_lo(s + 1)
                    if j == 5 and before:
                        out_add(s - 1)
                stack_maxima(s)
                if after:
                    for t in range(TB):
                        sum_squares(s + 1, t)
                        norm_qk(s + 1, t)
                    for t in range(TB):
                        rotate_cos(s + 1, t)
                        rotate_add(s + 1, t)
                        stack_los(s + 1, t)
                norm_av(s, 0)
                norm_av(s, 1)

            for i in range(2):
                last = nc.vector.memset(v[i][:], 1.0)
            last.then_inc(ones_set, 1)
            ln_stats(0)
            ln_apply(0)
            y_lo(0)
            for t in range(TB):
                sum_squares(0, t)
                norm_qk(0, t)
            for t in range(TB):
                rotate_cos(0, t)
                rotate_add(0, t)
                stack_los(0, t)
            sequence(0, 0, False, True)
            with dve.Fori(0, (B - 2) // 2) as r:
                for k in range(2):
                    sequence(2 * r + 1 + k, (1 + k) % 2, True, True)
            sequence(B - 1, (B - 1) % 2, True, False)
            out_lo(B - 1)
            out_add(B - 1)
            dve.wait_ge(out_added, B)

        @block.gpsimd
        def _(pool):
            def ln_rstd(s):
                pool_ln.start(s)
                pool.wait_ge(var_ready, s + 1)
                wait(pool, y_ready, s)
                passed(pool, waited_pool)
                pool_ln.inc(nc.gpsimd.tensor_scalar(var_eps[:], mv[:, :, 1], LN_EPS, None, ALU.add))
                pool_ln.wait(pool)
                nc.gpsimd.tensor_tensor(rstd[:], var_eps[:], half_neg[:].to_broadcast([P, TB]),
                                        ALU.pow).then_inc(rstd_ready, 1)

            def rms_rstd(s, t):
                if not multi:
                    return
                if t == 0:
                    pool_rs.start(s)
                pool.wait_ge(ss_done, TB * s + t + 1)
                wait(pool, qn_done, TB * s)
                passed(pool, waited_pool)
                pool_rs.inc(nc.gpsimd.tensor_scalar(ss_eps[:, t], ss[:, t], 1.0 / HD, 1e-6, ALU.mult, ALU.add))
                pool_rs.wait(pool)
                nc.gpsimd.tensor_tensor(rs[:, t], ss_eps[:, t], half_neg[:].to_broadcast([P, NH + NK]),
                                        ALU.pow).then_inc(rs_done, 1)

            def rotate_sin(s, t):
                half = HD // 2
                pool.wait_ge(qn_done, TB * s + t + 1)
                wait(pool, rot_done, TB * s)
                for (src, which), (dst, _) in zip(rot_parts(qn, t), rot_parts(rot_s, t)):
                    for a, b in ((0, half), (half, 0)):
                        last = nc.gpsimd.tensor_tensor(dst[:, :, :, a:a + half], src[:, :, :, b:b + half],
                                                       table(tab_s, t, which, src.shape[2], a, a + half), ALU.mult)
                last.then_inc(rot_s_done, 1)

            def cut(s, j):
                pool.wait_ge(exp_done, PAIRS * s + j + 1)
                passed(pool, waited_pool)
                diagonal = probs[:, j % 2].rearrange("p h (a k) -> p h a k", k=P)
                for a in (0, 2):
                    last = nc.gpsimd.affine_select(out=diagonal[:, :, a], in_=diagonal[:, :, a],
                                                   compare_op=ALU.is_ge, fill=0.0, base=0,
                                                   pattern=[[0, 2], [1, P]], channel_multiplier=-1)
                last.then_inc(cut_done, 1)

            def sequence(s, p, before, after):
                if after:
                    ln_rstd(s + 1)
                    for t in range(TB):
                        rms_rstd(s + 1, t)
                for j in range(PAIRS):
                    cut(s, j)
                    if j == 0 and after:
                        for t in range(TB):
                            rotate_sin(s + 1, t)

            ln_rstd(0)
            for t in range(TB):
                rms_rstd(0, t)
            for t in range(TB):
                rotate_sin(0, t)
            sequence(0, 0, False, True)
            with pool.Fori(0, (B - 2) // 2) as r:
                for k in range(2):
                    sequence(2 * r + 1 + k, (1 + k) % 2, True, True)
            sequence(B - 1, (B - 1) % 2, True, False)


def route(nc, env, layer, wts, E):
    x, ident, ident_r, half_neg, xT_hi, xT_lo, gatesT = (
        env["x"], env["ident"], env["ident_r"], env["half_neg"], env["xT_hi"], env["xT_lo"], env["gatesT"])
    wr_hi, wr_lo, bias = wts["router_hi"], wts["router_lo"], wts["router_bias"]
    pre = f"r{layer}_"
    with ExitStack() as ctx:
        def sb(name, shape, dt=F32):
            return ctx.enter_context(nc.sbuf_tensor(pre + name, shape, dt))

        stats = sb("stats", [P, TB, 6])
        mv = sb("mv", [P, NT, 2])
        pair_mv = sb("pair_mv", [P, TB, 2])
        var_eps = sb("var_eps", [P, NT])
        rstd = sb("rstd", [P, NT])
        y = sb("y", [P, 2, TB, H])
        yT_hi = sb("yT_hi", [P, 2, FC, N], F32R)
        yT_lo = sb("yT_lo", [P, 2, FC, N], F32R)
        logits = sb("logits", [P, NT, E])
        ps_y = [ctx.enter_context(nc.psum_tensor(pre + f"ps_y{i}", [P, 512], F32)) for i in range(2)]
        ps_l = [ctx.enter_context(nc.psum_tensor(pre + f"ps_l{i}", [P, 512], F32)) for i in range(2)]

        with semaphores(nc) as make_sem, ExitStack() as sems:
            def sem1(name):
                return make_sem(pre + name)

            stats_done = sem1("stats_done")
            waited_dve = sem1("waited_dve")
            pair_done = sem1("pair_done")
            var_ready = sem1("var_ready")
            rstd_ready = sem1("rstd_ready")
            pool_eps = sem1("pool_eps")
            y_ready = sem1("y_ready")
            yT_ps = sem1("yT_ps")
            hi_done = sem1("hi_done")
            lo_done = sem1("lo_done")
            l_ps = sem1("l_ps")
            l_done = sem1("l_done")
            stored = [sem1(f"stored{i}") for i in range(2)]
            block = sems.enter_context(nc.Block())

            @block.vector
            def _(dve):
                with dve.Fori(0, B) as s:
                    dve.wait_ge(var_ready, s)
                    for t in range(TB):
                        last = nc.vector.bn_stats(stats[:, t], x[:, ds(TB * s + t, 1)].rearrange("p a n -> p (a n)"))
                    last.then_inc(stats_done, 1)
                    dve.wait_ge(stats_done, s + 1)
                    passed(dve, waited_dve)
                    for t in range(TB):
                        last = nc.vector.bn_aggr(pair_mv[:, t], stats[:, t])
                    last.then_inc(pair_done, 1)
                    dve.wait_ge(pair_done, s + 1)
                    nc.vector.tensor_copy(mv[:, ds(TB * s, TB)], pair_mv[:]).then_inc(var_ready, 1)
                dve.wait_ge(rstd_ready, 1)
                with dve.Fori(0, B // 2) as r:
                    for p in range(2):
                        s = 2 * r + p
                        dve.wait_ge(yT_ps, 2 * r)
                        for t in range(TB):
                            last = nc.vector.tensor_scalar(
                                y[:, p, t], x[:, ds(TB * s + t, 1)].rearrange("p a n -> p (a n)"),
                                mv[:, ds(TB * s + t, 1), 0], rstd[:, ds(TB * s + t, 1)], ALU.subtract, ALU.mult)
                        last.then_inc(y_ready, 1)
                    for p in range(2):
                        s = 2 * r + p
                        dve.wait_ge(hi_done, s + 1)
                        dve.wait_ge(l_ps, 2 * r)
                        dve.wait_ge(stored[p], 32 * r)
                        nc.vector.tensor_tensor(yT_lo[:, p].rearrange("p c n -> p (c n)"), ps_y[p][:],
                                                yT_hi[:, p].rearrange("p c n -> p (c n)").bitcast(F32),
                                                ALU.subtract).then_inc(lo_done, 1)

            @block.gpsimd
            def _(pool):
                pool.wait_ge(var_ready, B)
                nc.gpsimd.tensor_scalar(var_eps[:], mv[:, :, 1], LN_EPS, None, ALU.add).then_inc(pool_eps, 1)
                pool.wait_ge(pool_eps, 1)
                nc.gpsimd.tensor_tensor(rstd[:], var_eps[:], half_neg[:].to_broadcast([P, NT]),
                                        ALU.pow).then_inc(rstd_ready, 1)

            @block.tensor
            def _(pe):
                with pe.Fori(0, B // 2) as r:
                    for p in range(2):
                        s = 2 * r + p
                        pe.wait_ge(y_ready, s + 1)
                        pe.wait_ge(lo_done, 2 * r)
                        for c in range(FC):
                            for t in range(TB):
                                last = nc.tensor.transpose(ps_y[p][:, c * N + t * P:c * N + (t + 1) * P],
                                                           y[:, p, t, c * P:(c + 1) * P], ident[:])
                        last.then_inc(yT_ps, 1)
                    for p in range(2):
                        s = 2 * r + p
                        pe.wait_ge(lo_done, s + 1)
                        pe.wait_ge(l_done, 2 * r)
                        for t in range(TB):
                            n = 0
                            for c in range(FC):
                                for a, w in split_passes(yT_hi, yT_lo, wr_hi, wr_lo):
                                    last = nc.tensor.matmul(ps_l[p][:, t * E:(t + 1) * E],
                                                            a[:, p, c, t * P:(t + 1) * P], w[:, c, :],
                                                            start=t == 0 and n == 0, stop=n == 3 * FC - 1,
                                                            skip_group_check=True)
                                    n += 1
                        last.then_inc(l_ps, 1)

            @block.scalar
            def _(act):
                with act.Fori(0, B // 2) as r:
                    for p in range(2):
                        s = 2 * r + p
                        act.wait_ge(yT_ps, s + 1)
                        act.wait_ge(l_ps, 2 * r)
                        act.wait_ge(stored[p], 32 * r)
                        nc.scalar.activation(yT_hi[:, p].rearrange("p c n -> p (c n)"), ps_y[p][:],
                                             ACT.Copy).then_inc(hi_done, 1)
                    for p in range(2):
                        s = 2 * r + p
                        act.wait_ge(l_ps, s + 1)
                        nc.scalar.activation(logits[:, ds(TB * s, TB)],
                                             ps_l[p][:, 0:TB * E].rearrange("p (t e) -> p t e", t=TB),
                                             ACT.Copy).then_inc(l_done, 1)

            @block.sync
            def _(sp):
                with sp.Fori(0, B // 2) as r:
                    for p in range(2):
                        s = 2 * r + p
                        sp.wait_ge(lo_done, s + 1)
                        sp.dma_start(xT_hi[:, :, ds(N * s, N)].bitcast(F32), yT_hi[:, p].bitcast(F32)).then_inc(stored[p], 16)
                        sp.dma_start(xT_lo[:, :, ds(N * s, N)].bitcast(F32), yT_lo[:, p].bitcast(F32)).then_inc(stored[p], 16)
                for p in range(2):
                    sp.wait_ge(stored[p], 32 * (B // 2))

        routing = route_top2 if layer == 0 else route_groups
        routing(nc, sb, logits, bias, env, E)


def store_gates(nc, dve, chain, gates, split, E):
    chain.wait(dve)
    chain.inc(nc.vector.tensor_copy(split[:, :, 0, 0:E], gates[:]))
    chain.wait(dve)
    chain.inc(nc.vector.tensor_tensor(split[:, :, 1, 0:E], gates[:], split[:, :, 0, 0:E].bitcast(F32),
                                      ALU.subtract))


def transpose_gates(nc, block, env, split, ps, gates_ready, count, ps_done, copied):
    ident_r, gatesT = env["ident_r"], env["gatesT"]

    @block.tensor
    def _(pe):
        pe.wait_ge(gates_ready, count)
        for g in range(NT // 4):
            if g >= 2:
                pe.wait_ge(copied, g - 1)
            for k in range(4):
                last = nc.tensor.transpose(ps[g % 2][0:64, k * P:(k + 1) * P].bitcast(F32R),
                                           split[:, 4 * g + k].rearrange("p s e -> p (s e)"), ident_r[:])
            last.then_inc(ps_done, 1)

    @block.scalar
    def _(act):
        for g in range(NT // 4):
            act.wait_ge(ps_done, g + 1)
            nc.scalar.activation(gatesT[:, g * 4 * P:(g + 1) * 4 * P], ps[g % 2][0:64, :],
                                 ACT.Copy).then_inc(copied, 1)
        act.wait_ge(copied, NT // 4)


def route_top2(nc, sb, logits, bias, env, E):
    EP = E + 8
    biased = sb("biased", [P, NT, EP])
    replaced = sb("replaced", [P, NT, EP])
    top = sb("top", [P, NT, 8])
    chosen = sb("chosen", [P, NT, E])
    lmax = sb("lmax", [P, NT])
    expo = sb("expo", [P, NT, E])
    total = sb("total", [P, NT])
    gates = sb("gates", [P, NT, E])
    split = sb("split", [P, NT, 2, 32], F32R)
    zero = sb("zero", [P, NT, 2, 32])
    ps = env["ps_gates"]
    with semaphores(nc) as make_sem, ExitStack() as ctx:
        steps = make_sem("r0_steps")
        shifted = make_sem("r0_shifted")
        exp_done = make_sem("r0_exp_done")
        ps_done = make_sem("r0_gates_ps")
        copied = make_sem("r0_gates_copied")
        tensors = [ctx.enter_context(nc.psum_tensor(f"{n}", [P, 512], F32)) for n in ps]
        block = ctx.enter_context(nc.Block())
        count = 16

        def bc(ap):
            return ap.unsqueeze(2).to_broadcast([P, NT, E])

        @block.vector
        def _(dve):
            ch = Chain(steps, count)
            ch.start(0)
            ch.inc(nc.vector.memset(zero[:], 0.0))
            nc.vector.memset(biased[:, :, E:EP], BIG)
            ch.inc(nc.vector.tensor_tensor(biased[:, :, 0:E], logits[:],
                                           bias[:].unsqueeze(1).to_broadcast([P, NT, E]), ALU.add))
            ch.inc(nc.vector.tensor_reduce(lmax[:], logits[:], AX_X, ALU.max))
            ch.wait(dve)
            nc.vector.tensor_copy(split[:], zero[:])
            nc.vector.tensor_tensor(expo[:], logits[:], bc(lmax[:]), ALU.subtract).then_inc(shifted, 1)
            for t in range(NT):
                last = nc.vector.max(top[:, t], biased[:, t, 0:E])
            ch.inc(last)
            ch.wait(dve)
            ch.inc(nc.vector.memset(top[:, :, 2:8], BIG))
            ch.wait(dve)
            for t in range(NT):
                last = nc.vector.match_replace(replaced[:, t], in_to_replace=top[:, t], in_values=biased[:, t],
                                               imm_value=-BIG)
            ch.inc(last)
            ch.wait(dve)
            ch.inc(nc.vector.tensor_tensor(chosen[:], replaced[:, :, 0:E], biased[:, :, 0:E], ALU.not_equal))
            dve.wait_ge(exp_done, 1)
            ch.inc(nc.vector.tensor_reduce(total[:], expo[:], AX_X, ALU.add))
            ch.wait(dve)
            ch.inc(nc.vector.reciprocal(total[:], total[:]))
            ch.wait(dve)
            ch.inc(nc.vector.tensor_tensor(expo[:], expo[:], bc(total[:]), ALU.mult))
            ch.wait(dve)
            ch.inc(nc.vector.tensor_tensor(gates[:], expo[:], chosen[:], ALU.mult))
            ch.wait(dve)
            ch.inc(nc.vector.tensor_reduce(total[:], gates[:], AX_X, ALU.add))
            ch.wait(dve)
            ch.inc(nc.vector.reciprocal(total[:], total[:]))
            ch.wait(dve)
            ch.inc(nc.vector.tensor_tensor(gates[:], gates[:], bc(total[:]), ALU.mult))
            store_gates(nc, dve, ch, gates, split, E)
            assert ch.n == count, ch.n

        @block.scalar
        def _(act):
            act.wait_ge(shifted, 1)
            nc.scalar.activation(expo[:], expo[:], ACT.Exp).then_inc(exp_done, 1)

        transpose_gates(nc, block, env, split, tensors, steps, count, ps_done, copied)


def route_groups(nc, sb, logits, bias, env, E):
    G, TOPG, K, SCALE = 8, 4, 8, 2.5
    EG = E // G
    scores = sb("scores", [P, NT, E])
    biased = sb("biased", [P, NT, E])
    pair_max = sb("pair_max", [P, NT, G, 2])
    pair_min = sb("pair_min", [P, NT, G, 2])
    first = sb("first", [P, NT, G])
    second = sb("second", [P, NT, G])
    second_low = sb("second_low", [P, NT, G])
    group = sb("group", [P, NT, 2 * G])
    group_out = sb("group_out", [P, NT, 2 * G])
    group_on = sb("group_on", [P, NT, G])
    top = sb("top", [P, NT, 8])
    masked = sb("masked", [P, NT, E])
    replaced = sb("replaced", [P, NT, E])
    chosen = sb("chosen", [P, NT, E])
    total = sb("total", [P, NT])
    gates = sb("gates", [P, NT, E])
    split = sb("split", [P, NT, 2, 32], F32R)
    ps = env["ps_gates"]
    with semaphores(nc) as make_sem, ExitStack() as ctx:
        steps = make_sem("r1_steps")
        sig_done = make_sem("r1_sig_done")
        ps_done = make_sem("r1_gates_ps")
        copied = make_sem("r1_gates_copied")
        tensors = [ctx.enter_context(nc.psum_tensor(f"{n}", [P, 512], F32)) for n in ps]
        block = ctx.enter_context(nc.Block())
        count = 21

        @block.vector
        def _(dve):
            ch = Chain(steps, count)
            ch.start(0)

            def step(ins):
                ch.inc(ins)
                ch.wait(dve)

            dve.wait_ge(sig_done, 1)
            nc.vector.memset(group[:, :, G:], BIG)
            step(nc.vector.tensor_tensor(biased[:], scores[:], bias[:].unsqueeze(1).to_broadcast([P, NT, E]),
                                         ALU.add))
            quad = biased[:].rearrange("p t (g a b) -> p (t g) a b", a=2, b=2)
            pmx = pair_max[:].rearrange("p t g a -> p (t g) a")
            pmn = pair_min[:].rearrange("p t g a -> p (t g) a")
            nc.vector.tensor_tensor(pmx, quad[:, :, :, 0], quad[:, :, :, 1], ALU.max)
            step(nc.vector.tensor_tensor(pmn, quad[:, :, :, 0], quad[:, :, :, 1], ALU.min))
            f, s, lo = (a[:].rearrange("p t g -> p (t g)") for a in (first, second, second_low))
            nc.vector.tensor_tensor(f, pmx[:, :, 0], pmx[:, :, 1], ALU.max)
            nc.vector.tensor_tensor(s, pmx[:, :, 0], pmx[:, :, 1], ALU.min)
            step(nc.vector.tensor_tensor(lo, pmn[:, :, 0], pmn[:, :, 1], ALU.max))
            step(nc.vector.tensor_tensor(s, s, lo, ALU.max))
            step(nc.vector.tensor_tensor(group[:, :, 0:G], first[:], second[:], ALU.add))
            for t in range(NT):
                last = nc.vector.max(top[:, t], group[:, t, 0:G])
            step(last)
            step(nc.vector.memset(top[:, :, TOPG:8], BIG))
            for t in range(NT):
                last = nc.vector.match_replace(group_out[:, t], in_to_replace=top[:, t], in_values=group[:, t],
                                               imm_value=-BIG)
            step(last)
            step(nc.vector.tensor_tensor(group_on[:], group_out[:, :, 0:G], group[:, :, 0:G], ALU.not_equal))
            step(nc.vector.tensor_tensor(
                masked[:].rearrange("p t (g e) -> p (t g) e", e=EG),
                biased[:].rearrange("p t (g e) -> p (t g) e", e=EG),
                group_on[:].rearrange("p t g -> p (t g)").unsqueeze(2).to_broadcast([P, NT * G, EG]), ALU.mult))
            step(nc.vector.tensor_scalar(masked[:], masked[:], 0.0, None, ALU.add))
            for t in range(NT):
                last = nc.vector.max(top[:, t], masked[:, t])
            step(last)
            for t in range(NT):
                last = nc.vector.match_replace(replaced[:, t], in_to_replace=top[:, t], in_values=masked[:, t],
                                               imm_value=-BIG)
            step(last)
            step(nc.vector.tensor_tensor(chosen[:], replaced[:], masked[:], ALU.not_equal))
            step(nc.vector.tensor_tensor(gates[:], scores[:], chosen[:], ALU.mult))
            step(nc.vector.tensor_reduce(total[:], gates[:], AX_X, ALU.add))
            step(nc.vector.reciprocal(total[:], total[:]))
            step(nc.vector.tensor_tensor(gates[:], gates[:], total[:].unsqueeze(2).to_broadcast([P, NT, E]),
                                         ALU.mult))
            step(nc.vector.tensor_scalar(gates[:], gates[:], SCALE, None, ALU.mult))
            store_gates(nc, dve, ch, gates, split, E)
            assert ch.n == count, ch.n

        @block.scalar
        def _(act):
            nc.scalar.activation(scores[:], logits[:], ACT.Sigmoid).then_inc(sig_done, 1)

        transpose_gates(nc, block, env, split, tensors, steps, count, ps_done, copied)


def experts(nc, env, layer, w_all, E, out=None):
    x, xT_hi, xT_lo, gatesT, sel_exp = env["x"], env["xT_hi"], env["xT_lo"], env["gatesT"], env["sel_exp"]
    NE = E + 2
    ITEMS = 2 * NE
    SHARED = 4
    pre = f"e{layer}_"
    with semaphores(nc) as make_sem, ExitStack() as ctx:
        def sb(name, shape, dt=F32):
            return ctx.enter_context(nc.sbuf_tensor(pre + name, shape, dt))

        def sem(name):
            return make_sem(pre + name)

        raw = [sb(f"raw{i}", [P, WCOLS]) for i in range(2)]
        w_hi = [sb(f"w_hi{i}", [P, WCOLS], F32R) for i in range(2)]
        w_lo = [sb(f"w_lo{i}", [P, WCOLS], F32R) for i in range(2)]
        sel = [sb(f"sel{i}", [64, P], F32R) for i in range(2)]
        act_out = [sb(f"act_out{i}", [P, BLK]) for i in range(2)]
        prod = sb("prod", [P, BLK])
        hid = [sb(f"hid{i}", [P, BLK]) for i in range(2)]
        hid_hi = [sb(f"hid_hi{i}", [P, BLK], F32R) for i in range(2)]
        hid_lo = [sb(f"hid_lo{i}", [P, BLK], F32R) for i in range(2)]
        acc = ctx.enter_context(nc.psum_tensor(pre + "acc", [P, HALF // P, H], F32))
        ps_a = ctx.enter_context(nc.psum_tensor(pre + "ps_a", [P, BLK], F32))
        ps_b = ctx.enter_context(nc.psum_tensor(pre + "ps_b", [P, BLK], F32))
        ps_g = ctx.enter_context(nc.psum_tensor(pre + "ps_g", [P, BLK], F32))

        w_loaded = [sem(f"w_loaded{i}") for i in range(2)]
        w_hi_done = sem("w_hi_done")
        w_lo_done = sem("w_lo_done")
        a_ps = sem("a_ps")
        b_ps = sem("b_ps")
        act_done = sem("act_done")
        prod_done = sem("prod_done")
        hid_done = sem("hid_done")
        hi_done = sem("hi_done")
        lo_done = sem("lo_done")
        down_ps = sem("down_ps")
        added = sem("added")
        stored = sem("stored")
        block = ctx.enter_context(nc.Block())

        A, Bc, D = 0, FC * P, 2 * FC * P

        def item_of(hf, n, blk):
            return hf * ITEMS + 2 * n + blk

        def expert_of(hf, n):
            return hf * NE + n

        @block.sync
        def _(sp):
            def load(k, n):
                sp.dma_start(raw[k][:], w_all[ds(n, 1)].rearrange("e p n -> p (e n)")).then_inc(w_loaded[k], 16)

            with sp.Fori(0, HALVES) as hf:
                with sp.Fori(0, NE // 2) as r:
                    for k in range(2):
                        sp.wait_ge(w_lo_done, expert_of(hf, 2 * r))
                        load(k, 2 * r + k)
            sp.wait_ge(w_lo_done, HALVES * NE)
            load(0, 0)

        @block.gpsimd
        def _(pool):
            def split_lo(k, m, gated=None):
                pool.wait_ge(w_hi_done, m + 1)
                wait(pool, down_ps, 2 * m - 2)
                if gated is not None:
                    nc.gpsimd.tensor_copy(sel[k][:], sel_exp[:, ds(gated, 1)].rearrange("p e n -> p (e n)"))
                nc.gpsimd.tensor_tensor(w_lo[k][:], raw[k][:], w_hi[k][:].bitcast(F32),
                                        ALU.subtract).then_inc(w_lo_done, 1)

            split_lo(0, 0)
            with pool.Fori(0, HALVES) as hf:
                split_lo(1, expert_of(hf, 1))
                with pool.Fori(1, NE // 2) as r:
                    for k in range(2):
                        split_lo(k, expert_of(hf, 2 * r + k), 2 * r + k - 2)
                split_lo(0, expert_of(hf, NE))
                if out is not None:
                    pool.wait_ge(added, hf + 1)
                    rows = ds(hf * (HALF // P), HALF // P)
                    pool.dma_start(out.rearrange("b (t p) n -> p (b t) n", p=P)[:, rows],
                                   x[:, rows]).then_inc(stored, 16)
            pool.wait_ge(w_lo_done, HALVES * NE + 1)
            if out is not None:
                pool.wait_ge(stored, 16 * HALVES)

        @block.scalar
        def _(act):
            def split_hi(k, m, turn):
                act.wait_ge(w_loaded[k], 16 * (turn + 1))
                wait(act, down_ps, 2 * m - 2)
                nc.scalar.activation(w_hi[k][:], raw[k][:], ACT.Copy).then_inc(w_hi_done, 1)

            def silu(hf, n, blk):
                i = item_of(hf, n, blk)
                act.wait_ge(a_ps, i + 1)
                act.wait_ge(hid_done, item_of(hf, n, 0))
                nc.scalar.activation(act_out[blk][:], ps_a[:], ACT.Silu).then_inc(act_done, 1)

            def hidden_hi(hf, n, blk):
                i = item_of(hf, n, blk)
                act.wait_ge(hid_done, i + 1)
                act.wait_ge(down_ps, item_of(hf, n, 0))
                nc.scalar.activation(hid_hi[blk][:], hid[blk][:], ACT.Copy).then_inc(hi_done, 1)

            split_hi(0, 0, 0)
            with act.Fori(0, HALVES) as hf:
                for k in range(2):
                    silu(hf, k, 0)
                    hidden_hi(hf, k, 0)
                    split_hi(1 - k, expert_of(hf, k + 1), hf * (NE // 2) + k)
                    silu(hf, k, 1)
                    hidden_hi(hf, k, 1)
                with act.Fori(1, NE // 2) as r:
                    for k in range(2):
                        n = 2 * r + k
                        silu(hf, n, 0)
                        hidden_hi(hf, n, 0)
                        split_hi(1 - k, expert_of(hf, n + 1), hf * (NE // 2) + r + k)
                        silu(hf, n, 1)
                        hidden_hi(hf, n, 1)

        @block.vector
        def _(dve):
            def hidden(hf, n, blk, gated=None):
                i = item_of(hf, n, blk)
                dve.wait_ge(act_done, i + 1)
                dve.wait_ge(b_ps, i + 1)
                dve.wait_ge(lo_done, item_of(hf, n, 0))
                if gated is None:
                    nc.vector.tensor_tensor(hid[blk][:], ps_b[:], act_out[blk][:], ALU.mult).then_inc(hid_done, 1)
                else:
                    dve.wait_ge(hid_done, i)
                    nc.vector.tensor_tensor(prod[:], ps_b[:], act_out[blk][:], ALU.mult).then_inc(prod_done, 1)
                    dve.wait_ge(prod_done, hf * (ITEMS - SHARED) + 2 * gated + blk + 1)
                    nc.vector.tensor_tensor(hid[blk][:], ps_g[:], prod[:], ALU.mult).then_inc(hid_done, 1)
                dve.wait_ge(hi_done, i + 1)
                nc.vector.tensor_tensor(hid_lo[blk][:], hid[blk][:], hid_hi[blk][:].bitcast(F32),
                                        ALU.subtract).then_inc(lo_done, 1)

            with dve.Fori(0, HALVES) as hf:
                for k in range(2):
                    for blk in range(2):
                        hidden(hf, k, blk)
                with dve.Fori(0, E // 2) as r:
                    for k in range(2):
                        for blk in range(2):
                            hidden(hf, 2 * r + k + 2, blk, 2 * r + k)
                dve.wait_ge(down_ps, (hf + 1) * ITEMS)
                for q in range(HALF // P // 2):
                    tiles = x[:, ds(hf * (HALF // P) + 2 * q, 2)]
                    last = nc.vector.tensor_tensor(tiles, acc[:, 2 * q:2 * q + 2], tiles, ALU.add)
                last.then_inc(added, 1)
            dve.wait_ge(added, HALVES)

        @block.tensor
        def _(pe):
            def up(hf, n, k, blk, shared):
                i = item_of(hf, n, blk)
                tokens = ds(hf * HALF + blk * BLK, BLK)
                if blk == 0:
                    pe.wait_ge(w_lo_done, hf * NE + n + 1)
                pe.wait_ge(act_done, i)
                for col, ps in ((A, ps_a), (Bc, ps_b)):
                    if col == Bc:
                        pe.wait_ge(hid_done, i)
                    m = 0
                    for c in range(FC):
                        for w, a in split_passes(w_hi[k], w_lo[k], xT_hi, xT_lo):
                            last = nc.tensor.matmul(ps[:], w[:, col + c * P:col + (c + 1) * P], a[:, c, tokens],
                                                    start=m == 0, stop=m == 3 * FC - 1)
                            m += 1
                    if col == A:
                        last.then_inc(a_ps, 1)
                if not shared:
                    last = nc.tensor.matmul(ps_g[:], sel[k][:], gatesT[:, tokens], start=True, stop=True)
                last.then_inc(b_ps, 1)

            def down(hf, i, k, blk, first=False):
                pe.wait_ge(lo_done, i + 1)
                if first:
                    pe.wait_ge(added, hf)
                for q in range(BLK // P):
                    at = blk * (BLK // P) + q
                    m = 0
                    for a, w in split_passes(hid_hi[blk], hid_lo[blk], w_hi[k], w_lo[k]):
                        last = nc.tensor.matmul(acc[:, at], a[:, q * P:(q + 1) * P], w[:, D:D + H],
                                                start=first and m == 0 and q % 2 == 0, stop=False,
                                                skip_group_check=True)
                        m += 1
                last.then_inc(down_ps, 1)

            with pe.Fori(0, HALVES) as hf:
                for k in range(2):
                    for blk in range(2):
                        up(hf, k, k, blk, True)
                        if (k, blk) != (0, 0):
                            n, pb = divmod(2 * k + blk - 1, 2)
                            down(hf, item_of(hf, n, pb), n, pb, first=n == 0)
                with pe.Fori(1, NE // 2) as r:
                    for k in range(2):
                        for blk in range(2):
                            up(hf, 2 * r + k, k, blk, False)
                            down(hf, item_of(hf, 2 * r + k, blk) - 1, k if blk else 1 - k, 1 - blk)
                down(hf, item_of(hf, NE - 1, 1), 1, 1)


def layers(nc, a, out):
    with ExitStack() as ctx:
        def sb(name, shape, dt=F32):
            return ctx.enter_context(nc.sbuf_tensor(name, shape, dt))

        env = {
            "x": sb("x", [P, NT, H]), "ident": sb("ident", [P, P]), "ident_r": sb("ident_r", [P, P], F32R),
            "mask_r": sb("mask_r", [P, P], F32R), "sel_head": sb("sel_head", [2 * NH, NH, P], F32R),
            "sel_exp": sb("sel_exp", [64, 32, P], F32R), "half_neg": sb("half_neg", [P, 1]),
            "ps_gates": ["ps_gates0", "ps_gates1"],
        }
        setup(nc, env, a["x"])
        for layer in range(2):
            qkv = 3 * H if layer == 0 else H + 2 * HD
            with ExitStack() as part:
                def psb(name, shape, dt=F32):
                    return part.enter_context(nc.sbuf_tensor(f"w{layer}_{name}", shape, dt))

                wts = {"qkv_hi": psb("qkv_hi", [P, FC, qkv], F32R), "qkv_lo": psb("qkv_lo", [P, FC, qkv], F32R),
                       "out_hi": psb("out_hi", [P, FC, H], F32R), "out_lo": psb("out_lo", [P, FC, H], F32R),
                       "tab_c": psb("tab_c", [P, TB, 2, HD]), "tab_s": psb("tab_s", [P, TB, 2, HD])}
                load_split(nc, [
                    (a[f"qkv{layer}"].rearrange("(c p) n -> p c n", p=P), [P, FC, qkv], wts["qkv_hi"], wts["qkv_lo"]),
                    (a[f"out{layer}"].rearrange("(c p) n -> p c n", p=P), [P, FC, H], wts["out_hi"], wts["out_lo"])],
                    f"l{layer}a")
                if layer == 0:
                    rope_tables(nc, a["rope_cos"], a["rope_sin"], a["q_gamma"], a["k_gamma"],
                                wts["tab_c"], wts["tab_s"])
                else:
                    wts["bias"] = psb("bias", [P, H])
                    load_tables(nc, [
                        (wts["tab_c"][:], a["xpos_cos"].rearrange("(t p) k d -> p t k d", p=P)),
                        (wts["tab_s"][:], a["xpos_sin"].rearrange("(t p) k d -> p t k d", p=P)),
                        (wts["bias"][:], a["b_proj"].partition_broadcast(P))], f"l{layer}a")
                attention(nc, env, layer, wts)
            E = 16 if layer == 0 else 32
            with ExitStack() as part:
                def psb(name, shape, dt=F32):
                    return part.enter_context(nc.sbuf_tensor(f"m{layer}_{name}", shape, dt))

                env["xT_hi"], env["xT_lo"] = psb("xT_hi", [P, FC, T], F32R), psb("xT_lo", [P, FC, T], F32R)
                env["gatesT"] = psb("gatesT", [64, T], F32R)
                env["ps_gates"] = [f"ps_gates{layer}{i}" for i in range(2)]
                wts = {"router_hi": psb("router_hi", [P, FC, E], F32R), "router_lo": psb("router_lo", [P, FC, E], F32R),
                       "router_bias": psb("router_bias", [P, E])}
                load_split(nc, [(a[f"router{layer}"].rearrange("(c p) n -> p c n", p=P), [P, FC, E],
                                 wts["router_hi"], wts["router_lo"])], f"l{layer}r")
                load_tables(nc, [(wts["router_bias"][:], a[f"router_bias{layer}"].partition_broadcast(P))],
                            f"l{layer}r")
                route(nc, env, layer, wts, E)
                experts(nc, env, layer, a[f"experts{layer}"], E, out if layer == 1 else None)


def position_tables():
    import numpy as np
    f = np.float32
    inv = (f(1.0) / f(10000.0) ** (np.arange(0, HD, 2, dtype=f) / f(HD))).astype(f)
    pos = np.arange(N, dtype=f)
    ang = (pos[:, None] * inv[None, :]).astype(f)
    ang = np.concatenate([ang, ang], -1)
    sign = np.concatenate([-np.ones(HD // 2, f), np.ones(HD // 2, f)])
    cos, sin = np.cos(ang).astype(f), (np.sin(ang) * sign).astype(f)
    base = ((np.arange(0, HD, 2, dtype=f) + f(0.4 * HD)) / f(1.4 * HD)).astype(f)
    power = ((pos - N // 2) / f(64)).astype(f)
    scale = (base[None, :] ** power[:, None]).astype(f)
    scale = np.concatenate([scale, scale], -1)
    both = np.stack([scale, (f(1.0) / scale).astype(f)], 1) * f(HD ** -0.5)
    return {"rope_cos": cos, "rope_sin": sin, "xpos_cos": (cos[:, None] * both).astype(f),
            "xpos_sin": (sin[:, None] * both).astype(f)}


def expert_layout(first, second, down, s_first, s_second, s_down):
    import numpy as np

    def pack(f, s, d):
        e = f.shape[0]
        def cut(w):
            return w.reshape(e, FC, P, P).transpose(0, 2, 1, 3).reshape(e, P, FC * P)
        return np.concatenate([cut(f), cut(s), d], -1)

    def halves(w):
        return np.stack([w[:, :P], w[:, P:]])

    shared = pack(halves(s_first), halves(s_second), s_down.reshape(2, P, H))
    return np.ascontiguousarray(np.concatenate([shared, pack(first, second, down)], 0))


def kernel(L0_attn_x, L0_attn_w_qkv, L0_attn_w_out, L0_attn_q_gamma, L0_attn_k_gamma, L0_ffn_router_w,
           L0_ffn_router_bias, L0_ffn_Wu, L0_ffn_Wg, L0_ffn_Wd, L0_ffn_Su, L0_ffn_Sg, L0_ffn_Sd, L1_attn_w_q,
           L1_attn_w_kv, L1_attn_w_proj, L1_attn_b_proj, L1_ffn_router_w, L1_ffn_router_bias, L1_ffn_w_gate,
           L1_ffn_w_up, L1_ffn_w_down, L1_ffn_sw_gate, L1_ffn_sw_up, L1_ffn_sw_down):
    import numpy as np
    import concourse.bacc as bacc
    from concourse import mybir as mb
    from concourse.bass_utils import run_bass_kernel_spmd

    g = np.asarray
    arrays = {
        "x": g(L0_attn_x), "qkv0": g(L0_attn_w_qkv), "out0": g(L0_attn_w_out),
        "q_gamma": g(L0_attn_q_gamma), "k_gamma": g(L0_attn_k_gamma),
        "router0": g(L0_ffn_router_w).T, "router_bias0": g(L0_ffn_router_bias),
        "experts0": expert_layout(g(L0_ffn_Wu), g(L0_ffn_Wg), g(L0_ffn_Wd), g(L0_ffn_Su)[0], g(L0_ffn_Sg)[0],
                                  g(L0_ffn_Sd)[0]),
        "qkv1": np.concatenate([g(L1_attn_w_q), g(L1_attn_w_kv)], 0).T, "out1": g(L1_attn_w_proj).T,
        "b_proj": g(L1_attn_b_proj), "router1": g(L1_ffn_router_w), "router_bias1": g(L1_ffn_router_bias),
        "experts1": expert_layout(g(L1_ffn_w_gate), g(L1_ffn_w_up), g(L1_ffn_w_down), g(L1_ffn_sw_gate),
                                  g(L1_ffn_sw_up), g(L1_ffn_sw_down)),
    }
    arrays.update(position_tables())
    arrays = {k: np.ascontiguousarray(v) for k, v in arrays.items()}
    nc = bacc.Bacc("TRN2", target_bir_lowering=False, num_devices=1)
    a = {k: nc.dram_tensor("in_" + k, v.shape, mb.dt.from_np(v.dtype), kind="ExternalInput").ap()
         for k, v in arrays.items()}
    out = nc.dram_tensor("out_0", (B, N, H), mb.dt.float32, kind="ExternalOutput").ap()
    layers(nc, a, out)
    r = run_bass_kernel_spmd(nc, [{"in_" + k: v for k, v in arrays.items()}], core_ids=[0])
    return r.results[0]["out_0"]
```

```python
from contextlib import ExitStack, contextmanager

import concourse.bass as bass
from concourse import mybir

F32 = mybir.dt.float32
F32R = mybir.dt.float32r
I32 = mybir.dt.int32
ALU = mybir.AluOpType
ACT = mybir.ActivationFunctionType
AX_X = mybir.AxisListType.X

P = 128
H = 256
FC = H // P
B, N = 8, 256
T = B * N
NT = T // P
TB = N // P
NH, HD = 16, 16
PAIRS = NH // 2
STK = 4 * HD
TRI = N + P
HV = 32
HALF_HEADS = NH // 2
NEG = -1e30
LN_EPS = 1e-5
RMS_EPS = 1e-6
RSQRT_GUESS = float(0x5F3759DF)
NEWTON = 3
BLK = 512
HALF = 2 * BLK
HALVES = T // HALF
WCOLS = 2 * FC * P + H
BIG = 3.0e38
NPB = 3
PE_ORDER = ("t0 t1 t2 a0 t3 a1 t4 a2 t5 a3 g0 t6 a4 h0 g1 t7 a5 g2 g3 a6 g4 g5 a7 g6 g7".split(),
            "t0 t1 t2 a0 t3 a1 t4 a2 g0 t5 a3 g1 t6 a4 h0 g2 t7 a5 g3 a6 g4 g5 a7".split())
ACT_ORDER = ("e0 e1 e2 e3 s0 e4 s1 e5 o0 c0 e6 c1 e7 c4 c5 o1".split(),
             "e0 e1 e2 e3 s0 e4 s1 c0 e5 o0 c1 e6 e7 c3 c4 o1".split())


def ds(start, size):
    return bass.DynSlice(start, size)


class Chain:

    def __init__(self, sem, per_round):
        self.sem, self.per_round = sem, per_round
        self.base = self.n = 0

    def start(self, r):
        self.base, self.n = r * self.per_round, 0

    def inc(self, ins):
        ins.then_inc(self.sem, 1)
        self.n += 1

    def wait(self, eng):
        eng.wait_ge(self.sem, self.base + self.n)

    def end(self):
        assert self.n == self.per_round, (self.n, self.per_round)


def wait(eng, sem, value):
    if isinstance(value, int) and value <= 0:
        return
    eng.wait_ge(sem, value)


@contextmanager
def semaphores(nc):
    used = []

    def make(name):
        used.append(nc.alloc_semaphore(name=name))
        return used[-1]

    yield make
    nc.clear_and_free_semaphores(used)
    nc.all_engine_barrier()


def passed(eng, sem):
    eng.sem_inc(sem, 1)


def split_passes(hi_a, lo_a, hi_b, lo_b):
    return ((hi_a, hi_b), (hi_a, lo_b), (lo_a, hi_b))


def setup(nc, env, x_in):
    x, ident, ident_r, mask_r, sel_head, sel_exp, half_neg = (
        env["x"], env["ident"], env["ident_r"], env["mask_r"], env["sel_head"], env["sel_exp"], env["half_neg"])
    with semaphores(nc) as make_sem, ExitStack() as ctx:
        tmp = ctx.enter_context(nc.sbuf_tensor("setup_tmp", [P, 32, P], F32))
        mask = ctx.enter_context(nc.sbuf_tensor("setup_mask", [P, P], F32))
        hd = ctx.enter_context(nc.sbuf_tensor("setup_head", [P, NH, P], F32))
        x_loaded = make_sem("x_loaded")
        made = make_sem("made")
        rounded = make_sem("rounded")
        block = ctx.enter_context(nc.Block())

        @block.sync
        def _(sp):
            sp.dma_start(x[:, :, :], x_in.rearrange("b (t p) n -> p (b t) n", p=P)).then_inc(x_loaded, 16)
            sp.wait_ge(x_loaded, 16)

        @block.gpsimd
        def _(pool):
            nc.gpsimd.memset(half_neg[:], -0.5)
            nc.gpsimd.memset(ident[:], 0.0)
            nc.gpsimd.memset(mask[:], 0.0)
            nc.gpsimd.memset(hd[:], 1.0)
            nc.gpsimd.memset(tmp[:], 0.0).then_inc(made, 1)
            pool.wait_ge(made, 1)
            nc.gpsimd.affine_select(out=ident[:], in_=ident[:], compare_op=ALU.not_equal, fill=1.0, base=0,
                                    pattern=[[-1, P]], channel_multiplier=1).then_inc(made, 1)
            nc.gpsimd.affine_select(out=mask[:], in_=mask[:], compare_op=ALU.is_ge, fill=NEG, base=0,
                                    pattern=[[-1, P]], channel_multiplier=1).then_inc(made, 1)
            nc.gpsimd.affine_select(out=hd[:], in_=hd[:], compare_op=ALU.is_ge, fill=0.0, base=0,
                                    pattern=[[-2, NH], [0, P]], channel_multiplier=1).then_inc(made, 1)
            pool.wait_ge(made, 4)
            nc.gpsimd.affine_select(out=hd[:], in_=hd[:], compare_op=ALU.is_ge, fill=0.0, base=1,
                                    pattern=[[2, NH], [0, P]], channel_multiplier=-1).then_inc(made, 1)
            nc.gpsimd.affine_select(out=tmp[:], in_=tmp[:], compare_op=ALU.not_equal, fill=1.0, base=0,
                                    pattern=[[-1, 32], [0, P]], channel_multiplier=1).then_inc(made, 1)
            pool.wait_ge(made, 6)
            nc.gpsimd.affine_select(out=tmp[:], in_=tmp[:], compare_op=ALU.not_equal, fill=1.0, base=-32,
                                    pattern=[[-1, 32], [0, P]], channel_multiplier=1).then_inc(made, 1)

        @block.vector
        def _(dve):
            dve.wait_ge(made, 7)
            nc.vector.tensor_copy(ident_r[:], ident[:])
            nc.vector.tensor_copy(mask_r[:], mask[:])
            nc.vector.tensor_copy(sel_head[:], hd[:])
            nc.vector.tensor_copy(sel_exp[:], tmp[0:64, :, :]).then_inc(rounded, 1)
            dve.wait_ge(rounded, 1)


def load_split(nc, weights, pre):
    with semaphores(nc) as make_sem, ExitStack() as ctx:
        raws = [ctx.enter_context(nc.sbuf_tensor(f"{pre}_raw{i}", w[1], F32)) for i, w in enumerate(weights)]
        loaded = [make_sem(f"{pre}_loaded{i}") for i in range(len(weights))]
        hi_done = make_sem(f"{pre}_hi_done")
        lo_done = make_sem(f"{pre}_lo_done")
        block = ctx.enter_context(nc.Block())

        @block.sync
        def _(sp):
            for (dram, *_), raw, sem in zip(weights, raws, loaded):
                sp.dma_start(raw[:], dram).then_inc(sem, 16)

        @block.scalar
        def _(act):
            for (_, _, hi, _), raw, sem in zip(weights, raws, loaded):
                act.wait_ge(sem, 16)
                nc.scalar.activation(hi[:], raw[:], ACT.Copy).then_inc(hi_done, 1)

        @block.vector
        def _(dve):
            for i, ((_, _, hi, lo), raw, sem) in enumerate(zip(weights, raws, loaded)):
                dve.wait_ge(sem, 16)
                dve.wait_ge(hi_done, i + 1)
                nc.vector.tensor_tensor(lo[:], raw[:], hi[:].bitcast(F32), ALU.subtract).then_inc(lo_done, 1)
            dve.wait_ge(lo_done, len(weights))


def rope_tables(nc, rope_c, rope_s, gam_q, gam_k, tab_c, tab_s):
    half = HD // 2
    with semaphores(nc) as make_sem, ExitStack() as ctx:
        cs = ctx.enter_context(nc.sbuf_tensor("rope_cs", [P, 2, TB, HD], F32))
        gam = ctx.enter_context(nc.sbuf_tensor("rope_gamma", [P, 2, HD], F32))
        loaded = make_sem("rope_loaded")
        done = make_sem("rope_done")
        block = ctx.enter_context(nc.Block())

        @block.sync
        def _(sp):
            sp.dma_start(cs[:, 0], rope_c.rearrange("(t p) d -> p t d", p=P)).then_inc(loaded, 16)
            sp.dma_start(cs[:, 1], rope_s.rearrange("(t p) d -> p t d", p=P)).then_inc(loaded, 16)
            sp.dma_start(gam[:, 0], gam_q.partition_broadcast(P)).then_inc(loaded, 16)
            sp.dma_start(gam[:, 1], gam_k.partition_broadcast(P)).then_inc(loaded, 16)

        @block.vector
        def _(dve):
            dve.wait_ge(loaded, 64)
            for t in range(TB):
                nc.vector.tensor_tensor(tab_c[:, t], gam[:], cs[:, 0, t].unsqueeze(1).to_broadcast([P, 2, HD]),
                                        ALU.mult)
                for a, b in ((0, half), (half, 0)):
                    last = nc.vector.tensor_tensor(
                        tab_s[:, t, :, a:a + half], gam[:, :, b:b + half],
                        cs[:, 1, t, a:a + half].unsqueeze(1).to_broadcast([P, 2, half]), ALU.mult)
            last.then_inc(done, 1)
            dve.wait_ge(done, 1)


def load_tables(nc, loads, pre):
    with semaphores(nc) as make_sem, ExitStack() as ctx:
        loaded = make_sem(f"{pre}_tables_loaded")
        block = ctx.enter_context(nc.Block())

        @block.sync
        def _(sp):
            for dst, src in loads:
                sp.dma_start(dst, src).then_inc(loaded, 16)
            sp.wait_ge(loaded, 16 * len(loads))


def attention(nc, env, layer, wts):
    x, ident, ident_r, mask_r, sel_head, half_neg = (
        env["x"], env["ident"], env["ident_r"], env["mask_r"], env["sel_head"], env["half_neg"])
    wqkv_hi, wqkv_lo, wout_hi, wout_lo, tab_c, tab_s = (
        wts["qkv_hi"], wts["qkv_lo"], wts["out_hi"], wts["out_lo"], wts["tab_c"], wts["tab_s"])
    bias = wts.get("bias")
    multi = layer == 0
    NK = NH if multi else 1
    QK = (NH + NK) * HD
    VW = NK * HD
    groups = [(0, 4, False), (4, 4, False)] + ([(8, 4, True), (12, 4, True)] if multi else [(8, 1, True)])
    NG = len(groups)
    NF = TB * NG
    key_groups = [i for i in range(NF) if groups[i % NG][2]]
    gs = [f"group{i}" for i in range(NF)]
    turns = ["half1", "oT", "yT", "qk1", "maxT"] + [
        "half0" if step[0] == "h" else gs[int(step[1:])] for step in PE_ORDER[layer] if step[0] in "gh"]
    bank = {name: i % 2 for i, name in enumerate(turns)}
    start_turns = ["yT", "qk1"] + gs
    first_turns = turns[2:]
    last_turns = ["half1", "oT", "maxT", "half0"]

    def uses(names, b):
        return sum(bank[n] == b for n in names)

    def turn(s, name):
        b = bank[name]
        names, before = turns, uses(start_turns, b) + uses(first_turns, b) + uses(turns, b) * (s - 1)
        if isinstance(s, int) and s == -1:
            names, before = start_turns, 0
        elif isinstance(s, int) and s == 0:
            names, before = first_turns, uses(start_turns, b)
        elif isinstance(s, int) and s == B - 1:
            names = last_turns
        elif isinstance(s, int) and s == B:
            before += uses(last_turns, b) - uses(turns, b)
        return before + uses(names[:names.index(name)], b)

    exp_scale = HD ** -0.5 if multi else 1.0
    pre = f"a{layer}_"

    with semaphores(nc) as make_sem, ExitStack() as ctx:
        def sb(name, shape, dt=F32):
            return ctx.enter_context(nc.sbuf_tensor(pre + name, shape, dt))

        def pb(name, shape):
            return ctx.enter_context(nc.psum_tensor(pre + name, shape, F32))

        def sem(name):
            return make_sem(pre + name)

        stats = sb("stats", [P, TB, 6])
        mv = sb("mv", [P, TB, 2])
        var_eps = sb("var_eps", [P, TB])
        rstd = sb("rstd", [P, TB])
        y = sb("y", [P, TB, H])
        yT_hi = sb("yT_hi", [P, FC, N], F32R)
        yT_lo = sb("yT_lo", [P, FC, N], F32R)
        sq = sb("sq", [P, TB, QK])
        ss = sb("ss", [P, TB, NH + NK])
        ss_eps = sb("ss_eps", [P, TB, NH + NK])
        rs = sb("rs", [P, TB, NH + NK])
        rs_step = sb("rs_step", [P, TB, NH + NK])
        qn = sb("qn", [P, TB, QK])
        rot_c = sb("rot_c", [P, TB, QK])
        rot_s = sb("rot_s", [P, TB, QK])
        rotated = sb("rotated", [P, TB, QK])
        pieces = NH // 2 + (NK // 2 if multi else 1)
        stack = sb("stack", [P, TB, pieces * P], F32R)
        qT = [sb(f"qT{i}", [P, PAIRS, N], F32R) for i in range(2)]
        kT = [sb(f"kT{i}", [P, PAIRS if multi else 1, 2, N], F32R) for i in range(2)]
        zero = sb("zero", [P, 1])
        v = [sb(f"v{i}", [P, TB, NK, HV]) for i in range(2)]
        neg_max = sb("neg_max", [P, TB, NH])
        max_stack = sb("max_stack", [P, TB, NH, 2], F32R)
        maxT = sb("maxT", [P, N], F32R)
        probs = sb("probs", [P, NPB, 2, TRI])
        av_sb = [sb(f"av_sb{i}", [P, 2, N]) for i in range(2)]
        recip = sb("recip", [P, 2, TB, HALF_HEADS])
        o = sb("o", [P, TB, NH, HD])
        oT_hi = sb("oT_hi", [P, FC, N], F32R)
        oT_lo = sb("oT_lo", [P, FC, N], F32R)

        ring = pb("ring", [P, 4, 512])
        ps_av = pb("ps_av", [P, 512])
        ps_t = [pb(f"ps_t{i}", [P, 512]) for i in range(2)]
        ps_p = pb("ps_p", [P, 512])

        t_out = [sem(f"t_out{i}") for i in range(2)]
        y_ready = sem("y_ready")
        yT_ps = sem("yT_ps")
        yT_hi_done = sem("yT_hi_done")
        qk_ps = sem("qk_ps")
        v_ps = sem("v_ps")
        v_done = sem("v_done")
        var_ready = sem("var_ready")
        rstd_ready = sem("rstd_ready")
        sq_done = sem("sq_done")
        ss_done = sem("ss_done")
        qn_done = sem("qn_done")
        rot_s_done = sem("rot_s_done")
        rot_done = sem("rot_done")
        stack_hi = sem("stack_hi")
        stack_lo = sem("stack_lo")
        group_ps = sem("group_ps")
        s_ps = sem("s_ps")
        max_done = sem("max_done")
        max_stacked = sem("max_stacked")
        maxT_ps = sem("maxT_ps")
        st_ps = sem("st_ps")
        exp_done = sem("exp_done")
        cut_done = sem("cut_done")
        av_ps = sem("av_ps")
        av_out = sem("av_out")
        half_ps = sem("half_ps")
        oT_ps = sem("oT_ps")
        oT_hi_done = sem("oT_hi_done")
        out_ps = sem("out_ps")
        out_added = sem("out_added")
        constants = sem("constants")
        waited_dve = sem("waited_dve")
        waited_pool = sem("waited_pool")
        dve_ln = Chain(sem("dve_ln"), 1)
        dve_rs = Chain(sem("dve_rs"), 2 + 3 * NEWTON)
        pool_ln = Chain(sem("pool_ln"), 1)
        dve_max = Chain(sem("dve_max"), 1)
        dve_norm = Chain(sem("dve_norm"), 2)
        dve_rot = Chain(sem("dve_rot"), TB + 1)
        dve_bias = Chain(sem("dve_bias"), 1)
        block = ctx.enter_context(nc.Block())

        def turn_free(eng, s, name):
            wait(eng, t_out[bank[name]], turn(s, name))

        def turn_done(eng, s, name):
            eng.wait_ge(t_out[bank[name]], turn(s, name) + 1)

        def t_bank(name):
            return ps_t[bank[name]]

        def groups_done(eng, s):
            turn_done(eng, s - 1, gs[-1])
            turn_done(eng, s - 1, gs[-2])

        def qn_ready(eng, s, t):
            if t == 0:
                eng.wait_ge(qn_done, s + 1)
            else:
                turn_done(eng, s - 1, "qk1")

        def head_view(ap, t):
            return ap[:, t, :].rearrange("p (k h d) -> p k h d", k=2, d=HD)

        def rot_parts(ap, t):
            if multi:
                return [(head_view(ap, t), slice(0, 2))]
            q = ap[:, t, 0:NH * HD].rearrange("p (k h d) -> p k h d", k=1, d=HD)
            k = ap[:, t, NH * HD:QK].rearrange("p (k h d) -> p k h d", k=1, d=HD)
            return [(q, slice(0, 1)), (k, slice(1, 2))]

        def table(tab, t, which, heads, lo=0, hi=HD):
            k = which.stop - which.start
            return tab[:, t, which, lo:hi].unsqueeze(2).to_broadcast([P, k, heads, hi - lo])

        def rotate_sin(eng, ops, s, t):
            half = HD // 2
            qn_ready(eng, s, t)
            for (src, which), (dst, _) in zip(rot_parts(qn, t), rot_parts(rot_s, t)):
                for a, b in ((0, half), (half, 0)):
                    last = ops.tensor_tensor(dst[:, :, :, a:a + half], src[:, :, :, b:b + half],
                                             table(tab_s, t, which, src.shape[2], a, a + half), ALU.mult)
            return last

        def q_stack(t):
            return stack[:, t, 0:NH * STK].rearrange("p (h r d) -> p h r d", r=4, d=HD)

        def k_stack(t):
            if multi:
                return stack[:, t, NH * STK:].rearrange("p (h r s d) -> p h r s d", r=2, s=2, d=HD)
            return stack[:, t, NH * STK:].rearrange("p (c r s d) -> p c r s d", c=2, r=2, s=2, d=HD)

        def q_part(ap, t):
            return ap[:, t, 0:NH * HD].rearrange("p (h d) -> p h d", d=HD).unsqueeze(2).to_broadcast([P, NH, 2, HD])

        def k_part(ap, t):
            c = ap[:, t, NH * HD:QK]
            if multi:
                return c.rearrange("p (h d) -> p h d", d=HD).unsqueeze(2).to_broadcast([P, NH, 2, HD])
            return c.unsqueeze(1).unsqueeze(1).to_broadcast([P, 2, 2, HD])

        @block.tensor
        def _(pe):
            def proj_transpose(s):
                pe.wait_ge(y_ready, s + 1)
                turn_free(pe, s - 1, "yT")
                for c in range(FC):
                    for t in range(TB):
                        last = nc.tensor.transpose(t_bank("yT")[:, c * N + t * P:c * N + (t + 1) * P],
                                                   y[:, t, c * P:(c + 1) * P], ident[:])
                last.then_inc(yT_ps, 1)

            def project(out, t, lo, hi, first):
                n = 0
                for c in range(FC):
                    for a, w in split_passes(yT_hi, yT_lo, wqkv_hi, wqkv_lo):
                        last = nc.tensor.matmul(out, a[:, c, t * P:(t + 1) * P], w[:, c, lo:hi],
                                                start=first and n == 0, stop=n == 3 * FC - 1,
                                                skip_group_check=True)
                        n += 1
                return last

            def proj_qk(s, t):
                if t == 0:
                    pe.wait_ge(v_done, s + 1)
                    out = ps_p
                else:
                    turn_free(pe, s - 1, "qk1")
                    out = t_bank("qk1")
                project(out[:, 0:QK], t, 0, QK, True).then_inc(qk_ps, 1)

            def proj_v(s):
                turn_done(pe, s - 1, "yT")
                wait(pe, qn_done, s)
                wait(pe, out_added, s - 1)
                for t in range(TB):
                    last = project(ps_p[:, t * VW:(t + 1) * VW], t, QK, QK + VW, t == 0)
                last.then_inc(v_ps, 1)

            def proj_group(s, i):
                t, g = divmod(i, NG)
                first, count, _ = groups[g]
                if g == 0:
                    pe.wait_ge(stack_hi, TB * s + t + 1)
                    pe.wait_ge(stack_lo, TB * s + t + 1)
                turn_free(pe, s - 1, gs[i])
                for k in range(count):
                    last = nc.tensor.transpose(t_bank(gs[i])[:, k * P:(k + 1) * P].bitcast(F32R),
                                               stack[:, t, (first + k) * P:(first + k + 1) * P], ident_r[:])
                last.then_inc(group_ps, 1)

            def keys(p, j, hh):
                return kT[p][:, j if multi else 0, hh]

            def scores(s, p, j):
                if j == 0:
                    groups_done(pe, s)
                    wait(pe, exp_done, PAIRS * s)
                if j >= 2:
                    pe.wait_ge(max_done, PAIRS * s + j - 1)
                for hh in range(2):
                    out = ring[:, 2 * (j % 2) + hh]
                    nc.tensor.matmul(out[:, 0:P], qT[p][:, j, 0:P], keys(p, j, hh)[:, 0:P],
                                     start=True, stop=False, skip_group_check=True)
                    nc.tensor.matmul(out[:, P:TRI], qT[p][:, j, P:N], keys(p, j, hh)[:, 0:N],
                                     start=False, stop=False, skip_group_check=True)
                    last = nc.tensor.matmul(
                        out[:, 0:2 * N].rearrange("p (a k) -> p a k", k=N)[:, :, 0:P], ident_r[:],
                        mask_r[:].unsqueeze(1).to_broadcast([P, 2, P]), start=False, stop=True,
                        skip_group_check=True)
                last.then_inc(s_ps, 1)

            def transpose_maxima(s):
                pe.wait_ge(max_stacked, s + 1)
                turn_free(pe, s, "maxT")
                for t in range(TB):
                    last = nc.tensor.transpose(t_bank("maxT")[0:2 * NH, t * P:(t + 1) * P].bitcast(F32R),
                                               max_stack[:, t].rearrange("p h s -> p (h s)"), ident_r[:])
                last.then_inc(maxT_ps, 1)

            def shifted_scores(s, p, j):
                if j == 0:
                    turn_done(pe, s, "maxT")
                    pe.wait_ge(max_done, PAIRS * (s + 1))
                if j >= 2:
                    pe.wait_ge(exp_done, PAIRS * s + j - 1)
                for hh in range(2):
                    out = ring[:, 2 * (j % 2) + hh]
                    nc.tensor.matmul(out[:, 0:N], keys(p, j, hh)[:, 0:P], qT[p][:, j, 0:N],
                                     start=True, stop=False, skip_group_check=True)
                    nc.tensor.matmul(out[:, N:TRI], keys(p, j, hh)[:, P:N], qT[p][:, j, P:N],
                                     start=False, stop=False, skip_group_check=True)
                    nc.tensor.matmul(out[:, 0:N], sel_head[:, 2 * j + hh], maxT[:, 0:N],
                                     start=False, stop=False, skip_group_check=True)
                    last = nc.tensor.matmul(out[:, N:TRI], sel_head[:, 2 * j + hh], maxT[:, P:N],
                                            start=False, stop=True, skip_group_check=True)
                last.then_inc(st_ps, 1)

            def attend(s, p, j):
                pe.wait_ge(cut_done, PAIRS * s + j + 1)
                if j == 0:
                    pe.wait_ge(v_done, s + 1)
                if j % (PAIRS // 2) == 0:
                    wait(pe, av_out, 2 * s + 2 * j // PAIRS)
                for hh in range(2):
                    h = 2 * j + hh
                    pr, vh, row, col = probs[:, j % NPB, hh], h if multi else 0, HV * (h % 4), N * (h // 4 % 2)
                    nc.tensor.matmul(ps_av[row:row + HV, col:col + N], v[p][:, 0, vh], pr[:, 0:N],
                                     start=col == 0, stop=False, skip_group_check=True)
                    last = nc.tensor.matmul(ps_av[row:row + HV, col + P:col + N], v[p][:, 1, vh], pr[:, N:TRI],
                                            start=False, stop=True, skip_group_check=True)
                last.then_inc(av_ps, 1)

            def half_transpose(s, half, during):
                pe.wait_ge(av_out, 2 * s + half + 1)
                turn_free(pe, during, f"half{half}")
                for t in range(TB):
                    for g in range(2):
                        at = (2 * t + g) * P
                        last = nc.tensor.transpose(t_bank(f"half{half}")[:, at:at + P],
                                                   av_sb[half][:, g, t * P:(t + 1) * P], ident[:])
                last.then_inc(half_ps, 1)

            def out_transpose(s):
                turn_done(pe, s, "half0")
                turn_done(pe, s + 1, "half1")
                turn_free(pe, s + 1, "oT")
                for c in range(FC):
                    for t in range(TB):
                        last = nc.tensor.transpose(
                            t_bank("oT")[:, c * N + t * P:c * N + (t + 1) * P],
                            o[:, t].rearrange("p h d -> p (h d)")[:, c * P:(c + 1) * P], ident[:])
                last.then_inc(oT_ps, 1)

            def out_project(s, qk_out):
                turn_done(pe, s + 1, "oT")
                pe.wait_ge(qn_done, qk_out)
                for t in range(TB):
                    n = 0
                    for c in range(FC):
                        for a, w in split_passes(oT_hi, oT_lo, wout_hi, wout_lo):
                            last = nc.tensor.matmul(ps_p[:, t * H:(t + 1) * H], a[:, c, t * P:(t + 1) * P],
                                                    w[:, c, :], start=t == 0 and n == 0,
                                                    stop=n == 3 * FC - 1, skip_group_check=True)
                            n += 1
                last.then_inc(out_ps, 1)

            def sequence(s, p, before, after):
                for j in range(PAIRS):
                    scores(s, p, j)
                    if j == 1 and before:
                        half_transpose(s - 1, 1, s)
                    if j == 2 and before:
                        out_transpose(s - 1)
                    if j == 3 and after:
                        proj_transpose(s + 1)
                    if j == 4 and before:
                        out_project(s - 1, s + 1)
                    if j == 6 and after:
                        proj_v(s + 1)
                if after:
                    proj_qk(s + 1, 0)
                    proj_qk(s + 1, 1)
                transpose_maxima(s)
                for step in PE_ORDER[layer]:
                    what, n = step[0], int(step[1:])
                    if what == "t":
                        shifted_scores(s, p, n)
                    elif what == "a":
                        attend(s, p, n)
                    elif what == "h":
                        half_transpose(s, n, s)
                    elif after:
                        proj_group(s + 1, n)

            pe.wait_ge(constants, 2)
            proj_transpose(0)
            proj_v(0)
            for t in range(TB):
                proj_qk(0, t)
            for i in range(NF):
                proj_group(0, i)
            sequence(0, 0, False, True)
            with pe.Fori(0, (B - 2) // 2) as r:
                for k in range(2):
                    sequence(2 * r + 1 + k, (1 + k) % 2, True, True)
            sequence(B - 1, (B - 1) % 2, True, False)
            half_transpose(B - 1, 1, B)
            out_transpose(B - 1)
            out_project(B - 1, B)

        @block.scalar
        def _(act):
            def y_hi(s):
                act.wait_ge(yT_ps, s + 1)
                wait(act, qk_ps, TB * s)
                nc.scalar.activation(yT_hi[:].rearrange("p c n -> p (c n)"), t_bank("yT")[:],
                                     ACT.Copy).then_inc(yT_hi_done, 1)

            def square(s, t):
                if not multi:
                    return
                act.wait_ge(qk_ps, TB * s + t + 1)
                wait(act, ss_done, TB * s)
                src = t_bank("qk1") if t else ps_p
                nc.scalar.activation(sq[:, t], src[:, 0:QK], ACT.Square).then_inc(sq_done, 1)

            def copy_v(s, p):
                act.wait_ge(v_ps, s + 1)
                nc.scalar.activation(v[p][:, :, :, 0:HD],
                                     ps_p[:, 0:TB * VW].rearrange("p (t h d) -> p t h d", t=TB, d=HD),
                                     ACT.Copy).then_inc(v_done, 1)

            def stack_his(s, t):
                act.wait_ge(rot_done, TB * s + t + 1)
                wait(act, group_ps, NF * s)
                nc.scalar.activation(q_stack(t)[:, :, 0:2], q_part(rotated, t), ACT.Copy)
                nc.scalar.activation(k_stack(t)[:, :, :, 0], k_part(rotated, t),
                                     ACT.Copy).then_inc(stack_hi, 1)

            def copy_queries(s, p, i):
                t, g = divmod(i, NG)
                first, count, _ = groups[g]
                act.wait_ge(group_ps, NF * s + i + 1)
                nc.scalar.activation(qT[p][:, first:first + count, t * P:(t + 1) * P],
                                     t_bank(gs[i])[:, 0:count * P].rearrange("p (k n) -> p k n", n=P),
                                     ACT.Copy).then_inc(t_out[bank[gs[i]]], 1)

            def maxima(s):
                act.wait_ge(maxT_ps, s + 1)
                wait(act, st_ps, PAIRS * s)
                nc.scalar.activation(maxT[0:2 * NH], t_bank("maxT")[0:2 * NH, 0:N],
                                     ACT.Copy).then_inc(t_out[bank["maxT"]], 1)

            def exponentials(s, j):
                act.wait_ge(st_ps, PAIRS * s + j + 1)
                if j >= NPB:
                    act.wait_ge(av_ps, PAIRS * s + j - NPB + 1)
                else:
                    wait(act, av_ps, PAIRS * s)
                nc.scalar.activation(probs[:, j % NPB], ring[:, 2 * (j % 2):2 * (j % 2) + 2, 0:TRI], ACT.Exp,
                                     scale=exp_scale).then_inc(exp_done, 1)

            def outputs(s, half):
                act.wait_ge(av_ps, PAIRS * s + (half + 1) * PAIRS // 2)
                wait(act, half_ps, 2 * s + half - 1)
                nc.scalar.activation(av_sb[half][:].rearrange("p g n -> p (g n)"), ps_av[:],
                                     ACT.Copy).then_inc(av_out, 1)

            def out_hi(s):
                act.wait_ge(oT_ps, s + 1)
                nc.scalar.activation(oT_hi[:].rearrange("p c n -> p (c n)"), t_bank("oT")[:],
                                     ACT.Copy).then_inc(oT_hi_done, 1)

            def sequence(s, p, before, after):
                if before:
                    out_hi(s - 1)
                if after:
                    y_hi(s + 1)
                    copy_v(s + 1, 1 - p)
                    square(s + 1, 0)
                    square(s + 1, 1)
                maxima(s)
                for step in ACT_ORDER[layer]:
                    what, n = step[0], int(step[1:])
                    if what == "e":
                        exponentials(s, n)
                    elif what == "o":
                        outputs(s, n)
                    elif what == "s" and after:
                        stack_his(s + 1, n)
                    elif what == "c" and after:
                        copy_queries(s + 1, 1 - p, n)

            y_hi(0)
            copy_v(0, 0)
            for t in range(TB):
                square(0, t)
            for t in range(TB):
                stack_his(0, t)
            for i in range(NF):
                if not groups[i % NG][2]:
                    copy_queries(0, 0, i)
            sequence(0, 0, False, True)
            with act.Fori(0, (B - 2) // 2) as r:
                for k in range(2):
                    sequence(2 * r + 1 + k, (1 + k) % 2, True, True)
            sequence(B - 1, (B - 1) % 2, True, False)
            out_hi(B - 1)

        @block.vector
        def _(dve):
            def ln_stats(s):
                dve_ln.start(s)
                for t in range(TB):
                    last = nc.vector.bn_stats(stats[:, t], x[:, ds(TB * s + t, 1)].rearrange("p a n -> p (a n)"))
                dve_ln.inc(last)
                dve_ln.wait(dve)
                passed(dve, waited_dve)
                for t in range(TB):
                    last = nc.vector.bn_aggr(mv[:, t], stats[:, t])
                last.then_inc(var_ready, 1)

            def ln_apply(s):
                dve.wait_ge(rstd_ready, s + 1)
                wait(dve, yT_ps, s)
                for t in range(TB):
                    last = nc.vector.tensor_scalar(y[:, t], x[:, ds(TB * s + t, 1)].rearrange("p a n -> p (a n)"),
                                                   mv[:, t, 0:1], rstd[:, t:t + 1], ALU.subtract, ALU.mult)
                last.then_inc(y_ready, 1)

            def y_lo(s):
                dve.wait_ge(yT_hi_done, s + 1)
                wait(dve, qk_ps, TB * s)
                nc.vector.tensor_tensor(yT_lo[:].rearrange("p c n -> p (c n)"), t_bank("yT")[:],
                                        yT_hi[:].rearrange("p c n -> p (c n)").bitcast(F32),
                                        ALU.subtract).then_inc(t_out[bank["yT"]], 1)

            def sum_squares(s, t):
                if not multi:
                    return
                dve.wait_ge(sq_done, TB * s + t + 1)
                nc.vector.tensor_reduce(ss[:, t], sq[:, t].rearrange("p (h d) -> p h d", d=HD), AX_X,
                                        ALU.add).then_inc(ss_done, 1)

            def rms_rstd(s):
                if not multi:
                    return
                dve_rs.start(s)
                v_, g, step = (a[:].rearrange("p t h -> p (t h)") for a in (ss_eps, rs, rs_step))
                dve.wait_ge(ss_done, TB * (s + 1))
                dve_rs.inc(nc.vector.tensor_scalar(v_, ss[:].rearrange("p t h -> p (t h)"), 1.0 / HD, RMS_EPS,
                                                   ALU.mult, ALU.add))
                dve_rs.wait(dve)
                dve_rs.inc(nc.vector.tensor_scalar(g.bitcast(I32), v_.bitcast(I32), -0.5, RSQRT_GUESS,
                                                   ALU.mult, ALU.add))
                for _ in range(NEWTON):
                    dve_rs.wait(dve)
                    dve_rs.inc(nc.vector.scalar_tensor_tensor(step, g, -0.5, g, ALU.mult, ALU.mult))
                    dve_rs.wait(dve)
                    dve_rs.inc(nc.vector.tensor_tensor(step, step, v_, ALU.mult))
                    dve_rs.wait(dve)
                    dve_rs.inc(nc.vector.scalar_tensor_tensor(g, step, 1.5, g, ALU.add, ALU.mult))
                dve_rs.wait(dve)
                dve_rs.end()

            def norm_qk(s, t):
                if not multi:
                    dve.wait_ge(qk_ps, TB * s + t + 1)
                if t == 0:
                    wait(dve, rot_s_done, s)
                src = (t_bank("qk1") if t else ps_p)[:, 0:QK].rearrange("p (h d) -> p h d", d=HD)
                dst = qn[:, t].rearrange("p (h d) -> p h d", d=HD)
                if multi:
                    ins = nc.vector.tensor_tensor(dst, src, rs[:, t].unsqueeze(2).to_broadcast([P, NH + NK, HD]),
                                                  ALU.mult)
                else:
                    ins = nc.vector.tensor_copy(dst, src)
                ins.then_inc(t_out[bank["qk1"]] if t else qn_done, 1)

            def rotate_cos(s, t):
                if t == 0:
                    dve_rot.start(s)
                qn_ready(dve, s, t)
                for (src, which), (dst, _) in zip(rot_parts(qn, t), rot_parts(rot_c, t)):
                    last = nc.vector.tensor_tensor(dst, src, table(tab_c, t, which, src.shape[2]), ALU.mult)
                dve_rot.inc(last)

            def rotate_add(s, t):
                dve_rot.wait(dve)
                if t == 0:
                    dve.wait_ge(rot_s_done, s + 1)
                wait(dve, stack_hi, TB * s)
                nc.vector.tensor_tensor(rotated[:, t], rot_c[:, t], rot_s[:, t], ALU.add).then_inc(rot_done, 1)

            def stack_los(s, t):
                dve.wait_ge(stack_hi, TB * s + t + 1)
                wait(dve, group_ps, NF * s)
                nc.vector.tensor_tensor(q_stack(t)[:, :, 2:4], q_part(rotated, t),
                                        q_stack(t)[:, :, 0:2].bitcast(F32), ALU.subtract)
                nc.vector.tensor_tensor(k_stack(t)[:, :, :, 1], k_part(rotated, t),
                                        k_stack(t)[:, :, :, 0].bitcast(F32), ALU.subtract).then_inc(stack_lo, 1)

            def maxima(s, j):
                dve.wait_ge(s_ps, PAIRS * s + j + 1)
                for c, lo, hi in ((0, 0, P), (1, P, TRI)):
                    last = nc.vector.tensor_reduce(neg_max[:, c, 2 * j:2 * j + 2],
                                                   ring[:, 2 * (j % 2):2 * (j % 2) + 2, lo:hi],
                                                   AX_X, ALU.max, negate=True)
                last.then_inc(max_done, 1)

            def stack_maxima(s):
                dve_max.start(s)
                dve.wait_ge(max_done, PAIRS * (s + 1))
                wait(dve, maxT_ps, s)
                dve_max.inc(nc.vector.tensor_copy(max_stack[:, :, :, 0], neg_max[:]))
                dve_max.wait(dve)
                nc.vector.tensor_tensor(max_stack[:, :, :, 1], neg_max[:], max_stack[:, :, :, 0].bitcast(F32),
                                        ALU.subtract).then_inc(max_stacked, 1)
                dve_max.end()

            def norm_half(s, half):
                dve_norm.start(s)
                dve_norm.n = half
                dve.wait_ge(half_ps, 2 * s + half + 1)
                if half == 0:
                    wait(dve, oT_ps, s)
                hs = slice(half * HALF_HEADS, (half + 1) * HALF_HEADS)
                out = t_bank(f"half{half}")[:].rearrange("p (t h d) -> p t h d", t=TB, d=HV)
                dve_norm.inc(nc.vector.reciprocal(recip[:, half], out[:, :, :, HD]))
                dve_norm.wait(dve)
                nc.vector.tensor_tensor(o[:, :, hs], out[:, :, :, 0:HD],
                                        recip[:, half].unsqueeze(3).to_broadcast([P, TB, HALF_HEADS, HD]),
                                        ALU.mult).then_inc(t_out[bank[f"half{half}"]], 1)

            def out_lo(s):
                dve.wait_ge(oT_hi_done, s + 1)
                nc.vector.tensor_tensor(oT_lo[:].rearrange("p c n -> p (c n)"), t_bank("oT")[:],
                                        oT_hi[:].rearrange("p c n -> p (c n)").bitcast(F32),
                                        ALU.subtract).then_inc(t_out[bank["oT"]], 1)

            def out_add(s):
                dve_bias.start(s)
                tiles = x[:, ds(TB * s, TB)]
                if bias is not None:
                    dve_bias.inc(nc.vector.tensor_tensor(tiles, tiles, bias[:].unsqueeze(1).to_broadcast([P, TB, H]),
                                                         ALU.add))
                    dve_bias.wait(dve)
                dve.wait_ge(out_ps, s + 1)
                nc.vector.tensor_tensor(tiles, ps_p[:].rearrange("p (t n) -> p t n", t=TB), tiles,
                                        ALU.add).then_inc(out_added, 1)

            def copy_keys(s, p, i):
                t, g = divmod(i, NG)
                first, count, _ = groups[g]
                dve.wait_ge(group_ps, NF * s + i + 1)
                src = t_bank(gs[i])[:, 0:count * P].rearrange("p (k n) -> p k n", n=P)
                at, cols = first - PAIRS, slice(t * P, (t + 1) * P)
                nc.vector.tensor_copy(kT[p][0:STK, at:at + count, 0, cols], src[0:STK])
                nc.vector.tensor_copy(kT[p][STK:P, at:at + count, 1, cols],
                                      src[STK:P]).then_inc(t_out[bank[gs[i]]], 1)

            def prepare(s):
                for t in range(TB):
                    sum_squares(s, t)
                rms_rstd(s)
                norm_qk(s, 0)
                norm_qk(s, 1)
                rotate_cos(s, 0)
                dve_rot.inc(rotate_sin(dve, nc.vector, s, 1))
                rotate_add(s, 0)
                rotate_cos(s, 1)
                rotate_add(s, 1)
                dve_rot.end()
                stack_los(s, 0)
                stack_los(s, 1)

            def sequence(s, p, before, after):
                if after:
                    ln_stats(s + 1)
                for j in range(PAIRS):
                    maxima(s, j)
                    if j == 1 and before:
                        norm_half(s - 1, 1)
                    if j == 1 and after:
                        ln_apply(s + 1)
                    if j == 2 and before:
                        out_lo(s - 1)
                    if j == 3 and after:
                        y_lo(s + 1)
                    if j == 4 and before:
                        out_add(s - 1)
                stack_maxima(s)
                if after:
                    prepare(s + 1)
                norm_half(s, 0)
                if after:
                    for i in key_groups:
                        copy_keys(s + 1, 1 - p, i)

            for i in range(2):
                nc.vector.memset(v[i][:, :, :, HD:HV], 0.0)
            nc.vector.memset(zero[:], 0.0).then_inc(constants, 1)
            dve.wait_ge(constants, 1)
            nc.vector.tensor_copy(maxT[:], zero[:].to_broadcast([P, N]))
            for i in range(2):
                for hh, rows in ((0, slice(STK, P)), (1, slice(0, STK))):
                    for c in range(kT[i].shape[1]):
                        nc.vector.tensor_copy(kT[i][rows, c, hh], zero[rows].to_broadcast([STK, N]))
                last = nc.vector.memset(v[i][:, :, :, HD:HD + 1], 1.0)
            last.then_inc(constants, 1)
            ln_stats(0)
            ln_apply(0)
            y_lo(0)
            prepare(0)
            for i in key_groups:
                copy_keys(0, 0, i)
            sequence(0, 0, False, True)
            with dve.Fori(0, (B - 2) // 2) as r:
                for k in range(2):
                    sequence(2 * r + 1 + k, (1 + k) % 2, True, True)
            sequence(B - 1, (B - 1) % 2, True, False)
            norm_half(B - 1, 1)
            out_lo(B - 1)
            out_add(B - 1)
            dve.wait_ge(out_added, B)

        @block.gpsimd
        def _(pool):
            def ln_rstd(s):
                pool_ln.start(s)
                pool.wait_ge(var_ready, s + 1)
                wait(pool, y_ready, s)
                passed(pool, waited_pool)
                pool_ln.inc(nc.gpsimd.tensor_scalar(var_eps[:], mv[:, :, 1], LN_EPS, None, ALU.add))
                pool_ln.wait(pool)
                nc.gpsimd.tensor_tensor(rstd[:], var_eps[:], half_neg[:].to_broadcast([P, TB]),
                                        ALU.pow).then_inc(rstd_ready, 1)

            def rotate_first(s):
                wait(pool, rot_done, TB * s)
                rotate_sin(pool, nc.gpsimd, s, 0).then_inc(rot_s_done, 1)

            def cut(s, j):
                pool.wait_ge(exp_done, PAIRS * s + j + 1)
                passed(pool, waited_pool)
                diagonal = probs[:, j % NPB].rearrange("p h (a k) -> p h a k", k=P)
                for a in (0, 2):
                    last = nc.gpsimd.affine_select(out=diagonal[:, :, a], in_=diagonal[:, :, a],
                                                   compare_op=ALU.is_ge, fill=0.0, base=0,
                                                   pattern=[[0, 2], [1, P]], channel_multiplier=-1)
                last.then_inc(cut_done, 1)

            def sequence(s, p, before, after):
                if after:
                    ln_rstd(s + 1)
                for j in range(PAIRS):
                    cut(s, j)
                    if j == 1 and after:
                        rotate_first(s + 1)

            ln_rstd(0)
            rotate_first(0)
            sequence(0, 0, False, True)
            with pool.Fori(0, (B - 2) // 2) as r:
                for k in range(2):
                    sequence(2 * r + 1 + k, (1 + k) % 2, True, True)
            sequence(B - 1, (B - 1) % 2, True, False)


def route(nc, env, layer, wts, E):
    x, ident, ident_r, half_neg, xT_hi, xT_lo, gatesT = (
        env["x"], env["ident"], env["ident_r"], env["half_neg"], env["xT_hi"], env["xT_lo"], env["gatesT"])
    wr_hi, wr_lo, bias = wts["router_hi"], wts["router_lo"], wts["router_bias"]
    pre = f"r{layer}_"
    with ExitStack() as ctx:
        def sb(name, shape, dt=F32):
            return ctx.enter_context(nc.sbuf_tensor(pre + name, shape, dt))

        stats = sb("stats", [P, TB, 6])
        mv = sb("mv", [P, NT, 2])
        pair_mv = sb("pair_mv", [P, TB, 2])
        var_eps = sb("var_eps", [P, NT])
        rstd = sb("rstd", [P, NT])
        y = sb("y", [P, 2, TB, H])
        yT_hi = sb("yT_hi", [P, 2, FC, N], F32R)
        yT_lo = sb("yT_lo", [P, 2, FC, N], F32R)
        logits = sb("logits", [P, NT, E])
        ps_y = [ctx.enter_context(nc.psum_tensor(pre + f"ps_y{i}", [P, 512], F32)) for i in range(2)]
        ps_l = [ctx.enter_context(nc.psum_tensor(pre + f"ps_l{i}", [P, 512], F32)) for i in range(2)]

        with semaphores(nc) as make_sem, ExitStack() as sems:
            def sem1(name):
                return make_sem(pre + name)

            stats_done = sem1("stats_done")
            waited_dve = sem1("waited_dve")
            pair_done = sem1("pair_done")
            var_ready = sem1("var_ready")
            rstd_ready = sem1("rstd_ready")
            pool_eps = sem1("pool_eps")
            y_ready = sem1("y_ready")
            yT_ps = sem1("yT_ps")
            hi_done = sem1("hi_done")
            lo_done = sem1("lo_done")
            l_ps = sem1("l_ps")
            l_done = sem1("l_done")
            stored = [sem1(f"stored{i}") for i in range(2)]
            block = sems.enter_context(nc.Block())

            @block.vector
            def _(dve):
                with dve.Fori(0, B) as s:
                    dve.wait_ge(var_ready, s)
                    for t in range(TB):
                        last = nc.vector.bn_stats(stats[:, t], x[:, ds(TB * s + t, 1)].rearrange("p a n -> p (a n)"))
                    last.then_inc(stats_done, 1)
                    dve.wait_ge(stats_done, s + 1)
                    passed(dve, waited_dve)
                    for t in range(TB):
                        last = nc.vector.bn_aggr(pair_mv[:, t], stats[:, t])
                    last.then_inc(pair_done, 1)
                    dve.wait_ge(pair_done, s + 1)
                    nc.vector.tensor_copy(mv[:, ds(TB * s, TB)], pair_mv[:]).then_inc(var_ready, 1)
                dve.wait_ge(rstd_ready, 1)
                with dve.Fori(0, B // 2) as r:
                    for p in range(2):
                        s = 2 * r + p
                        dve.wait_ge(yT_ps, 2 * r)
                        for t in range(TB):
                            last = nc.vector.tensor_scalar(
                                y[:, p, t], x[:, ds(TB * s + t, 1)].rearrange("p a n -> p (a n)"),
                                mv[:, ds(TB * s + t, 1), 0], rstd[:, ds(TB * s + t, 1)], ALU.subtract, ALU.mult)
                        last.then_inc(y_ready, 1)
                    for p in range(2):
                        s = 2 * r + p
                        dve.wait_ge(hi_done, s + 1)
                        dve.wait_ge(l_ps, 2 * r)
                        dve.wait_ge(stored[p], 32 * r)
                        nc.vector.tensor_tensor(yT_lo[:, p].rearrange("p c n -> p (c n)"), ps_y[p][:],
                                                yT_hi[:, p].rearrange("p c n -> p (c n)").bitcast(F32),
                                                ALU.subtract).then_inc(lo_done, 1)

            @block.gpsimd
            def _(pool):
                pool.wait_ge(var_ready, B)
                nc.gpsimd.tensor_scalar(var_eps[:], mv[:, :, 1], LN_EPS, None, ALU.add).then_inc(pool_eps, 1)
                pool.wait_ge(pool_eps, 1)
                nc.gpsimd.tensor_tensor(rstd[:], var_eps[:], half_neg[:].to_broadcast([P, NT]),
                                        ALU.pow).then_inc(rstd_ready, 1)

            @block.tensor
            def _(pe):
                with pe.Fori(0, B // 2) as r:
                    for p in range(2):
                        s = 2 * r + p
                        pe.wait_ge(y_ready, s + 1)
                        pe.wait_ge(lo_done, 2 * r)
                        for c in range(FC):
                            for t in range(TB):
                                last = nc.tensor.transpose(ps_y[p][:, c * N + t * P:c * N + (t + 1) * P],
                                                           y[:, p, t, c * P:(c + 1) * P], ident[:])
                        last.then_inc(yT_ps, 1)
                    for p in range(2):
                        s = 2 * r + p
                        pe.wait_ge(lo_done, s + 1)
                        pe.wait_ge(l_done, 2 * r)
                        for t in range(TB):
                            n = 0
                            for c in range(FC):
                                for a, w in split_passes(yT_hi, yT_lo, wr_hi, wr_lo):
                                    last = nc.tensor.matmul(ps_l[p][:, t * E:(t + 1) * E],
                                                            a[:, p, c, t * P:(t + 1) * P], w[:, c, :],
                                                            start=t == 0 and n == 0, stop=n == 3 * FC - 1,
                                                            skip_group_check=True)
                                    n += 1
                        last.then_inc(l_ps, 1)

            @block.scalar
            def _(act):
                with act.Fori(0, B // 2) as r:
                    for p in range(2):
                        s = 2 * r + p
                        act.wait_ge(yT_ps, s + 1)
                        act.wait_ge(l_ps, 2 * r)
                        act.wait_ge(stored[p], 32 * r)
                        nc.scalar.activation(yT_hi[:, p].rearrange("p c n -> p (c n)"), ps_y[p][:],
                                             ACT.Copy).then_inc(hi_done, 1)
                    for p in range(2):
                        s = 2 * r + p
                        act.wait_ge(l_ps, s + 1)
                        nc.scalar.activation(logits[:, ds(TB * s, TB)],
                                             ps_l[p][:, 0:TB * E].rearrange("p (t e) -> p t e", t=TB),
                                             ACT.Copy).then_inc(l_done, 1)

            @block.sync
            def _(sp):
                with sp.Fori(0, B // 2) as r:
                    for p in range(2):
                        s = 2 * r + p
                        sp.wait_ge(lo_done, s + 1)
                        sp.dma_start(xT_hi[:, :, ds(N * s, N)].bitcast(F32), yT_hi[:, p].bitcast(F32)).then_inc(stored[p], 16)
                        sp.dma_start(xT_lo[:, :, ds(N * s, N)].bitcast(F32), yT_lo[:, p].bitcast(F32)).then_inc(stored[p], 16)
                for p in range(2):
                    sp.wait_ge(stored[p], 32 * (B // 2))

        routing = route_top2 if layer == 0 else route_groups
        routing(nc, sb, logits, bias, env, E)


def store_gates(nc, dve, chain, gates, split, E):
    chain.wait(dve)
    chain.inc(nc.vector.tensor_copy(split[:, :, 0, 0:E], gates[:]))
    chain.wait(dve)
    chain.inc(nc.vector.tensor_tensor(split[:, :, 1, 0:E], gates[:], split[:, :, 0, 0:E].bitcast(F32),
                                      ALU.subtract))


def transpose_gates(nc, block, env, split, ps, gates_ready, count, ps_done, copied):
    ident_r, gatesT = env["ident_r"], env["gatesT"]

    @block.tensor
    def _(pe):
        pe.wait_ge(gates_ready, count)
        for g in range(NT // 4):
            if g >= 2:
                pe.wait_ge(copied, g - 1)
            for k in range(4):
                last = nc.tensor.transpose(ps[g % 2][0:64, k * P:(k + 1) * P].bitcast(F32R),
                                           split[:, 4 * g + k].rearrange("p s e -> p (s e)"), ident_r[:])
            last.then_inc(ps_done, 1)

    @block.scalar
    def _(act):
        for g in range(NT // 4):
            act.wait_ge(ps_done, g + 1)
            nc.scalar.activation(gatesT[:, g * 4 * P:(g + 1) * 4 * P], ps[g % 2][0:64, :],
                                 ACT.Copy).then_inc(copied, 1)
        act.wait_ge(copied, NT // 4)


def route_top2(nc, sb, logits, bias, env, E):
    EP = E + 8
    biased = sb("biased", [P, NT, EP])
    replaced = sb("replaced", [P, NT, EP])
    top = sb("top", [P, NT, 8])
    chosen = sb("chosen", [P, NT, E])
    lmax = sb("lmax", [P, NT])
    expo = sb("expo", [P, NT, E])
    total = sb("total", [P, NT])
    gates = sb("gates", [P, NT, E])
    split = sb("split", [P, NT, 2, 32], F32R)
    zero = sb("zero", [P, NT, 2, 32])
    ps = env["ps_gates"]
    with semaphores(nc) as make_sem, ExitStack() as ctx:
        steps = make_sem("r0_steps")
        shifted = make_sem("r0_shifted")
        exp_done = make_sem("r0_exp_done")
        ps_done = make_sem("r0_gates_ps")
        copied = make_sem("r0_gates_copied")
        tensors = [ctx.enter_context(nc.psum_tensor(f"{n}", [P, 512], F32)) for n in ps]
        block = ctx.enter_context(nc.Block())
        count = 16

        def bc(ap):
            return ap.unsqueeze(2).to_broadcast([P, NT, E])

        @block.vector
        def _(dve):
            ch = Chain(steps, count)
            ch.start(0)
            ch.inc(nc.vector.memset(zero[:], 0.0))
            nc.vector.memset(biased[:, :, E:EP], BIG)
            ch.inc(nc.vector.tensor_tensor(biased[:, :, 0:E], logits[:],
                                           bias[:].unsqueeze(1).to_broadcast([P, NT, E]), ALU.add))
            ch.inc(nc.vector.tensor_reduce(lmax[:], logits[:], AX_X, ALU.max))
            ch.wait(dve)
            nc.vector.tensor_copy(split[:], zero[:])
            nc.vector.tensor_tensor(expo[:], logits[:], bc(lmax[:]), ALU.subtract).then_inc(shifted, 1)
            for t in range(NT):
                last = nc.vector.max(top[:, t], biased[:, t, 0:E])
            ch.inc(last)
            ch.wait(dve)
            ch.inc(nc.vector.memset(top[:, :, 2:8], BIG))
            ch.wait(dve)
            for t in range(NT):
                last = nc.vector.match_replace(replaced[:, t], in_to_replace=top[:, t], in_values=biased[:, t],
                                               imm_value=-BIG)
            ch.inc(last)
            ch.wait(dve)
            ch.inc(nc.vector.tensor_tensor(chosen[:], replaced[:, :, 0:E], biased[:, :, 0:E], ALU.not_equal))
            dve.wait_ge(exp_done, 1)
            ch.inc(nc.vector.tensor_reduce(total[:], expo[:], AX_X, ALU.add))
            ch.wait(dve)
            ch.inc(nc.vector.reciprocal(total[:], total[:]))
            ch.wait(dve)
            ch.inc(nc.vector.tensor_tensor(expo[:], expo[:], bc(total[:]), ALU.mult))
            ch.wait(dve)
            ch.inc(nc.vector.tensor_tensor(gates[:], expo[:], chosen[:], ALU.mult))
            ch.wait(dve)
            ch.inc(nc.vector.tensor_reduce(total[:], gates[:], AX_X, ALU.add))
            ch.wait(dve)
            ch.inc(nc.vector.reciprocal(total[:], total[:]))
            ch.wait(dve)
            ch.inc(nc.vector.tensor_tensor(gates[:], gates[:], bc(total[:]), ALU.mult))
            store_gates(nc, dve, ch, gates, split, E)
            assert ch.n == count, ch.n

        @block.scalar
        def _(act):
            act.wait_ge(shifted, 1)
            nc.scalar.activation(expo[:], expo[:], ACT.Exp).then_inc(exp_done, 1)

        transpose_gates(nc, block, env, split, tensors, steps, count, ps_done, copied)


def route_groups(nc, sb, logits, bias, env, E):
    G, TOPG, K, SCALE = 8, 4, 8, 2.5
    EG = E // G
    scores = sb("scores", [P, NT, E])
    biased = sb("biased", [P, NT, E])
    pair_max = sb("pair_max", [P, NT, G, 2])
    pair_min = sb("pair_min", [P, NT, G, 2])
    first = sb("first", [P, NT, G])
    second = sb("second", [P, NT, G])
    second_low = sb("second_low", [P, NT, G])
    group = sb("group", [P, NT, 2 * G])
    group_out = sb("group_out", [P, NT, 2 * G])
    group_on = sb("group_on", [P, NT, G])
    top = sb("top", [P, NT, 8])
    masked = sb("masked", [P, NT, E])
    replaced = sb("replaced", [P, NT, E])
    chosen = sb("chosen", [P, NT, E])
    total = sb("total", [P, NT])
    gates = sb("gates", [P, NT, E])
    split = sb("split", [P, NT, 2, 32], F32R)
    ps = env["ps_gates"]
    with semaphores(nc) as make_sem, ExitStack() as ctx:
        steps = make_sem("r1_steps")
        sig_done = make_sem("r1_sig_done")
        ps_done = make_sem("r1_gates_ps")
        copied = make_sem("r1_gates_copied")
        tensors = [ctx.enter_context(nc.psum_tensor(f"{n}", [P, 512], F32)) for n in ps]
        block = ctx.enter_context(nc.Block())
        count = 21

        @block.vector
        def _(dve):
            ch = Chain(steps, count)
            ch.start(0)

            def step(ins):
                ch.inc(ins)
                ch.wait(dve)

            dve.wait_ge(sig_done, 1)
            nc.vector.memset(group[:, :, G:], BIG)
            step(nc.vector.tensor_tensor(biased[:], scores[:], bias[:].unsqueeze(1).to_broadcast([P, NT, E]),
                                         ALU.add))
            quad = biased[:].rearrange("p t (g a b) -> p (t g) a b", a=2, b=2)
            pmx = pair_max[:].rearrange("p t g a -> p (t g) a")
            pmn = pair_min[:].rearrange("p t g a -> p (t g) a")
            nc.vector.tensor_tensor(pmx, quad[:, :, :, 0], quad[:, :, :, 1], ALU.max)
            step(nc.vector.tensor_tensor(pmn, quad[:, :, :, 0], quad[:, :, :, 1], ALU.min))
            f, s, lo = (a[:].rearrange("p t g -> p (t g)") for a in (first, second, second_low))
            nc.vector.tensor_tensor(f, pmx[:, :, 0], pmx[:, :, 1], ALU.max)
            nc.vector.tensor_tensor(s, pmx[:, :, 0], pmx[:, :, 1], ALU.min)
            step(nc.vector.tensor_tensor(lo, pmn[:, :, 0], pmn[:, :, 1], ALU.max))
            step(nc.vector.tensor_tensor(s, s, lo, ALU.max))
            step(nc.vector.tensor_tensor(group[:, :, 0:G], first[:], second[:], ALU.add))
            for t in range(NT):
                last = nc.vector.max(top[:, t], group[:, t, 0:G])
            step(last)
            step(nc.vector.memset(top[:, :, TOPG:8], BIG))
            for t in range(NT):
                last = nc.vector.match_replace(group_out[:, t], in_to_replace=top[:, t], in_values=group[:, t],
                                               imm_value=-BIG)
            step(last)
            step(nc.vector.tensor_tensor(group_on[:], group_out[:, :, 0:G], group[:, :, 0:G], ALU.not_equal))
            step(nc.vector.tensor_tensor(
                masked[:].rearrange("p t (g e) -> p (t g) e", e=EG),
                biased[:].rearrange("p t (g e) -> p (t g) e", e=EG),
                group_on[:].rearrange("p t g -> p (t g)").unsqueeze(2).to_broadcast([P, NT * G, EG]), ALU.mult))
            step(nc.vector.tensor_scalar(masked[:], masked[:], 0.0, None, ALU.add))
            for t in range(NT):
                last = nc.vector.max(top[:, t], masked[:, t])
            step(last)
            for t in range(NT):
                last = nc.vector.match_replace(replaced[:, t], in_to_replace=top[:, t], in_values=masked[:, t],
                                               imm_value=-BIG)
            step(last)
            step(nc.vector.tensor_tensor(chosen[:], replaced[:], masked[:], ALU.not_equal))
            step(nc.vector.tensor_tensor(gates[:], scores[:], chosen[:], ALU.mult))
            step(nc.vector.tensor_reduce(total[:], gates[:], AX_X, ALU.add))
            step(nc.vector.reciprocal(total[:], total[:]))
            step(nc.vector.tensor_tensor(gates[:], gates[:], total[:].unsqueeze(2).to_broadcast([P, NT, E]),
                                         ALU.mult))
            step(nc.vector.tensor_scalar(gates[:], gates[:], SCALE, None, ALU.mult))
            store_gates(nc, dve, ch, gates, split, E)
            assert ch.n == count, ch.n

        @block.scalar
        def _(act):
            nc.scalar.activation(scores[:], logits[:], ACT.Sigmoid).then_inc(sig_done, 1)

        transpose_gates(nc, block, env, split, tensors, steps, count, ps_done, copied)


def experts(nc, env, layer, w_all, E, out=None):
    x, xT_hi, xT_lo, gatesT, sel_exp = env["x"], env["xT_hi"], env["xT_lo"], env["gatesT"], env["sel_exp"]
    NE = E + 2
    ITEMS = 2 * NE
    SHARED = 4
    pre = f"e{layer}_"
    with semaphores(nc) as make_sem, ExitStack() as ctx:
        def sb(name, shape, dt=F32):
            return ctx.enter_context(nc.sbuf_tensor(pre + name, shape, dt))

        def sem(name):
            return make_sem(pre + name)

        raw = [sb(f"raw{i}", [P, WCOLS]) for i in range(2)]
        w_hi = [sb(f"w_hi{i}", [P, WCOLS], F32R) for i in range(2)]
        w_lo = [sb(f"w_lo{i}", [P, WCOLS], F32R) for i in range(2)]
        sel = [sb(f"sel{i}", [64, P], F32R) for i in range(2)]
        act_out = [sb(f"act_out{i}", [P, BLK]) for i in range(2)]
        prod = sb("prod", [P, BLK])
        hid = [sb(f"hid{i}", [P, BLK]) for i in range(2)]
        hid_hi = [sb(f"hid_hi{i}", [P, BLK], F32R) for i in range(2)]
        hid_lo = [sb(f"hid_lo{i}", [P, BLK], F32R) for i in range(2)]
        acc = ctx.enter_context(nc.psum_tensor(pre + "acc", [P, HALF // P, H], F32))
        ps_a = ctx.enter_context(nc.psum_tensor(pre + "ps_a", [P, BLK], F32))
        ps_b = ctx.enter_context(nc.psum_tensor(pre + "ps_b", [P, BLK], F32))
        ps_g = ctx.enter_context(nc.psum_tensor(pre + "ps_g", [P, BLK], F32))

        w_loaded = [sem(f"w_loaded{i}") for i in range(2)]
        w_hi_done = sem("w_hi_done")
        w_lo_done = sem("w_lo_done")
        a_ps = sem("a_ps")
        b_ps = sem("b_ps")
        act_done = sem("act_done")
        prod_done = sem("prod_done")
        hid_done = sem("hid_done")
        hi_done = sem("hi_done")
        lo_done = sem("lo_done")
        down_ps = sem("down_ps")
        added = sem("added")
        stored = sem("stored")
        block = ctx.enter_context(nc.Block())

        A, Bc, D = 0, FC * P, 2 * FC * P

        def item_of(hf, n, blk):
            return hf * ITEMS + 2 * n + blk

        def expert_of(hf, n):
            return hf * NE + n

        @block.sync
        def _(sp):
            def load(k, n):
                sp.dma_start(raw[k][:], w_all[ds(n, 1)].rearrange("e p n -> p (e n)")).then_inc(w_loaded[k], 16)

            with sp.Fori(0, HALVES) as hf:
                with sp.Fori(0, NE // 2) as r:
                    for k in range(2):
                        sp.wait_ge(w_lo_done, expert_of(hf, 2 * r))
                        load(k, 2 * r + k)
            sp.wait_ge(w_lo_done, HALVES * NE)
            load(0, 0)

        @block.gpsimd
        def _(pool):
            def split_lo(k, m, gated=None):
                pool.wait_ge(w_hi_done, m + 1)
                wait(pool, down_ps, 2 * m - 2)
                if gated is not None:
                    nc.gpsimd.tensor_copy(sel[k][:], sel_exp[:, ds(gated, 1)].rearrange("p e n -> p (e n)"))
                nc.gpsimd.tensor_tensor(w_lo[k][:], raw[k][:], w_hi[k][:].bitcast(F32),
                                        ALU.subtract).then_inc(w_lo_done, 1)

            split_lo(0, 0)
            with pool.Fori(0, HALVES) as hf:
                split_lo(1, expert_of(hf, 1))
                with pool.Fori(1, NE // 2) as r:
                    for k in range(2):
                        split_lo(k, expert_of(hf, 2 * r + k), 2 * r + k - 2)
                split_lo(0, expert_of(hf, NE))
                if out is not None:
                    pool.wait_ge(added, hf + 1)
                    rows = ds(hf * (HALF // P), HALF // P)
                    pool.dma_start(out.rearrange("b (t p) n -> p (b t) n", p=P)[:, rows],
                                   x[:, rows]).then_inc(stored, 16)
            pool.wait_ge(w_lo_done, HALVES * NE + 1)
            if out is not None:
                pool.wait_ge(stored, 16 * HALVES)

        @block.scalar
        def _(act):
            def split_hi(k, m, turn):
                act.wait_ge(w_loaded[k], 16 * (turn + 1))
                wait(act, down_ps, 2 * m - 2)
                nc.scalar.activation(w_hi[k][:], raw[k][:], ACT.Copy).then_inc(w_hi_done, 1)

            def silu(hf, n, blk):
                i = item_of(hf, n, blk)
                act.wait_ge(a_ps, i + 1)
                act.wait_ge(hid_done, item_of(hf, n, 0))
                nc.scalar.activation(act_out[blk][:], ps_a[:], ACT.Silu).then_inc(act_done, 1)

            def hidden_hi(hf, n, blk):
                i = item_of(hf, n, blk)
                act.wait_ge(hid_done, i + 1)
                act.wait_ge(down_ps, item_of(hf, n, 0))
                nc.scalar.activation(hid_hi[blk][:], hid[blk][:], ACT.Copy).then_inc(hi_done, 1)

            split_hi(0, 0, 0)
            with act.Fori(0, HALVES) as hf:
                for k in range(2):
                    silu(hf, k, 0)
                    hidden_hi(hf, k, 0)
                    split_hi(1 - k, expert_of(hf, k + 1), hf * (NE // 2) + k)
                    silu(hf, k, 1)
                    hidden_hi(hf, k, 1)
                with act.Fori(1, NE // 2) as r:
                    for k in range(2):
                        n = 2 * r + k
                        silu(hf, n, 0)
                        hidden_hi(hf, n, 0)
                        split_hi(1 - k, expert_of(hf, n + 1), hf * (NE // 2) + r + k)
                        silu(hf, n, 1)
                        hidden_hi(hf, n, 1)

        @block.vector
        def _(dve):
            def hidden(hf, n, blk, gated=None):
                i = item_of(hf, n, blk)
                dve.wait_ge(act_done, i + 1)
                dve.wait_ge(b_ps, i + 1)
                dve.wait_ge(lo_done, item_of(hf, n, 0))
                if gated is None:
                    nc.vector.tensor_tensor(hid[blk][:], ps_b[:], act_out[blk][:], ALU.mult).then_inc(hid_done, 1)
                else:
                    dve.wait_ge(hid_done, i)
                    nc.vector.tensor_tensor(prod[:], ps_b[:], act_out[blk][:], ALU.mult).then_inc(prod_done, 1)
                    dve.wait_ge(prod_done, hf * (ITEMS - SHARED) + 2 * gated + blk + 1)
                    nc.vector.tensor_tensor(hid[blk][:], ps_g[:], prod[:], ALU.mult).then_inc(hid_done, 1)
                dve.wait_ge(hi_done, i + 1)
                nc.vector.tensor_tensor(hid_lo[blk][:], hid[blk][:], hid_hi[blk][:].bitcast(F32),
                                        ALU.subtract).then_inc(lo_done, 1)

            with dve.Fori(0, HALVES) as hf:
                for k in range(2):
                    for blk in range(2):
                        hidden(hf, k, blk)
                with dve.Fori(0, E // 2) as r:
                    for k in range(2):
                        for blk in range(2):
                            hidden(hf, 2 * r + k + 2, blk, 2 * r + k)
                dve.wait_ge(down_ps, (hf + 1) * ITEMS)
                for q in range(HALF // P // 2):
                    tiles = x[:, ds(hf * (HALF // P) + 2 * q, 2)]
                    last = nc.vector.tensor_tensor(tiles, acc[:, 2 * q:2 * q + 2], tiles, ALU.add)
                last.then_inc(added, 1)
            dve.wait_ge(added, HALVES)

        @block.tensor
        def _(pe):
            def up(hf, n, k, blk, shared):
                i = item_of(hf, n, blk)
                tokens = ds(hf * HALF + blk * BLK, BLK)
                if blk == 0:
                    pe.wait_ge(w_lo_done, hf * NE + n + 1)
                pe.wait_ge(act_done, i)
                for col, ps in ((A, ps_a), (Bc, ps_b)):
                    if col == Bc:
                        pe.wait_ge(hid_done, i)
                    m = 0
                    for c in range(FC):
                        for w, a in split_passes(w_hi[k], w_lo[k], xT_hi, xT_lo):
                            last = nc.tensor.matmul(ps[:], w[:, col + c * P:col + (c + 1) * P], a[:, c, tokens],
                                                    start=m == 0, stop=m == 3 * FC - 1)
                            m += 1
                    if col == A:
                        last.then_inc(a_ps, 1)
                if not shared:
                    last = nc.tensor.matmul(ps_g[:], sel[k][:], gatesT[:, tokens], start=True, stop=True)
                last.then_inc(b_ps, 1)

            def down(hf, i, k, blk, first=False):
                pe.wait_ge(lo_done, i + 1)
                if first:
                    pe.wait_ge(added, hf)
                for q in range(BLK // P):
                    at = blk * (BLK // P) + q
                    m = 0
                    for a, w in split_passes(hid_hi[blk], hid_lo[blk], w_hi[k], w_lo[k]):
                        last = nc.tensor.matmul(acc[:, at], a[:, q * P:(q + 1) * P], w[:, D:D + H],
                                                start=first and m == 0 and q % 2 == 0, stop=False,
                                                skip_group_check=True)
                        m += 1
                last.then_inc(down_ps, 1)

            with pe.Fori(0, HALVES) as hf:
                for k in range(2):
                    for blk in range(2):
                        up(hf, k, k, blk, True)
                        if (k, blk) != (0, 0):
                            n, pb = divmod(2 * k + blk - 1, 2)
                            down(hf, item_of(hf, n, pb), n, pb, first=n == 0)
                with pe.Fori(1, NE // 2) as r:
                    for k in range(2):
                        for blk in range(2):
                            up(hf, 2 * r + k, k, blk, False)
                            down(hf, item_of(hf, 2 * r + k, blk) - 1, k if blk else 1 - k, 1 - blk)
                down(hf, item_of(hf, NE - 1, 1), 1, 1)


def layers(nc, a, out):
    with ExitStack() as ctx:
        def sb(name, shape, dt=F32):
            return ctx.enter_context(nc.sbuf_tensor(name, shape, dt))

        env = {
            "x": sb("x", [P, NT, H]), "ident": sb("ident", [P, P]), "ident_r": sb("ident_r", [P, P], F32R),
            "mask_r": sb("mask_r", [P, P], F32R), "sel_head": sb("sel_head", [P, NH, P], F32R),
            "sel_exp": sb("sel_exp", [64, 32, P], F32R), "half_neg": sb("half_neg", [P, 1]),
            "ps_gates": ["ps_gates0", "ps_gates1"],
        }
        setup(nc, env, a["x"])
        for layer in range(2):
            qkv = 3 * H if layer == 0 else H + 2 * HD
            with ExitStack() as part:
                def psb(name, shape, dt=F32):
                    return part.enter_context(nc.sbuf_tensor(f"w{layer}_{name}", shape, dt))

                wts = {"qkv_hi": psb("qkv_hi", [P, FC, qkv], F32R), "qkv_lo": psb("qkv_lo", [P, FC, qkv], F32R),
                       "out_hi": psb("out_hi", [P, FC, H], F32R), "out_lo": psb("out_lo", [P, FC, H], F32R),
                       "tab_c": psb("tab_c", [P, TB, 2, HD]), "tab_s": psb("tab_s", [P, TB, 2, HD])}
                load_split(nc, [
                    (a[f"qkv{layer}"].rearrange("(c p) n -> p c n", p=P), [P, FC, qkv], wts["qkv_hi"], wts["qkv_lo"]),
                    (a[f"out{layer}"].rearrange("(c p) n -> p c n", p=P), [P, FC, H], wts["out_hi"], wts["out_lo"])],
                    f"l{layer}a")
                if layer == 0:
                    rope_tables(nc, a["rope_cos"], a["rope_sin"], a["q_gamma"], a["k_gamma"],
                                wts["tab_c"], wts["tab_s"])
                else:
                    wts["bias"] = psb("bias", [P, H])
                    load_tables(nc, [
                        (wts["tab_c"][:], a["xpos_cos"].rearrange("(t p) k d -> p t k d", p=P)),
                        (wts["tab_s"][:], a["xpos_sin"].rearrange("(t p) k d -> p t k d", p=P)),
                        (wts["bias"][:], a["b_proj"].partition_broadcast(P))], f"l{layer}a")
                attention(nc, env, layer, wts)
            E = 16 if layer == 0 else 32
            with ExitStack() as part:
                def psb(name, shape, dt=F32):
                    return part.enter_context(nc.sbuf_tensor(f"m{layer}_{name}", shape, dt))

                env["xT_hi"], env["xT_lo"] = psb("xT_hi", [P, FC, T], F32R), psb("xT_lo", [P, FC, T], F32R)
                env["gatesT"] = psb("gatesT", [64, T], F32R)
                env["ps_gates"] = [f"ps_gates{layer}{i}" for i in range(2)]
                wts = {"router_hi": psb("router_hi", [P, FC, E], F32R), "router_lo": psb("router_lo", [P, FC, E], F32R),
                       "router_bias": psb("router_bias", [P, E])}
                load_split(nc, [(a[f"router{layer}"].rearrange("(c p) n -> p c n", p=P), [P, FC, E],
                                 wts["router_hi"], wts["router_lo"])], f"l{layer}r")
                load_tables(nc, [(wts["router_bias"][:], a[f"router_bias{layer}"].partition_broadcast(P))],
                            f"l{layer}r")
                route(nc, env, layer, wts, E)
                experts(nc, env, layer, a[f"experts{layer}"], E, out if layer == 1 else None)


def position_tables():
    import numpy as np
    f = np.float32
    inv = (f(1.0) / f(10000.0) ** (np.arange(0, HD, 2, dtype=f) / f(HD))).astype(f)
    pos = np.arange(N, dtype=f)
    ang = (pos[:, None] * inv[None, :]).astype(f)
    ang = np.concatenate([ang, ang], -1)
    sign = np.concatenate([-np.ones(HD // 2, f), np.ones(HD // 2, f)])
    cos, sin = np.cos(ang).astype(f), (np.sin(ang) * sign).astype(f)
    base = ((np.arange(0, HD, 2, dtype=f) + f(0.4 * HD)) / f(1.4 * HD)).astype(f)
    power = ((pos - N // 2) / f(64)).astype(f)
    scale = (base[None, :] ** power[:, None]).astype(f)
    scale = np.concatenate([scale, scale], -1)
    both = np.stack([scale, (f(1.0) / scale).astype(f)], 1) * f(HD ** -0.5)
    return {"rope_cos": cos, "rope_sin": sin, "xpos_cos": (cos[:, None] * both).astype(f),
            "xpos_sin": (sin[:, None] * both).astype(f)}


def expert_layout(first, second, down, s_first, s_second, s_down):
    import numpy as np

    def pack(f, s, d):
        e = f.shape[0]
        def cut(w):
            return w.reshape(e, FC, P, P).transpose(0, 2, 1, 3).reshape(e, P, FC * P)
        return np.concatenate([cut(f), cut(s), d], -1)

    def halves(w):
        return np.stack([w[:, :P], w[:, P:]])

    shared = pack(halves(s_first), halves(s_second), s_down.reshape(2, P, H))
    return np.ascontiguousarray(np.concatenate([shared, pack(first, second, down)], 0))


def kernel(L0_attn_x, L0_attn_w_qkv, L0_attn_w_out, L0_attn_q_gamma, L0_attn_k_gamma, L0_ffn_router_w,
           L0_ffn_router_bias, L0_ffn_Wu, L0_ffn_Wg, L0_ffn_Wd, L0_ffn_Su, L0_ffn_Sg, L0_ffn_Sd, L1_attn_w_q,
           L1_attn_w_kv, L1_attn_w_proj, L1_attn_b_proj, L1_ffn_router_w, L1_ffn_router_bias, L1_ffn_w_gate,
           L1_ffn_w_up, L1_ffn_w_down, L1_ffn_sw_gate, L1_ffn_sw_up, L1_ffn_sw_down):
    import numpy as np
    import concourse.bacc as bacc
    from concourse import mybir as mb
    from concourse.bass_utils import run_bass_kernel_spmd

    g = np.asarray
    arrays = {
        "x": g(L0_attn_x), "qkv0": g(L0_attn_w_qkv), "out0": g(L0_attn_w_out),
        "q_gamma": g(L0_attn_q_gamma), "k_gamma": g(L0_attn_k_gamma),
        "router0": g(L0_ffn_router_w).T, "router_bias0": g(L0_ffn_router_bias),
        "experts0": expert_layout(g(L0_ffn_Wu), g(L0_ffn_Wg), g(L0_ffn_Wd), g(L0_ffn_Su)[0], g(L0_ffn_Sg)[0],
                                  g(L0_ffn_Sd)[0]),
        "qkv1": np.concatenate([g(L1_attn_w_q), g(L1_attn_w_kv)], 0).T, "out1": g(L1_attn_w_proj).T,
        "b_proj": g(L1_attn_b_proj), "router1": g(L1_ffn_router_w), "router_bias1": g(L1_ffn_router_bias),
        "experts1": expert_layout(g(L1_ffn_w_gate), g(L1_ffn_w_up), g(L1_ffn_w_down), g(L1_ffn_sw_gate),
                                  g(L1_ffn_sw_up), g(L1_ffn_sw_down)),
    }
    arrays.update(position_tables())
    arrays = {k: np.ascontiguousarray(v) for k, v in arrays.items()}
    nc = bacc.Bacc("TRN2", target_bir_lowering=False, num_devices=1)
    a = {k: nc.dram_tensor("in_" + k, v.shape, mb.dt.from_np(v.dtype), kind="ExternalInput").ap()
         for k, v in arrays.items()}
    out = nc.dram_tensor("out_0", (B, N, H), mb.dt.float32, kind="ExternalOutput").ap()
    layers(nc, a, out)
    r = run_bass_kernel_spmd(nc, [{"in_" + k: v for k, v in arrays.items()}], core_ids=[0])
    return r.results[0]["out_0"]
```

```python
from contextlib import ExitStack, contextmanager

import concourse.bass as bass
from concourse import mybir

F32 = mybir.dt.float32
F32R = mybir.dt.float32r
I32 = mybir.dt.int32
ALU = mybir.AluOpType
ACT = mybir.ActivationFunctionType
AX_X = mybir.AxisListType.X

P = 128
H = 256
FC = H // P
B, N = 8, 256
T = B * N
NT = T // P
TB = N // P
NH, HD = 16, 16
PAIRS = NH // 2
STK = 4 * HD
TRI = N + P
HV = 32
HALF_HEADS = NH // 2
NEG = -1e30
LN_EPS = 1e-5
RMS_EPS = 1e-6
RSQRT_GUESS = float(0x5F3759DF)
NEWTON = 3
BLK = 512
NBLK = T // BLK
TPB = BLK // P
WCOLS = 2 * FC * P + H
BIG = 3.0e38
GATE_STEPS = (3, 7)
NPB = 3
PE_ORDER = ("t0 t1 t2 a0 t3 a1 t4 a2 t5 a3 t6 a4 h0 t7 a5 g0 g1 a6 g2 g3 a7 g4 g5 g6 g7".split(),
            "t0 t1 t2 a0 t3 a1 t4 g0 a2 t5 g1 a3 t6 g2 a4 h0 t7 a5 g3 a6 g4 a7 g5".split())
ACT_ORDER = ("e0 e1 e2 e3 e4 e5 o0 s0 e6 s1 c0 e7 c1 c3 c5 c7 o1".split(),
             "e0 e1 e2 s0 e3 s1 e4 c0 e5 c1 o0 e6 e7 c3 c4 o1".split())
DVE_ORDER = ("l0 n0 l1 c2 c4 c6".split(), "l0 l1 c2 n0 c5".split())


def ds(start, size):
    return bass.DynSlice(start, size)


class Chain:

    def __init__(self, sem, per_round):
        self.sem, self.per_round = sem, per_round
        self.base = self.n = 0

    def start(self, r):
        self.base, self.n = r * self.per_round, 0

    def inc(self, ins):
        ins.then_inc(self.sem, 1)
        self.n += 1

    def wait(self, eng):
        eng.wait_ge(self.sem, self.base + self.n)

    def end(self):
        assert self.n == self.per_round, (self.n, self.per_round)


def wait(eng, sem, value):
    if isinstance(value, int) and value <= 0:
        return
    eng.wait_ge(sem, value)


@contextmanager
def semaphores(nc):
    used = []

    def make(name):
        used.append(nc.alloc_semaphore(name=name))
        return used[-1]

    yield make
    nc.clear_and_free_semaphores(used)
    nc.all_engine_barrier()


def passed(eng, sem):
    eng.sem_inc(sem, 1)


def split_passes(hi_a, lo_a, hi_b, lo_b):
    return ((hi_a, hi_b), (hi_a, lo_b), (lo_a, hi_b))


def prepare(nc, env, plain, weights, rope):
    ident, ident_r, mask_r, sel_head, half_neg = (
        env["ident"], env["ident_r"], env["mask_r"], env["sel_head"], env["half_neg"])
    rope_c, rope_s, gam_q, gam_k, tab_c, tab_s = rope
    half = HD // 2
    with semaphores(nc) as make_sem, ExitStack() as ctx:
        mask = ctx.enter_context(nc.sbuf_tensor("setup_mask", [P, P], F32))
        head = ctx.enter_context(nc.sbuf_tensor("setup_head", [P, NH], F32))
        cs = ctx.enter_context(nc.sbuf_tensor("rope_cs", [P, 2, TB, HD], F32))
        gam = ctx.enter_context(nc.sbuf_tensor("rope_gamma", [P, 2, HD], F32))
        raws = [ctx.enter_context(nc.sbuf_tensor(f"raw{i}", w[1], F32)) for i, w in enumerate(weights)]
        loaded = [make_sem(f"weights_loaded{i}") for i in range(len(weights))]
        plain_loaded = make_sem("plain_loaded")
        rope_loaded = make_sem("rope_loaded")
        hi_done = make_sem("weights_hi_done")
        lo_done = make_sem("weights_lo_done")
        made = make_sem("made")
        rounded = make_sem("rounded")
        tables_done = make_sem("tables_done")
        block = ctx.enter_context(nc.Block())

        @block.sync
        def _(sp):
            for dst, src in plain:
                sp.dma_start(dst, src).then_inc(plain_loaded, 16)
            sp.wait_ge(plain_loaded, 16 * len(plain))

        @block.gpsimd
        def _(pool):
            nc.gpsimd.memset(half_neg[:], -0.5)
            nc.gpsimd.memset(ident[:], 0.0)
            nc.gpsimd.memset(mask[:], 0.0)
            nc.gpsimd.memset(head[:], 1.0).then_inc(made, 1)
            pool.wait_ge(made, 1)
            nc.gpsimd.affine_select(out=ident[:], in_=ident[:], compare_op=ALU.not_equal, fill=1.0, base=0,
                                    pattern=[[-1, P]], channel_multiplier=1)
            nc.gpsimd.affine_select(out=mask[:], in_=mask[:], compare_op=ALU.is_ge, fill=NEG, base=0,
                                    pattern=[[-1, P]], channel_multiplier=1)
            nc.gpsimd.affine_select(out=head[:], in_=head[:], compare_op=ALU.is_ge, fill=0.0, base=0,
                                    pattern=[[-2, NH]], channel_multiplier=1).then_inc(made, 1)
            pool.wait_ge(made, 2)
            nc.gpsimd.affine_select(out=head[:], in_=head[:], compare_op=ALU.is_ge, fill=0.0, base=1,
                                    pattern=[[2, NH]], channel_multiplier=-1).then_inc(made, 1)

        @block.scalar
        def _(act):
            for (dram, *_), raw, sem in zip(weights, raws, loaded):
                act.dma_start(raw[:], dram).then_inc(sem, 16)
            act.dma_start(cs[:, 0], rope_c.rearrange("(t p) d -> p t d", p=P)).then_inc(rope_loaded, 16)
            act.dma_start(cs[:, 1], rope_s.rearrange("(t p) d -> p t d", p=P)).then_inc(rope_loaded, 16)
            act.dma_start(gam[:, 0], gam_q.partition_broadcast(P)).then_inc(rope_loaded, 16)
            act.dma_start(gam[:, 1], gam_k.partition_broadcast(P)).then_inc(rope_loaded, 16)
            for (_, _, hi, _), raw, sem in zip(weights, raws, loaded):
                act.wait_ge(sem, 16)
                nc.scalar.activation(hi[:], raw[:], ACT.Copy).then_inc(hi_done, 1)

        @block.vector
        def _(dve):
            dve.wait_ge(made, 3)
            nc.vector.tensor_copy(ident_r[:], ident[:])
            nc.vector.tensor_copy(mask_r[:], mask[:])
            nc.vector.tensor_copy(sel_head[:], head[:].unsqueeze(2).to_broadcast([P, NH, P])).then_inc(rounded, 1)
            for i, ((_, _, hi, lo), raw, sem) in enumerate(zip(weights, raws, loaded)):
                dve.wait_ge(sem, 16)
                dve.wait_ge(hi_done, i + 1)
                nc.vector.tensor_tensor(lo[:], raw[:], hi[:].bitcast(F32), ALU.subtract).then_inc(lo_done, 1)
            dve.wait_ge(rope_loaded, 64)
            for t in range(TB):
                nc.vector.tensor_tensor(tab_c[:, t], gam[:], cs[:, 0, t].unsqueeze(1).to_broadcast([P, 2, HD]),
                                        ALU.mult)
                for a, b in ((0, half), (half, 0)):
                    last = nc.vector.tensor_tensor(
                        tab_s[:, t, :, a:a + half], gam[:, :, b:b + half],
                        cs[:, 1, t, a:a + half].unsqueeze(1).to_broadcast([P, 2, half]), ALU.mult)
            last.then_inc(tables_done, 1)
            dve.wait_ge(tables_done, 1)
            dve.wait_ge(lo_done, len(weights))
            dve.wait_ge(rounded, 1)


def attention(nc, env, layer, wts):
    x, ident, ident_r, mask_r, sel_head, half_neg = (
        env["x"], env["ident"], env["ident_r"], env["mask_r"], env["sel_head"], env["half_neg"])
    wqkv_hi, wqkv_lo, wout_hi, wout_lo, tab_c, tab_s = (
        wts["qkv_hi"], wts["qkv_lo"], wts["out_hi"], wts["out_lo"], wts["tab_c"], wts["tab_s"])
    bias = wts.get("bias")
    multi = layer == 0
    NK = NH if multi else 1
    QK = (NH + NK) * HD
    VW = NK * HD
    groups = [(0, 4, False), (4, 4, False)] + ([(8, 4, True), (12, 4, True)] if multi else [(8, 1, True)])
    NG = len(groups)
    NF = TB * NG
    gs = [f"group{i}" for i in range(NF)]
    turns = ["half1", "oT", "yT", "maxT", "qk1"] + [
        "half0" if step[0] == "h" else gs[int(step[1:])] for step in PE_ORDER[layer] if step[0] in "gh"]
    bank = {name: i % 2 for i, name in enumerate(turns)}
    start_turns = ["yT", "qk1"] + gs
    first_turns = turns[2:]
    last_turns = ["half1", "oT", "maxT", "half0"]
    vector_groups = [int(step[1:]) for step in DVE_ORDER[layer] if step[0] == "c"]

    def uses(names, b):
        return sum(bank[n] == b for n in names)

    def turn(s, name):
        b = bank[name]
        names, before = turns, uses(start_turns, b) + uses(first_turns, b) + uses(turns, b) * (s - 1)
        if isinstance(s, int) and s == -1:
            names, before = start_turns, 0
        elif isinstance(s, int) and s == 0:
            names, before = first_turns, uses(start_turns, b)
        elif isinstance(s, int) and s == B - 1:
            names = last_turns
        elif isinstance(s, int) and s == B:
            before += uses(last_turns, b) - uses(turns, b)
        return before + uses(names[:names.index(name)], b)

    exp_scale = HD ** -0.5 if multi else 1.0
    pre = f"a{layer}_"

    with semaphores(nc) as make_sem, ExitStack() as ctx:
        def sb(name, shape, dt=F32):
            return ctx.enter_context(nc.sbuf_tensor(pre + name, shape, dt))

        def pb(name, shape):
            return ctx.enter_context(nc.psum_tensor(pre + name, shape, F32))

        def sem(name):
            return make_sem(pre + name)

        stats = sb("stats", [P, TB, 6])
        mv = sb("mv", [P, TB, 2])
        var_eps = sb("var_eps", [P, TB])
        rstd = sb("rstd", [P, TB])
        y = sb("y", [P, TB, H])
        yT_hi = sb("yT_hi", [P, FC, N], F32R)
        yT_lo = sb("yT_lo", [P, FC, N], F32R)
        sq = sb("sq", [P, TB, QK])
        ss = sb("ss", [P, TB, NH + NK])
        ss_eps = sb("ss_eps", [P, TB, NH + NK])
        rs = sb("rs", [P, TB, NH + NK])
        rs_step = sb("rs_step", [P, TB, NH + NK])
        qn = sb("qn", [P, TB, QK])
        rot_c = sb("rot_c", [P, TB, QK])
        rot_s = sb("rot_s", [P, TB, QK])
        rotated = sb("rotated", [P, TB, QK])
        pieces = NH // 2 + (NK // 2 if multi else 1)
        stack = sb("stack", [P, TB, pieces * P], F32R)
        qT = [sb(f"qT{i}", [P, PAIRS, N], F32R) for i in range(2)]
        kT = [sb(f"kT{i}", [P, PAIRS if multi else 1, 2, N], F32R) for i in range(2)]
        zero = sb("zero", [P, 1])
        v = [sb(f"v{i}", [P, TB, NK, HV]) for i in range(2)]
        block_max = sb("block_max", [P, NH, 3])
        neg_max = sb("neg_max", [P, TB, NH])
        max_stack = sb("max_stack", [P, TB, NH, 2], F32R)
        maxT = sb("maxT", [P, N], F32R)
        probs = sb("probs", [P, NPB, 2, TRI])
        av_sb = [sb(f"av_sb{i}", [P, 2, N]) for i in range(2)]
        recip = sb("recip", [P, 2, TB, HALF_HEADS])
        o = sb("o", [P, TB, NH, HD])
        oT_hi = sb("oT_hi", [P, FC, N], F32R)
        oT_lo = sb("oT_lo", [P, FC, N], F32R)

        ring = pb("ring", [P, 4, 512])
        ps_av = pb("ps_av", [P, 512])
        ps_t = [pb(f"ps_t{i}", [P, 512]) for i in range(2)]
        ps_p = pb("ps_p", [P, 512])

        t_out = [sem(f"t_out{i}") for i in range(2)]
        y_ready = sem("y_ready")
        yT_ps = sem("yT_ps")
        yT_hi_done = sem("yT_hi_done")
        qk_ps = sem("qk_ps")
        v_ps = sem("v_ps")
        v_done = sem("v_done")
        var_ready = sem("var_ready")
        rstd_ready = sem("rstd_ready")
        sq_done = sem("sq_done")
        ss_done = sem("ss_done")
        qn_done = sem("qn_done")
        rot_done = sem("rot_done")
        stack_hi = sem("stack_hi")
        stack_lo = sem("stack_lo")
        group_ps = sem("group_ps")
        s_ps = sem("s_ps")
        max_done = sem("max_done")
        max_stacked = sem("max_stacked")
        maxT_ps = sem("maxT_ps")
        st_ps = sem("st_ps")
        exp_done = sem("exp_done")
        cut_done = sem("cut_done")
        av_ps = sem("av_ps")
        av_out = sem("av_out")
        half_ps = sem("half_ps")
        oT_ps = sem("oT_ps")
        oT_hi_done = sem("oT_hi_done")
        out_ps = sem("out_ps")
        out_added = sem("out_added")
        bias_added = sem("bias_added")
        constants = sem("constants")
        waited_dve = sem("waited_dve")
        waited_pool = sem("waited_pool")
        dve_ln = Chain(sem("dve_ln"), 1)
        dve_rs = Chain(sem("dve_rs"), 2 + 3 * NEWTON)
        pool_ln = Chain(sem("pool_ln"), 2)
        dve_max = Chain(sem("dve_max"), 2)
        dve_norm = Chain(sem("dve_norm"), 2)
        dve_rot = Chain(sem("dve_rot"), 2 * TB)
        block = ctx.enter_context(nc.Block())

        def turn_free(eng, s, name):
            wait(eng, t_out[bank[name]], turn(s, name))

        def turn_done(eng, s, name):
            eng.wait_ge(t_out[bank[name]], turn(s, name) + 1)

        def t_bank(name):
            return ps_t[bank[name]]

        def groups_done(eng, s):
            turn_done(eng, s - 1, gs[-1])
            turn_done(eng, s - 1, gs[-2])

        def head_view(ap, t):
            return ap[:, t, :].rearrange("p (k h d) -> p k h d", k=2, d=HD)

        def rot_parts(ap, t):
            if multi:
                return [(head_view(ap, t), slice(0, 2))]
            q = ap[:, t, 0:NH * HD].rearrange("p (k h d) -> p k h d", k=1, d=HD)
            k = ap[:, t, NH * HD:QK].rearrange("p (k h d) -> p k h d", k=1, d=HD)
            return [(q, slice(0, 1)), (k, slice(1, 2))]

        def table(tab, t, which, heads, lo=0, hi=HD):
            k = which.stop - which.start
            return tab[:, t, which, lo:hi].unsqueeze(2).to_broadcast([P, k, heads, hi - lo])

        def copy_group(copy, p, i):
            t, g = divmod(i, NG)
            first, count, is_key = groups[g]
            src = t_bank(gs[i])[:, 0:count * P].rearrange("p (k n) -> p k n", n=P)
            cols = slice(t * P, (t + 1) * P)
            if is_key:
                at = first - PAIRS
                copy(kT[p][0:STK, at:at + count, 0, cols], src[0:STK])
                last = copy(kT[p][STK:P, at:at + count, 1, cols], src[STK:P])
            else:
                last = copy(qT[p][:, first:first + count, cols], src)
            last.then_inc(t_out[bank[gs[i]]], 1)

        def q_stack(t):
            return stack[:, t, 0:NH * STK].rearrange("p (h r d) -> p h r d", r=4, d=HD)

        def k_stack(t):
            if multi:
                return stack[:, t, NH * STK:].rearrange("p (h r s d) -> p h r s d", r=2, s=2, d=HD)
            return stack[:, t, NH * STK:].rearrange("p (c r s d) -> p c r s d", c=2, r=2, s=2, d=HD)

        def q_part(ap, t):
            return ap[:, t, 0:NH * HD].rearrange("p (h d) -> p h d", d=HD).unsqueeze(2).to_broadcast([P, NH, 2, HD])

        def k_part(ap, t):
            c = ap[:, t, NH * HD:QK]
            if multi:
                return c.rearrange("p (h d) -> p h d", d=HD).unsqueeze(2).to_broadcast([P, NH, 2, HD])
            return c.unsqueeze(1).unsqueeze(1).to_broadcast([P, 2, 2, HD])

        @block.tensor
        def _(pe):
            def proj_transpose(s):
                pe.wait_ge(y_ready, s + 1)
                turn_free(pe, s - 1, "yT")
                for c in range(FC):
                    for t in range(TB):
                        last = nc.tensor.transpose(t_bank("yT")[:, c * N + t * P:c * N + (t + 1) * P],
                                                   y[:, t, c * P:(c + 1) * P], ident[:])
                last.then_inc(yT_ps, 1)

            def project(out, t, lo, hi, first):
                n = 0
                for c in range(FC):
                    for a, w in split_passes(yT_hi, yT_lo, wqkv_hi, wqkv_lo):
                        last = nc.tensor.matmul(out, a[:, c, t * P:(t + 1) * P], w[:, c, lo:hi],
                                                start=first and n == 0, stop=n == 3 * FC - 1,
                                                skip_group_check=True)
                        n += 1
                return last

            def projection_free(s):
                turn_done(pe, s - 1, "yT")
                wait(pe, qn_done, s)
                wait(pe, out_added, s - 1)

            def proj_qk(s, t):
                if t == 0 and multi:
                    pe.wait_ge(v_done, s + 1)
                    out = ps_p
                elif t == 0:
                    projection_free(s)
                    out = ps_p
                else:
                    turn_free(pe, s - 1, "qk1")
                    out = t_bank("qk1")
                cols = QK if multi else QK + VW
                project(out[:, 0:cols], t, 0, cols, True).then_inc(qk_ps, 1)

            def proj_v(s):
                if not multi:
                    return
                projection_free(s)
                for t in range(TB):
                    last = project(ps_p[:, t * VW:(t + 1) * VW], t, QK, QK + VW, t == 0)
                last.then_inc(v_ps, 1)

            def proj_group(s, i):
                t, g = divmod(i, NG)
                first, count, _ = groups[g]
                if g == 0:
                    pe.wait_ge(stack_hi, TB * s + t + 1)
                    pe.wait_ge(stack_lo, TB * s + t + 1)
                turn_free(pe, s - 1, gs[i])
                for k in range(count):
                    last = nc.tensor.transpose(t_bank(gs[i])[:, k * P:(k + 1) * P].bitcast(F32R),
                                               stack[:, t, (first + k) * P:(first + k + 1) * P], ident_r[:])
                last.then_inc(group_ps, 1)

            def keys(p, j, hh):
                return kT[p][:, j if multi else 0, hh]

            def scores(s, p, j):
                if j == 0:
                    groups_done(pe, s)
                    wait(pe, exp_done, PAIRS * s)
                if j >= 2:
                    pe.wait_ge(max_done, PAIRS * s + j - 1)
                for hh in range(2):
                    out = ring[:, 2 * (j % 2) + hh]
                    nc.tensor.matmul(out[:, 0:P], qT[p][:, j, 0:P], keys(p, j, hh)[:, 0:P],
                                     start=True, stop=False, skip_group_check=True)
                    nc.tensor.matmul(out[:, P:TRI], qT[p][:, j, P:N], keys(p, j, hh)[:, 0:N],
                                     start=False, stop=False, skip_group_check=True)
                    last = nc.tensor.matmul(
                        out[:, 0:2 * N].rearrange("p (a k) -> p a k", k=N)[:, :, 0:P], ident_r[:],
                        mask_r[:].unsqueeze(1).to_broadcast([P, 2, P]), start=False, stop=True,
                        skip_group_check=True)
                last.then_inc(s_ps, 1)

            def transpose_maxima(s):
                pe.wait_ge(max_stacked, s + 1)
                turn_free(pe, s, "maxT")
                for t in range(TB):
                    last = nc.tensor.transpose(t_bank("maxT")[0:2 * NH, t * P:(t + 1) * P].bitcast(F32R),
                                               max_stack[:, t].rearrange("p h s -> p (h s)"), ident_r[:])
                last.then_inc(maxT_ps, 1)

            def shifted_scores(s, p, j):
                if j == 0:
                    turn_done(pe, s, "maxT")
                    pe.wait_ge(max_done, PAIRS * (s + 1))
                if j >= 2:
                    pe.wait_ge(exp_done, PAIRS * s + j - 1)
                for hh in range(2):
                    out = ring[:, 2 * (j % 2) + hh]
                    nc.tensor.matmul(out[:, 0:N], keys(p, j, hh)[:, 0:P], qT[p][:, j, 0:N],
                                     start=True, stop=False, skip_group_check=True)
                    nc.tensor.matmul(out[:, N:TRI], keys(p, j, hh)[:, P:N], qT[p][:, j, P:N],
                                     start=False, stop=False, skip_group_check=True)
                    nc.tensor.matmul(out[:, 0:N], sel_head[:, 2 * j + hh], maxT[:, 0:N],
                                     start=False, stop=False, skip_group_check=True)
                    last = nc.tensor.matmul(out[:, N:TRI], sel_head[:, 2 * j + hh], maxT[:, P:N],
                                            start=False, stop=True, skip_group_check=True)
                last.then_inc(st_ps, 1)

            def attend(s, p, j):
                pe.wait_ge(cut_done, PAIRS * s + j + 1)
                if j == 0 and multi:
                    pe.wait_ge(v_done, s + 1)
                elif j == 0:
                    pe.wait_ge(qn_done, s + 1)
                    turn_done(pe, s - 1, "qk1")
                if j % (PAIRS // 2) == 0:
                    wait(pe, av_out, 2 * s + 2 * j // PAIRS)
                for hh in range(2):
                    h = 2 * j + hh
                    pr, vh, row, col = probs[:, j % NPB, hh], h if multi else 0, HV * (h % 4), N * (h // 4 % 2)
                    nc.tensor.matmul(ps_av[row:row + HV, col:col + N], v[p][:, 0, vh], pr[:, 0:N],
                                     start=col == 0, stop=False, skip_group_check=True)
                    last = nc.tensor.matmul(ps_av[row:row + HV, col + P:col + N], v[p][:, 1, vh], pr[:, N:TRI],
                                            start=False, stop=True, skip_group_check=True)
                last.then_inc(av_ps, 1)

            def half_transpose(s, half, during):
                pe.wait_ge(av_out, 2 * s + half + 1)
                turn_free(pe, during, f"half{half}")
                for t in range(TB):
                    for g in range(2):
                        at = (2 * t + g) * P
                        last = nc.tensor.transpose(t_bank(f"half{half}")[:, at:at + P],
                                                   av_sb[half][:, g, t * P:(t + 1) * P], ident[:])
                last.then_inc(half_ps, 1)

            def out_transpose(s):
                turn_done(pe, s, "half0")
                turn_done(pe, s + 1, "half1")
                turn_free(pe, s + 1, "oT")
                for c in range(FC):
                    for t in range(TB):
                        last = nc.tensor.transpose(
                            t_bank("oT")[:, c * N + t * P:c * N + (t + 1) * P],
                            o[:, t].rearrange("p h d -> p (h d)")[:, c * P:(c + 1) * P], ident[:])
                last.then_inc(oT_ps, 1)

            def out_project(s, qk_out):
                turn_done(pe, s + 1, "oT")
                pe.wait_ge(qn_done, qk_out)
                for t in range(TB):
                    n = 0
                    for c in range(FC):
                        for a, w in split_passes(oT_hi, oT_lo, wout_hi, wout_lo):
                            last = nc.tensor.matmul(ps_p[:, t * H:(t + 1) * H], a[:, c, t * P:(t + 1) * P],
                                                    w[:, c, :], start=t == 0 and n == 0,
                                                    stop=n == 3 * FC - 1, skip_group_check=True)
                            n += 1
                last.then_inc(out_ps, 1)

            def sequence(s, p, before, after):
                for j in range(PAIRS):
                    scores(s, p, j)
                    if j == 1 and before:
                        half_transpose(s - 1, 1, s)
                    if j == 2 and before:
                        out_transpose(s - 1)
                    if j == 3 and after:
                        proj_transpose(s + 1)
                    if j == 4 and before:
                        out_project(s - 1, s + 1)
                    if j == 6 and after:
                        proj_v(s + 1)
                if after:
                    proj_qk(s + 1, 0)
                transpose_maxima(s)
                if after:
                    proj_qk(s + 1, 1)
                for step in PE_ORDER[layer]:
                    what, n = step[0], int(step[1:])
                    if what == "t":
                        shifted_scores(s, p, n)
                    elif what == "a":
                        attend(s, p, n)
                    elif what == "h":
                        half_transpose(s, n, s)
                    elif after:
                        proj_group(s + 1, n)

            proj_transpose(0)
            proj_v(0)
            for t in range(TB):
                proj_qk(0, t)
            for i in range(NF):
                proj_group(0, i)
            pe.wait_ge(constants, 2)
            sequence(0, 0, False, True)
            with pe.Fori(0, (B - 2) // 2) as r:
                for k in range(2):
                    sequence(2 * r + 1 + k, (1 + k) % 2, True, True)
            sequence(B - 1, (B - 1) % 2, True, False)
            half_transpose(B - 1, 1, B)
            out_transpose(B - 1)
            out_project(B - 1, B)

        @block.scalar
        def _(act):
            def y_hi(s):
                act.wait_ge(yT_ps, s + 1)
                wait(act, qk_ps, TB * s)
                nc.scalar.activation(yT_hi[:].rearrange("p c n -> p (c n)"), t_bank("yT")[:],
                                     ACT.Copy).then_inc(yT_hi_done, 1)

            def square(s, t):
                if not multi:
                    return
                act.wait_ge(qk_ps, TB * s + t + 1)
                wait(act, ss_done, TB * s)
                src = t_bank("qk1") if t else ps_p
                nc.scalar.activation(sq[:, t], src[:, 0:QK], ACT.Square).then_inc(sq_done, 1)

            def copy_v(s, p):
                if not multi:
                    return
                act.wait_ge(v_ps, s + 1)
                nc.scalar.activation(v[p][:, :, :, 0:HD],
                                     ps_p[:, 0:TB * VW].rearrange("p (t h d) -> p t h d", t=TB, d=HD),
                                     ACT.Copy).then_inc(v_done, 1)

            def stack_his(s, t):
                act.wait_ge(rot_done, TB * s + t + 1)
                wait(act, group_ps, NF * s)
                nc.scalar.activation(q_stack(t)[:, :, 0:2], q_part(rotated, t), ACT.Copy)
                nc.scalar.activation(k_stack(t)[:, :, :, 0], k_part(rotated, t),
                                     ACT.Copy).then_inc(stack_hi, 1)

            def scalar_copy(out, src):
                return nc.scalar.activation(out, src, ACT.Copy)

            def maxima(s):
                act.wait_ge(maxT_ps, s + 1)
                wait(act, st_ps, PAIRS * s)
                nc.scalar.activation(maxT[0:2 * NH], t_bank("maxT")[0:2 * NH, 0:N],
                                     ACT.Copy).then_inc(t_out[bank["maxT"]], 1)

            def exponentials(s, j):
                act.wait_ge(st_ps, PAIRS * s + j + 1)
                if j >= NPB:
                    act.wait_ge(av_ps, PAIRS * s + j - NPB + 1)
                else:
                    wait(act, av_ps, PAIRS * s)
                nc.scalar.activation(probs[:, j % NPB], ring[:, 2 * (j % 2):2 * (j % 2) + 2, 0:TRI], ACT.Exp,
                                     scale=exp_scale).then_inc(exp_done, 1)

            def outputs(s, half):
                act.wait_ge(av_ps, PAIRS * s + (half + 1) * PAIRS // 2)
                wait(act, half_ps, 2 * s + half - 1)
                nc.scalar.activation(av_sb[half][:].rearrange("p g n -> p (g n)"), ps_av[:],
                                     ACT.Copy).then_inc(av_out, 1)

            def out_hi(s):
                act.wait_ge(oT_ps, s + 1)
                nc.scalar.activation(oT_hi[:].rearrange("p c n -> p (c n)"), t_bank("oT")[:],
                                     ACT.Copy).then_inc(oT_hi_done, 1)

            def sequence(s, p, before, after):
                if before:
                    out_hi(s - 1)
                if after:
                    y_hi(s + 1)
                    copy_v(s + 1, 1 - p)
                    square(s + 1, 0)
                maxima(s)
                if after:
                    square(s + 1, 1)
                for step in ACT_ORDER[layer]:
                    what, n = step[0], int(step[1:])
                    if what == "e":
                        exponentials(s, n)
                    elif what == "o":
                        outputs(s, n)
                    elif what == "s" and after:
                        stack_his(s + 1, n)
                    elif what == "c" and after:
                        act.wait_ge(group_ps, NF * (s + 1) + n + 1)
                        copy_group(scalar_copy, 1 - p, n)

            y_hi(0)
            copy_v(0, 0)
            for t in range(TB):
                square(0, t)
            for t in range(TB):
                stack_his(0, t)
            for i in range(NF):
                if i not in vector_groups:
                    act.wait_ge(group_ps, i + 1)
                    copy_group(scalar_copy, 0, i)
            sequence(0, 0, False, True)
            with act.Fori(0, (B - 2) // 2) as r:
                for k in range(2):
                    sequence(2 * r + 1 + k, (1 + k) % 2, True, True)
            sequence(B - 1, (B - 1) % 2, True, False)
            out_hi(B - 1)

        @block.vector
        def _(dve):
            def ln_stats(s):
                dve_ln.start(s)
                for t in range(TB):
                    last = nc.vector.bn_stats(stats[:, t], x[:, ds(TB * s + t, 1)].rearrange("p a n -> p (a n)"))
                dve_ln.inc(last)
                dve_ln.wait(dve)
                passed(dve, waited_dve)
                for t in range(TB):
                    last = nc.vector.bn_aggr(mv[:, t], stats[:, t])
                last.then_inc(var_ready, 1)

            def y_lo(s):
                dve.wait_ge(yT_hi_done, s + 1)
                wait(dve, qk_ps, TB * s)
                nc.vector.tensor_tensor(yT_lo[:].rearrange("p c n -> p (c n)"), t_bank("yT")[:],
                                        yT_hi[:].rearrange("p c n -> p (c n)").bitcast(F32),
                                        ALU.subtract).then_inc(t_out[bank["yT"]], 1)

            def sum_squares(s, t):
                if not multi:
                    return
                dve.wait_ge(sq_done, TB * s + t + 1)
                nc.vector.tensor_reduce(ss[:, t], sq[:, t].rearrange("p (h d) -> p h d", d=HD), AX_X,
                                        ALU.add).then_inc(ss_done, 1)

            def rms_rstd(s):
                if not multi:
                    return
                dve_rs.start(s)
                v_, g, step = (a[:].rearrange("p t h -> p (t h)") for a in (ss_eps, rs, rs_step))
                dve.wait_ge(ss_done, TB * (s + 1))
                dve_rs.inc(nc.vector.tensor_scalar(v_, ss[:].rearrange("p t h -> p (t h)"), 1.0 / HD, RMS_EPS,
                                                   ALU.mult, ALU.add))
                dve_rs.wait(dve)
                dve_rs.inc(nc.vector.tensor_scalar(g.bitcast(I32), v_.bitcast(I32), -0.5, RSQRT_GUESS,
                                                   ALU.mult, ALU.add))
                for _ in range(NEWTON):
                    dve_rs.wait(dve)
                    dve_rs.inc(nc.vector.scalar_tensor_tensor(step, g, -0.5, g, ALU.mult, ALU.mult))
                    dve_rs.wait(dve)
                    dve_rs.inc(nc.vector.tensor_tensor(step, step, v_, ALU.mult))
                    dve_rs.wait(dve)
                    dve_rs.inc(nc.vector.scalar_tensor_tensor(g, step, 1.5, g, ALU.add, ALU.mult))
                dve_rs.wait(dve)
                dve_rs.end()

            def norm_qk(s, p, t):
                if not multi:
                    dve.wait_ge(qk_ps, TB * s + t + 1)
                wait(dve, rot_done, TB * s)
                ps = t_bank("qk1") if t else ps_p
                src = ps[:, 0:QK].rearrange("p (h d) -> p h d", d=HD)
                dst = qn[:, t].rearrange("p (h d) -> p h d", d=HD)
                if multi:
                    ins = nc.vector.tensor_tensor(dst, src, rs[:, t].unsqueeze(2).to_broadcast([P, NH + NK, HD]),
                                                  ALU.mult)
                else:
                    nc.vector.tensor_copy(v[p][:, t, 0, 0:HD], ps[:, QK:QK + VW])
                    ins = nc.vector.tensor_copy(dst, src)
                ins.then_inc(t_out[bank["qk1"]] if t else qn_done, 1)

            def rotate(s, t):
                half = HD // 2
                if t == 0:
                    dve.wait_ge(qn_done, s + 1)
                else:
                    turn_done(dve, s - 1, "qk1")
                for (src, which), (dst, _) in zip(rot_parts(qn, t), rot_parts(rot_c, t)):
                    last = nc.vector.tensor_tensor(dst, src, table(tab_c, t, which, src.shape[2]), ALU.mult)
                dve_rot.inc(last)
                for (src, which), (dst, _) in zip(rot_parts(qn, t), rot_parts(rot_s, t)):
                    for a, b in ((0, half), (half, 0)):
                        last = nc.vector.tensor_tensor(dst[:, :, :, a:a + half], src[:, :, :, b:b + half],
                                                       table(tab_s, t, which, src.shape[2], a, a + half), ALU.mult)
                dve_rot.inc(last)
                dve_rot.wait(dve)
                wait(dve, stack_hi, TB * s)
                nc.vector.tensor_tensor(rotated[:, t], rot_c[:, t], rot_s[:, t], ALU.add).then_inc(rot_done, 1)

            def stack_los(s, t):
                dve.wait_ge(stack_hi, TB * s + t + 1)
                wait(dve, group_ps, NF * s)
                nc.vector.tensor_tensor(q_stack(t)[:, :, 2:4], q_part(rotated, t),
                                        q_stack(t)[:, :, 0:2].bitcast(F32), ALU.subtract)
                nc.vector.tensor_tensor(k_stack(t)[:, :, :, 1], k_part(rotated, t),
                                        k_stack(t)[:, :, :, 0].bitcast(F32), ALU.subtract).then_inc(stack_lo, 1)

            def maxima(s, j):
                dve.wait_ge(s_ps, PAIRS * s + j + 1)
                blocks = ring[:, 2 * (j % 2):2 * (j % 2) + 2, 0:TRI].rearrange("p h (b k) -> p h b k", k=P)
                nc.vector.tensor_reduce(block_max[:, 2 * j:2 * j + 2], blocks, AX_X, ALU.max,
                                        negate=True).then_inc(max_done, 1)

            def stack_maxima(s):
                dve_max.start(s)
                dve.wait_ge(max_done, PAIRS * (s + 1))
                wait(dve, maxT_ps, s)
                nc.vector.tensor_copy(neg_max[:, 0], block_max[:, :, 0])
                dve_max.inc(nc.vector.tensor_tensor(neg_max[:, 1], block_max[:, :, 1], block_max[:, :, 2], ALU.min))
                dve_max.wait(dve)
                dve_max.inc(nc.vector.tensor_copy(max_stack[:, :, :, 0], neg_max[:]))
                dve_max.wait(dve)
                nc.vector.tensor_tensor(max_stack[:, :, :, 1], neg_max[:], max_stack[:, :, :, 0].bitcast(F32),
                                        ALU.subtract).then_inc(max_stacked, 1)
                dve_max.end()

            def norm_half(s, half):
                dve_norm.start(s)
                dve_norm.n = half
                dve.wait_ge(half_ps, 2 * s + half + 1)
                if half == 0:
                    wait(dve, oT_ps, s)
                hs = slice(half * HALF_HEADS, (half + 1) * HALF_HEADS)
                out = t_bank(f"half{half}")[:].rearrange("p (t h d) -> p t h d", t=TB, d=HV)
                dve_norm.inc(nc.vector.reciprocal(recip[:, half], out[:, :, :, HD]))
                dve_norm.wait(dve)
                nc.vector.tensor_tensor(o[:, :, hs], out[:, :, :, 0:HD],
                                        recip[:, half].unsqueeze(3).to_broadcast([P, TB, HALF_HEADS, HD]),
                                        ALU.mult).then_inc(t_out[bank[f"half{half}"]], 1)

            def out_lo(s):
                dve.wait_ge(oT_hi_done, s + 1)
                nc.vector.tensor_tensor(oT_lo[:].rearrange("p c n -> p (c n)"), t_bank("oT")[:],
                                        oT_hi[:].rearrange("p c n -> p (c n)").bitcast(F32),
                                        ALU.subtract).then_inc(t_out[bank["oT"]], 1)

            def out_add(s):
                tiles = x[:, ds(TB * s, TB)]
                if bias is not None:
                    dve.wait_ge(bias_added, s + 1)
                dve.wait_ge(out_ps, s + 1)
                nc.vector.tensor_tensor(tiles, ps_p[:].rearrange("p (t n) -> p t n", t=TB), tiles,
                                        ALU.add).then_inc(out_added, 1)

            def prepare(s, p):
                for t in range(TB):
                    sum_squares(s, t)
                rms_rstd(s)
                norm_qk(s, p, 0)
                norm_qk(s, p, 1)
                dve_rot.start(s)
                for t in range(TB):
                    rotate(s, t)
                dve_rot.end()

            def sequence(s, p, before, after):
                if after:
                    ln_stats(s + 1)
                for j in range(PAIRS):
                    maxima(s, j)
                    if j == 1 and before:
                        norm_half(s - 1, 1)
                    if j == 2 and before:
                        out_lo(s - 1)
                    if j == 3 and after:
                        y_lo(s + 1)
                    if j == 4 and before:
                        out_add(s - 1)
                stack_maxima(s)
                if after:
                    prepare(s + 1, 1 - p)
                for step in DVE_ORDER[layer]:
                    what, n = step[0], int(step[1:])
                    if what == "n":
                        norm_half(s, n)
                    elif what == "l" and after:
                        stack_los(s + 1, n)
                    elif after:
                        dve.wait_ge(group_ps, NF * (s + 1) + n + 1)
                        copy_group(nc.vector.tensor_copy, 1 - p, n)

            ln_stats(0)
            for i in range(2):
                nc.vector.memset(v[i][:, :, :, HD:HV], 0.0)
            nc.vector.memset(zero[:], 0.0).then_inc(constants, 1)
            dve.wait_ge(constants, 1)
            nc.vector.tensor_copy(maxT[:], zero[:].to_broadcast([P, N]))
            for i in range(2):
                for hh, rows in ((0, slice(STK, P)), (1, slice(0, STK))):
                    for c in range(kT[i].shape[1]):
                        nc.vector.tensor_copy(kT[i][rows, c, hh], zero[rows].to_broadcast([STK, N]))
                last = nc.vector.memset(v[i][:, :, :, HD:HD + 1], 1.0)
            last.then_inc(constants, 1)
            y_lo(0)
            prepare(0, 0)
            for t in range(TB):
                stack_los(0, t)
            for i in vector_groups:
                dve.wait_ge(group_ps, i + 1)
                copy_group(nc.vector.tensor_copy, 0, i)
            sequence(0, 0, False, True)
            with dve.Fori(0, (B - 2) // 2) as r:
                for k in range(2):
                    sequence(2 * r + 1 + k, (1 + k) % 2, True, True)
            sequence(B - 1, (B - 1) % 2, True, False)
            norm_half(B - 1, 1)
            out_lo(B - 1)
            out_add(B - 1)
            dve.wait_ge(out_added, B)

        @block.gpsimd
        def _(pool):
            def ln_rstd(s):
                pool_ln.start(s)
                pool.wait_ge(var_ready, s + 1)
                wait(pool, y_ready, s)
                passed(pool, waited_pool)
                pool_ln.inc(nc.gpsimd.tensor_scalar(var_eps[:], mv[:, :, 1], LN_EPS, None, ALU.add))
                pool_ln.wait(pool)
                nc.gpsimd.tensor_tensor(rstd[:], var_eps[:], half_neg[:].to_broadcast([P, TB]),
                                        ALU.pow).then_inc(rstd_ready, 1)

            def ln_apply(s):
                pool.wait_ge(rstd_ready, s + 1)
                wait(pool, yT_ps, s)
                pool_ln.inc(nc.gpsimd.tensor_tensor(y[:], x[:, ds(TB * s, TB)],
                                                    mv[:, :, 0].unsqueeze(2).to_broadcast([P, TB, H]),
                                                    ALU.subtract))
                pool_ln.wait(pool)
                nc.gpsimd.tensor_tensor(y[:], y[:], rstd[:].unsqueeze(2).to_broadcast([P, TB, H]),
                                        ALU.mult).then_inc(y_ready, 1)

            def add_bias(s):
                if bias is None:
                    return
                pool.wait_ge(y_ready, s + 1)
                passed(pool, waited_pool)
                tiles = x[:, ds(TB * s, TB)]
                nc.gpsimd.tensor_tensor(tiles, tiles, bias[:].unsqueeze(1).to_broadcast([P, TB, H]),
                                        ALU.add).then_inc(bias_added, 1)

            def cut(s, j):
                pool.wait_ge(exp_done, PAIRS * s + j + 1)
                passed(pool, waited_pool)
                diagonal = probs[:, j % NPB].rearrange("p h (a k) -> p h a k", k=P)
                for a in (0, 2):
                    last = nc.gpsimd.affine_select(out=diagonal[:, :, a], in_=diagonal[:, :, a],
                                                   compare_op=ALU.is_ge, fill=0.0, base=0,
                                                   pattern=[[0, 2], [1, P]], channel_multiplier=-1)
                last.then_inc(cut_done, 1)

            def sequence(s, p, before, after):
                if after:
                    ln_rstd(s + 1)
                    ln_apply(s + 1)
                add_bias(s)
                for j in range(PAIRS):
                    cut(s, j)

            ln_rstd(0)
            ln_apply(0)
            sequence(0, 0, False, True)
            with pool.Fori(0, (B - 2) // 2) as r:
                for k in range(2):
                    sequence(2 * r + 1 + k, (1 + k) % 2, True, True)
            sequence(B - 1, (B - 1) % 2, True, False)


def route(nc, env, layer, wts, E, w_all):
    x, ident, half_neg, xT_hi, xT_lo = env["x"], env["ident"], env["half_neg"], env["xT_hi"], env["xT_lo"]
    logits, raw, w_hi, w_lo = env["logits"], env["raw"], env["w_hi"], env["w_lo"]
    wr_hi, wr_lo = wts["router_hi"], wts["router_lo"]
    pre = f"r{layer}_"
    with ExitStack() as ctx:
        def sb(name, shape, dt=F32):
            return ctx.enter_context(nc.sbuf_tensor(pre + name, shape, dt))

        stats = [sb(f"stats{i}", [P, TB, 6]) for i in range(2)]
        mv = [sb(f"mv{i}", [P, TB, 2]) for i in range(2)]
        var_eps = [sb(f"var_eps{i}", [P, TB]) for i in range(2)]
        rstd = [sb(f"rstd{i}", [P, TB]) for i in range(2)]
        y = [sb(f"y{i}", [P, TB, H]) for i in range(2)]
        logitsT = sb("logitsT", [E, T])
        ps_y = [ctx.enter_context(nc.psum_tensor(pre + f"ps_y{i}", [P, 512], F32)) for i in range(2)]
        ps_l = [ctx.enter_context(nc.psum_tensor(pre + f"ps_l{i}", [P, 512], F32)) for i in range(2)]
        ps_t = ctx.enter_context(nc.psum_tensor(pre + "ps_t", [P, 512], F32))

        with semaphores(nc) as make_sem, ExitStack() as sems:
            def sem1(name):
                return make_sem(pre + name)

            stats_done = sem1("stats_done")
            var_ready = sem1("var_ready")
            eps_done = sem1("eps_done")
            rstd_ready = sem1("rstd_ready")
            y_ready = sem1("y_ready")
            yT_ps = sem1("yT_ps")
            hi_done = sem1("hi_done")
            lo_done = sem1("lo_done")
            l_ps = sem1("l_ps")
            l_done = sem1("l_done")
            t_ps = sem1("t_ps")
            t_done = sem1("t_done")
            waited_dve = sem1("waited_dve")
            waited_pool = sem1("waited_pool")
            w_loaded = [sem1(f"w_loaded{i}") for i in range(2)]
            w_hi_done = sem1("w_hi_done")
            w_lo_done = sem1("w_lo_done")
            block = sems.enter_context(nc.Block())

            @block.sync
            def _(sp):
                for k in range(2):
                    sp.dma_start(raw[k][:], w_all[k]).then_inc(w_loaded[k], 16)

            def run(eng, body):
                for s in range(2):
                    body(s, s)
                with eng.Fori(1, B // 2 - 1) as r:
                    for k in range(2):
                        body(2 * r + k, k)
                for s in range(B - 2, B):
                    body(s, s % 2)

            def behind(s, n):
                return not isinstance(s, int) or s + n < B

            @block.vector
            def _(dve):
                def statistics(s, p):
                    wait(dve, y_ready, s - 1)
                    for t in range(TB):
                        last = nc.vector.bn_stats(stats[p][:, t],
                                                  x[:, ds(TB * s + t, 1)].rearrange("p a n -> p (a n)"))
                    last.then_inc(stats_done, 1)
                    dve.wait_ge(stats_done, s + 1)
                    passed(dve, waited_dve)
                    for t in range(TB):
                        last = nc.vector.bn_aggr(mv[p][:, t], stats[p][:, t])
                    last.then_inc(var_ready, 1)

                def apply(s, p):
                    dve.wait_ge(rstd_ready, s + 1)
                    wait(dve, yT_ps, s - 1)
                    for t in range(TB):
                        last = nc.vector.tensor_scalar(y[p][:, t],
                                                       x[:, ds(TB * s + t, 1)].rearrange("p a n -> p (a n)"),
                                                       mv[p][:, t, 0:1], rstd[p][:, t:t + 1],
                                                       ALU.subtract, ALU.mult)
                    last.then_inc(y_ready, 1)

                def lo(s, p):
                    dve.wait_ge(hi_done, s + 1)
                    nc.vector.tensor_tensor(xT_lo[:, :, ds(N * s, N)], ps_y[p][:].rearrange("p (c n) -> p c n", n=N),
                                            xT_hi[:, :, ds(N * s, N)].bitcast(F32), ALU.subtract).then_inc(lo_done, 1)

                def body(s, p):
                    if behind(s, 1):
                        apply(s + 1, 1 - p)
                    if behind(s, 2):
                        statistics(s + 2, p)
                    lo(s, p)

                statistics(0, 0)
                statistics(1, 1)
                apply(0, 0)
                run(dve, body)

            @block.gpsimd
            def _(pool):
                def body(s, p):
                    pool.wait_ge(var_ready, s + 1)
                    wait(pool, y_ready, s - 1)
                    passed(pool, waited_pool)
                    nc.gpsimd.tensor_scalar(var_eps[p][:], mv[p][:, :, 1], LN_EPS, None, ALU.add).then_inc(eps_done, 1)
                    pool.wait_ge(eps_done, s + 1)
                    nc.gpsimd.tensor_tensor(rstd[p][:], var_eps[p][:], half_neg[:].to_broadcast([P, TB]),
                                            ALU.pow).then_inc(rstd_ready, 1)

                run(pool, body)
                for k in range(2):
                    pool.wait_ge(w_hi_done, k + 1)
                    nc.gpsimd.tensor_tensor(w_lo[k][:], raw[k][:], w_hi[k][:].bitcast(F32),
                                            ALU.subtract).then_inc(w_lo_done, 1)
                pool.wait_ge(w_lo_done, 2)

            @block.tensor
            def _(pe):
                def transpose(s, p):
                    pe.wait_ge(y_ready, s + 1)
                    wait(pe, lo_done, s - 1)
                    for c in range(FC):
                        for t in range(TB):
                            last = nc.tensor.transpose(ps_y[p][:, c * N + t * P:c * N + (t + 1) * P],
                                                       y[p][:, t, c * P:(c + 1) * P], ident[:])
                    last.then_inc(yT_ps, 1)

                def project(s, p):
                    pe.wait_ge(lo_done, s + 1)
                    wait(pe, l_done, s - 1)
                    n = 0
                    for c in range(FC):
                        for w, a in split_passes(wr_hi, wr_lo, xT_hi, xT_lo):
                            last = nc.tensor.matmul(ps_l[p][0:E, 0:N], w[:, c, :], a[:, c, ds(N * s, N)],
                                                    start=n == 0, stop=n == 3 * FC - 1)
                            n += 1
                    last.then_inc(l_ps, 1)

                def body(s, p):
                    if behind(s, 1):
                        transpose(s + 1, 1 - p)
                    project(s, p)

                transpose(0, 0)
                run(pe, body)
                pe.wait_ge(l_done, B)
                for t in range(NT):
                    last = nc.tensor.transpose(ps_t[:, t * E:(t + 1) * E], logitsT[:, t * P:(t + 1) * P],
                                               ident[0:E, 0:E])
                last.then_inc(t_ps, 1)

            @block.scalar
            def _(act):
                def hi(s, p):
                    act.wait_ge(yT_ps, s + 1)
                    nc.scalar.activation(xT_hi[:, :, ds(N * s, N)], ps_y[p][:].rearrange("p (c n) -> p c n", n=N),
                                         ACT.Copy).then_inc(hi_done, 1)

                def body(s, p):
                    if behind(s, 1):
                        hi(s + 1, 1 - p)
                    act.wait_ge(l_ps, s + 1)
                    nc.scalar.activation(logitsT[:, ds(N * s, N)], ps_l[p][0:E, 0:N], ACT.Copy).then_inc(l_done, 1)

                def split_hi(k):
                    act.wait_ge(w_loaded[k], 16)
                    nc.scalar.activation(w_hi[k][:], raw[k][:], ACT.Copy).then_inc(w_hi_done, 1)

                split_hi(0)
                hi(0, 0)
                split_hi(1)
                run(act, body)
                act.wait_ge(t_ps, 1)
                nc.scalar.activation(logits[:].rearrange("p t e -> p (t e)"), ps_t[:, 0:NT * E],
                                     ACT.Copy).then_inc(t_done, 1)
                act.wait_ge(t_done, 1)


def gates_top2(nc, dve, sb, ch, shifted, exp_done, logits, bias, gates, expo, E):
    EP = E + 8
    biased = sb("biased", [P, NT, EP])
    replaced = sb("replaced", [P, NT, EP])
    top = sb("top", [P, NT, 8])
    chosen = sb("chosen", [P, NT, E])
    lmax = sb("lmax", [P, NT])
    total = sb("total", [P, NT])

    def bc(ap):
        return ap.unsqueeze(2).to_broadcast([P, NT, E])

    nc.vector.memset(biased[:, :, E:EP], BIG)
    ch.inc(nc.vector.tensor_tensor(biased[:, :, 0:E], logits[:],
                                   bias[:].unsqueeze(1).to_broadcast([P, NT, E]), ALU.add))
    ch.inc(nc.vector.tensor_reduce(lmax[:], logits[:], AX_X, ALU.max))
    ch.wait(dve)
    yield
    nc.vector.tensor_tensor(expo[:], logits[:], bc(lmax[:]), ALU.subtract).then_inc(shifted, 1)
    for t in range(NT):
        last = nc.vector.max(top[:, t], biased[:, t, 0:E])
    ch.inc(last)
    ch.wait(dve)
    yield
    ch.inc(nc.vector.memset(top[:, :, 2:8], BIG))
    ch.wait(dve)
    yield
    for t in range(NT):
        last = nc.vector.match_replace(replaced[:, t], in_to_replace=top[:, t], in_values=biased[:, t],
                                       imm_value=-BIG)
    ch.inc(last)
    ch.wait(dve)
    yield
    ch.inc(nc.vector.tensor_tensor(chosen[:], replaced[:, :, 0:E], biased[:, :, 0:E], ALU.not_equal))
    dve.wait_ge(exp_done, 1)
    ch.inc(nc.vector.tensor_reduce(total[:], expo[:], AX_X, ALU.add))
    ch.wait(dve)
    yield
    ch.inc(nc.vector.reciprocal(total[:], total[:]))
    ch.wait(dve)
    yield
    ch.inc(nc.vector.tensor_tensor(expo[:], expo[:], bc(total[:]), ALU.mult))
    ch.wait(dve)
    yield
    ch.inc(nc.vector.tensor_tensor(gates[:], expo[:], chosen[:], ALU.mult))
    ch.wait(dve)
    yield
    ch.inc(nc.vector.tensor_reduce(total[:], gates[:], AX_X, ALU.add))
    ch.wait(dve)
    yield
    ch.inc(nc.vector.reciprocal(total[:], total[:]))
    ch.wait(dve)
    yield
    ch.inc(nc.vector.tensor_tensor(gates[:], gates[:], bc(total[:]), ALU.mult))
    ch.wait(dve)
    yield
    ch.end()


def gates_groups(nc, dve, sb, ch, sig_done, logits, bias, gates, scores, E):
    G, TOPG, SCALE = 8, 4, 2.5
    EG = E // G
    biased = sb("biased", [P, NT, E])
    pair_max = sb("pair_max", [P, NT, G, 2])
    pair_min = sb("pair_min", [P, NT, G, 2])
    first = sb("first", [P, NT, G])
    second = sb("second", [P, NT, G])
    second_low = sb("second_low", [P, NT, G])
    group = sb("group", [P, NT, 2 * G])
    group_out = sb("group_out", [P, NT, 2 * G])
    group_on = sb("group_on", [P, NT, G])
    top = sb("top", [P, NT, 8])
    masked = sb("masked", [P, NT, E])
    replaced = sb("replaced", [P, NT, E])
    chosen = sb("chosen", [P, NT, E])
    total = sb("total", [P, NT])

    def step(ins):
        ch.inc(ins)
        ch.wait(dve)

    dve.wait_ge(sig_done, 1)
    nc.vector.memset(group[:, :, G:], BIG)
    step(nc.vector.tensor_tensor(biased[:], scores[:], bias[:].unsqueeze(1).to_broadcast([P, NT, E]),
                                 ALU.add))
    yield
    quad = biased[:].rearrange("p t (g a b) -> p (t g) a b", a=2, b=2)
    pmx = pair_max[:].rearrange("p t g a -> p (t g) a")
    pmn = pair_min[:].rearrange("p t g a -> p (t g) a")
    nc.vector.tensor_tensor(pmx, quad[:, :, :, 0], quad[:, :, :, 1], ALU.max)
    step(nc.vector.tensor_tensor(pmn, quad[:, :, :, 0], quad[:, :, :, 1], ALU.min))
    yield
    f, s, lo = (a[:].rearrange("p t g -> p (t g)") for a in (first, second, second_low))
    nc.vector.tensor_tensor(f, pmx[:, :, 0], pmx[:, :, 1], ALU.max)
    nc.vector.tensor_tensor(s, pmx[:, :, 0], pmx[:, :, 1], ALU.min)
    step(nc.vector.tensor_tensor(lo, pmn[:, :, 0], pmn[:, :, 1], ALU.max))
    yield
    step(nc.vector.tensor_tensor(s, s, lo, ALU.max))
    yield
    step(nc.vector.tensor_tensor(group[:, :, 0:G], first[:], second[:], ALU.add))
    yield
    for t in range(NT):
        last = nc.vector.max(top[:, t], group[:, t, 0:G])
        if t == NT // 2 - 1:
            yield
    step(last)
    yield
    step(nc.vector.memset(top[:, :, TOPG:8], BIG))
    yield
    for t in range(NT):
        last = nc.vector.match_replace(group_out[:, t], in_to_replace=top[:, t], in_values=group[:, t],
                                       imm_value=-BIG)
    step(last)
    yield
    step(nc.vector.tensor_tensor(group_on[:], group_out[:, :, 0:G], group[:, :, 0:G], ALU.not_equal))
    yield
    step(nc.vector.tensor_tensor(
        masked[:].rearrange("p t (g e) -> p (t g) e", e=EG),
        biased[:].rearrange("p t (g e) -> p (t g) e", e=EG),
        group_on[:].rearrange("p t g -> p (t g)").unsqueeze(2).to_broadcast([P, NT * G, EG]), ALU.mult))
    yield
    step(nc.vector.tensor_scalar(masked[:], masked[:], 0.0, None, ALU.add))
    yield
    for t in range(NT):
        last = nc.vector.max(top[:, t], masked[:, t])
        if t == NT // 2 - 1:
            yield
    step(last)
    yield
    for t in range(NT):
        last = nc.vector.match_replace(replaced[:, t], in_to_replace=top[:, t], in_values=masked[:, t],
                                       imm_value=-BIG)
        if t == NT // 2 - 1:
            yield
    step(last)
    yield
    step(nc.vector.tensor_tensor(chosen[:], replaced[:], masked[:], ALU.not_equal))
    yield
    step(nc.vector.tensor_tensor(gates[:], scores[:], chosen[:], ALU.mult))
    yield
    step(nc.vector.tensor_reduce(total[:], gates[:], AX_X, ALU.add))
    yield
    step(nc.vector.reciprocal(total[:], total[:]))
    yield
    step(nc.vector.tensor_tensor(gates[:], gates[:], total[:].unsqueeze(2).to_broadcast([P, NT, E]),
                                 ALU.mult))
    yield
    step(nc.vector.tensor_scalar(gates[:], gates[:], SCALE, None, ALU.mult))
    yield
    ch.wait(dve)
    ch.end()


def experts(nc, env, layer, w_all, router_bias, E, out=None):
    x, xT_hi, xT_lo, logits = env["x"], env["xT_hi"], env["xT_lo"], env["logits"]
    NE = E + 2
    pre = f"e{layer}_"
    with semaphores(nc) as make_sem, ExitStack() as ctx:
        def sb(name, shape, dt=F32):
            return ctx.enter_context(nc.sbuf_tensor(pre + name, shape, dt))

        def pb(name, shape):
            return ctx.enter_context(nc.psum_tensor(pre + name, shape, F32))

        def sem(name):
            return make_sem(pre + name)

        raw, w_hi, w_lo = env["raw"], env["w_hi"], env["w_lo"]
        gates = sb("gates", [P, NT, E])
        scores = sb("scores", [P, NT, E])
        act_out = [sb(f"act_out{i}", [P, BLK]) for i in range(2)]
        hid = [sb(f"hid{i}", [P, BLK]) for i in range(2)]
        hid_hi = [sb(f"hid_hi{i}", [P, BLK], F32R) for i in range(2)]
        hid_lo = [sb(f"hid_lo{i}", [P, BLK], F32R) for i in range(2)]
        ps_a = [pb(f"ps_a{i}", [P, BLK]) for i in range(2)]
        ps_b = [pb(f"ps_b{i}", [P, BLK]) for i in range(2)]
        ps_d = [pb(f"ps_d{i}", [P, TPB, H]) for i in range(2)]

        w_loaded = [sem(f"w_loaded{i}") for i in range(2)]
        w_hi_done = sem("w_hi_done")
        w_lo_done = sem("w_lo_done")
        a_ps = sem("a_ps")
        b_ps = sem("b_ps")
        act_done = sem("act_done")
        hid_done = sem("hid_done")
        hi_done = sem("hi_done")
        lo_done = sem("lo_done")
        down_ps = sem("down_ps")
        added = sem("added")
        shifted = sem("shifted")
        scored = sem("scored")
        gate_chain = Chain(sem("gate_steps"), 13 if layer == 0 else 19)
        stored = [sem(f"stored{i}") for i in range(NBLK)]
        block = ctx.enter_context(nc.Block())

        A, Bc, D = 0, FC * P, 2 * FC * P

        @block.sync
        def _(sp):
            def load(k, n):
                sp.dma_start(raw[k][:], w_all[ds(n, 1)].rearrange("e p n -> p (e n)")).then_inc(w_loaded[k], 16)

            for k in range(2):
                load(k, 2 + k)
            with sp.Fori(2, NE // 2) as r:
                for k in range(2):
                    sp.wait_ge(w_lo_done, 2 * r + k - 3)
                    load(k, 2 * r + k)
            sp.wait_ge(w_lo_done, NE - 3)
            load(0, 0)
            if out is not None:
                rows = out.rearrange("b (t p) n -> p (b t) n", p=P)
                for blk in range(NBLK):
                    tiles = slice(blk * TPB, (blk + 1) * TPB)
                    sp.wait_ge(added, NBLK * (NE - 1) + blk + 1)
                    sp.dma_start(rows[:, tiles], x[:, tiles]).then_inc(stored[blk], 16)
                for blk in range(NBLK):
                    sp.wait_ge(stored[blk], 16)

        @block.gpsimd
        def _(pool):
            def split_lo(k, m):
                pool.wait_ge(w_hi_done, m - 1)
                pool.wait_ge(down_ps, NBLK * (m - 1))
                nc.gpsimd.tensor_tensor(w_lo[k][:], raw[k][:], w_hi[k][:].bitcast(F32),
                                        ALU.subtract).then_inc(w_lo_done, 1)

            with pool.Fori(1, NE // 2) as r:
                for k in range(2):
                    split_lo(k, 2 * r + k)
            split_lo(0, NE)
            pool.wait_ge(w_lo_done, NE - 1)

        @block.scalar
        def _(act):
            def split_hi(k, m, turn):
                act.wait_ge(w_loaded[k], 16 * turn)
                act.wait_ge(down_ps, NBLK * (m - 1))
                nc.scalar.activation(w_hi[k][:], raw[k][:], ACT.Copy).then_inc(w_hi_done, 1)

            def silu(i, p):
                act.wait_ge(a_ps, i + 1)
                wait(act, hid_done, i - 1)
                nc.scalar.activation(act_out[p][:], ps_a[p][:], ACT.Silu).then_inc(act_done, 1)

            def hidden_hi(i, p):
                act.wait_ge(hid_done, i + 1)
                wait(act, down_ps, i - 1)
                nc.scalar.activation(hid_hi[p][:], hid[p][:], ACT.Copy).then_inc(hi_done, 1)

            def expert(n, k, turn):
                for blk in range(NBLK):
                    silu(NBLK * n + blk, blk % 2)
                    hidden_hi(NBLK * n + blk, blk % 2)
                    if blk == 1 and not (isinstance(n, int) and n == 0):
                        split_hi(1 - k, n + 1, turn + k)

            if layer == 0:
                act.wait_ge(shifted, 1)
                nc.scalar.activation(scores[:], scores[:], ACT.Exp).then_inc(scored, 1)
            else:
                nc.scalar.activation(scores[:], logits[:], ACT.Sigmoid).then_inc(scored, 1)
            expert(0, 0, 0)
            expert(1, 1, 0)
            with act.Fori(1, NE // 2) as r:
                for k in range(2):
                    expert(2 * r + k, k, r)

        @block.vector
        def _(dve):
            def hidden(i, p, steps=None):
                dve.wait_ge(act_done, i + 1)
                dve.wait_ge(b_ps, i + 1)
                wait(dve, lo_done, i - 1)
                nc.vector.tensor_tensor(hid[p][:], ps_b[p][:], act_out[p][:], ALU.mult).then_inc(hid_done, 1)
                if steps is not None:
                    next(steps, None)
                dve.wait_ge(hi_done, i + 1)
                wait(dve, down_ps, i - 1)
                nc.vector.tensor_tensor(hid_lo[p][:], hid[p][:], hid_hi[p][:].bitcast(F32),
                                        ALU.subtract).then_inc(lo_done, 1)

            def add(i, blk, gate=None):
                dve.wait_ge(down_ps, i + 1)
                wait(dve, added, i + 1 - NBLK)
                for q in range(TPB):
                    t, d = blk * TPB + q, ps_d[blk % 2][:, q]
                    if gate is None:
                        last = nc.vector.tensor_tensor(x[:, t], d, x[:, t], ALU.add)
                    else:
                        last = nc.vector.scalar_tensor_tensor(x[:, t], d, gates[:, t, ds(gate, 1)], x[:, t],
                                                              ALU.mult, ALU.add)
                last.then_inc(added, 1)

            def expert(n, gate, gate_before):
                for blk in range(NBLK):
                    i = NBLK * n + blk
                    hidden(i, blk % 2)
                    if blk > 0:
                        add(i - 1, blk - 1, gate)
                    else:
                        add(i - 1, NBLK - 1, gate_before)

            gate_chain.start(0)
            if layer == 0:
                steps = gates_top2(nc, dve, sb, gate_chain, shifted, scored, logits, router_bias, gates, scores, E)
            else:
                steps = gates_groups(nc, dve, sb, gate_chain, scored, logits, router_bias, gates, scores, E)
            for _ in range(GATE_STEPS[layer]):
                next(steps)
            for i in range(2 * NBLK):
                hidden(i, i % 2, steps)
                if i > 0:
                    add(i - 1, (i - 1) % NBLK)
                next(steps, None)
            for _ in steps:
                pass
            expert(2, 0, None)
            expert(3, 1, 0)
            with dve.Fori(2, NE // 2) as r:
                for k in range(2):
                    expert(2 * r + k, 2 * r + k - 2, 2 * r + k - 3)
            add(NBLK * NE - 1, NBLK - 1, E - 1)
            dve.wait_ge(added, NBLK * NE)

        @block.tensor
        def _(pe):
            def up(i, n, k, blk):
                tokens, p = slice(blk * BLK, (blk + 1) * BLK), blk % 2
                if blk == 0:
                    wait(pe, w_lo_done, n - 1)
                wait(pe, act_done, i - 1)
                for col, ps in ((A, ps_a[p]), (Bc, ps_b[p])):
                    if col == Bc:
                        wait(pe, hid_done, i - 1)
                    m = 0
                    for c in range(FC):
                        for w, a in split_passes(w_hi[k], w_lo[k], xT_hi, xT_lo):
                            last = nc.tensor.matmul(ps[:], w[:, col + c * P:col + (c + 1) * P], a[:, c, tokens],
                                                    start=m == 0, stop=m == 3 * FC - 1)
                            m += 1
                    last.then_inc(a_ps if col == A else b_ps, 1)

            def down(i, k, p):
                pe.wait_ge(lo_done, i + 1)
                wait(pe, added, i - 1)
                for q in range(TPB):
                    m = 0
                    for a, w in split_passes(hid_hi[p], hid_lo[p], w_hi[k], w_lo[k]):
                        last = nc.tensor.matmul(ps_d[p][:, q], a[:, q * P:(q + 1) * P], w[:, D:D + H],
                                                start=m == 0 and q % 2 == 0, stop=m == 2,
                                                skip_group_check=True)
                        m += 1
                last.then_inc(down_ps, 1)

            def expert(n, k, first=False):
                for blk in range(NBLK):
                    i = NBLK * n + blk
                    up(i, n, k, blk)
                    if blk > 0 or not first:
                        down(i - 1, k if blk else 1 - k, 1 - blk % 2)

            expert(0, 0, first=True)
            expert(1, 1)
            with pe.Fori(1, NE // 2) as r:
                for k in range(2):
                    expert(2 * r + k, k)
            down(NBLK * NE - 1, 1, 1)


def layers(nc, a, out):
    with ExitStack() as ctx:
        def sb(name, shape, dt=F32):
            return ctx.enter_context(nc.sbuf_tensor(name, shape, dt))

        env = {
            "x": sb("x", [P, NT, H]), "ident": sb("ident", [P, P]), "ident_r": sb("ident_r", [P, P], F32R),
            "mask_r": sb("mask_r", [P, P], F32R), "sel_head": sb("sel_head", [P, NH, P], F32R),
            "half_neg": sb("half_neg", [P, 1]),
        }
        experts_of = (16, 32)
        plain = [(env["x"][:], a["x"].rearrange("b (t p) n -> p (b t) n", p=P))]
        weights, wts = [], []
        for layer, E in enumerate(experts_of):
            w = {"tab_c": sb(f"tab_c{layer}", [P, TB, 2, HD]), "tab_s": sb(f"tab_s{layer}", [P, TB, 2, HD]),
                 "router_bias": sb(f"router_bias{layer}_sb", [P, E])}
            for name, cols in (("qkv", 3 * H if layer == 0 else H + 2 * HD), ("out", H), ("router", E)):
                hi, lo = (sb(f"{name}{layer}_{part}", [P, FC, cols], F32R) for part in ("hi", "lo"))
                w[name + "_hi"], w[name + "_lo"] = hi, lo
                weights.append((a[f"{name}{layer}"].rearrange("(c p) n -> p c n", p=P), [P, FC, cols], hi, lo))
            plain.append((w["router_bias"][:], a[f"router_bias{layer}"].partition_broadcast(P)))
            wts.append(w)
        wts[1]["bias"] = sb("bias", [P, H])
        plain += [(wts[1]["bias"][:], a["b_proj"].partition_broadcast(P)),
                  (wts[1]["tab_c"][:], a["xpos_cos"].rearrange("(t p) k d -> p t k d", p=P)),
                  (wts[1]["tab_s"][:], a["xpos_sin"].rearrange("(t p) k d -> p t k d", p=P))]
        prepare(nc, env, plain, weights, (a["rope_cos"], a["rope_sin"], a["q_gamma"], a["k_gamma"],
                                          wts[0]["tab_c"], wts[0]["tab_s"]))
        for layer, E in enumerate(experts_of):
            attention(nc, env, layer, wts[layer])
            with ExitStack() as part:
                def psb(name, shape, dt=F32):
                    return part.enter_context(nc.sbuf_tensor(f"m{layer}_{name}", shape, dt))

                env["xT_hi"], env["xT_lo"] = psb("xT_hi", [P, FC, T], F32R), psb("xT_lo", [P, FC, T], F32R)
                env["logits"] = psb("logits", [P, NT, E])
                env["raw"] = [psb(f"raw{i}", [P, WCOLS]) for i in range(2)]
                env["w_hi"] = [psb(f"w_hi{i}", [P, WCOLS], F32R) for i in range(2)]
                env["w_lo"] = [psb(f"w_lo{i}", [P, WCOLS], F32R) for i in range(2)]
                route(nc, env, layer, wts[layer], E, a[f"experts{layer}"])
                experts(nc, env, layer, a[f"experts{layer}"], wts[layer]["router_bias"], E, out if layer == 1 else None)


def position_tables():
    import numpy as np
    f = np.float32
    inv = (f(1.0) / f(10000.0) ** (np.arange(0, HD, 2, dtype=f) / f(HD))).astype(f)
    pos = np.arange(N, dtype=f)
    ang = (pos[:, None] * inv[None, :]).astype(f)
    ang = np.concatenate([ang, ang], -1)
    sign = np.concatenate([-np.ones(HD // 2, f), np.ones(HD // 2, f)])
    cos, sin = np.cos(ang).astype(f), (np.sin(ang) * sign).astype(f)
    base = ((np.arange(0, HD, 2, dtype=f) + f(0.4 * HD)) / f(1.4 * HD)).astype(f)
    power = ((pos - N // 2) / f(64)).astype(f)
    scale = (base[None, :] ** power[:, None]).astype(f)
    scale = np.concatenate([scale, scale], -1)
    both = np.stack([scale, (f(1.0) / scale).astype(f)], 1) * f(HD ** -0.5)
    return {"rope_cos": cos, "rope_sin": sin, "xpos_cos": (cos[:, None] * both).astype(f),
            "xpos_sin": (sin[:, None] * both).astype(f)}


def expert_layout(first, second, down, s_first, s_second, s_down):
    import numpy as np

    def pack(f, s, d):
        e = f.shape[0]
        def cut(w):
            return w.reshape(e, FC, P, P).transpose(0, 2, 1, 3).reshape(e, P, FC * P)
        return np.concatenate([cut(f), cut(s), d], -1)

    def halves(w):
        return np.stack([w[:, :P], w[:, P:]])

    shared = pack(halves(s_first), halves(s_second), s_down.reshape(2, P, H))
    return np.ascontiguousarray(np.concatenate([shared, pack(first, second, down)], 0))


def kernel(L0_attn_x, L0_attn_w_qkv, L0_attn_w_out, L0_attn_q_gamma, L0_attn_k_gamma, L0_ffn_router_w,
           L0_ffn_router_bias, L0_ffn_Wu, L0_ffn_Wg, L0_ffn_Wd, L0_ffn_Su, L0_ffn_Sg, L0_ffn_Sd, L1_attn_w_q,
           L1_attn_w_kv, L1_attn_w_proj, L1_attn_b_proj, L1_ffn_router_w, L1_ffn_router_bias, L1_ffn_w_gate,
           L1_ffn_w_up, L1_ffn_w_down, L1_ffn_sw_gate, L1_ffn_sw_up, L1_ffn_sw_down):
    import numpy as np
    import concourse.bacc as bacc
    from concourse import mybir as mb
    from concourse.bass_utils import run_bass_kernel_spmd

    g = np.asarray
    arrays = {
        "x": g(L0_attn_x), "qkv0": g(L0_attn_w_qkv), "out0": g(L0_attn_w_out),
        "q_gamma": g(L0_attn_q_gamma), "k_gamma": g(L0_attn_k_gamma),
        "router0": g(L0_ffn_router_w).T, "router_bias0": g(L0_ffn_router_bias),
        "experts0": expert_layout(g(L0_ffn_Wu), g(L0_ffn_Wg), g(L0_ffn_Wd), g(L0_ffn_Su)[0], g(L0_ffn_Sg)[0],
                                  g(L0_ffn_Sd)[0]),
        "qkv1": np.concatenate([g(L1_attn_w_q), g(L1_attn_w_kv)], 0).T, "out1": g(L1_attn_w_proj).T,
        "b_proj": g(L1_attn_b_proj), "router1": g(L1_ffn_router_w), "router_bias1": g(L1_ffn_router_bias),
        "experts1": expert_layout(g(L1_ffn_w_gate), g(L1_ffn_w_up), g(L1_ffn_w_down), g(L1_ffn_sw_gate),
                                  g(L1_ffn_sw_up), g(L1_ffn_sw_down)),
    }
    arrays.update(position_tables())
    arrays = {k: np.ascontiguousarray(v) for k, v in arrays.items()}
    nc = bacc.Bacc("TRN2", target_bir_lowering=False, num_devices=1)
    a = {k: nc.dram_tensor("in_" + k, v.shape, mb.dt.from_np(v.dtype), kind="ExternalInput").ap()
         for k, v in arrays.items()}
    out = nc.dram_tensor("out_0", (B, N, H), mb.dt.float32, kind="ExternalOutput").ap()
    layers(nc, a, out)
    r = run_bass_kernel_spmd(nc, [{"in_" + k: v for k, v in arrays.items()}], core_ids=[0])
    return r.results[0]["out_0"]
```
